# Optimizing a Trainium2 kernel written in Bass

```python
import numpy as np
import jax
import jax.numpy as jnp

def _softmax(x, axis=-1):
    return jax.nn.softmax(x, axis=axis)

def _gelu(x):
    return jax.nn.gelu(x, approximate=True)

def _silu(x):
    return jax.nn.silu(x)

def _sigmoid(x):
    return jax.nn.sigmoid(x)

def _layernorm(x, axis=-1, eps=1e-05):
    m = jnp.mean(x, axis=axis, keepdims=True)
    v = jnp.var(x, axis=axis, keepdims=True)
    return (x - m) / jnp.sqrt(v + eps)

def _scatter_add(tgt, idx, src, axis=0):
    return tgt.at[idx].add(src)

def _segment_sum(src, seg, n):
    return jax.ops.segment_sum(src, seg, n)
kernel_name = 'mk_recurrent_d4_jaxref_r8_5c59cd'

def setup_inputs(seed: int=0):
    np.random.seed(seed)
    _w = jnp.asarray

    def _L0_attn_setup():
        import jax, jax.numpy as jnp
        import numpy as np
        LN_EPS = 1e-05
        D_HEAD = 64

        def _layernorm(x, w, b):
            x = x - jnp.mean(x, axis=-1, keepdims=True)
            scale = jnp.sqrt(jnp.mean(x * x, axis=-1, keepdims=True) + LN_EPS)
            return x / scale * w + b
        key = jax.random.key(seed)
        ks = jax.random.split(key, 6)
        B, S, D, H, Dh = (2, 256, 128, 16, D_HEAD)
        std = 0.02
        return {'resid_pre': jax.random.normal(ks[0], (B, S, D), dtype=jnp.float32), 'W_Q': jax.random.normal(ks[1], (H, D, Dh), dtype=jnp.float32) * std, 'b_Q': jnp.zeros((H, Dh), dtype=jnp.float32), 'W_K': jax.random.normal(ks[2], (H, D, Dh), dtype=jnp.float32) * std, 'b_K': jnp.zeros((H, Dh), dtype=jnp.float32), 'W_V': jax.random.normal(ks[3], (H, D, Dh), dtype=jnp.float32) * std, 'b_V': jnp.zeros((H, Dh), dtype=jnp.float32), 'W_O': jax.random.normal(ks[4], (H, Dh, D), dtype=jnp.float32) * std, 'b_O': jnp.zeros((D,), dtype=jnp.float32), 'ln1_w': jnp.ones((D,), dtype=jnp.float32), 'ln1_b': jnp.zeros((D,), dtype=jnp.float32), 'ln2_w': jnp.ones((D,), dtype=jnp.float32), 'ln2_b': jnp.zeros((D,), dtype=jnp.float32)}
    _L0_attn_in = _L0_attn_setup()

    def _L0_ffn_setup():
        import jax, jax.numpy as jnp
        import numpy as np
        IN_DIM = 128
        HIDDEN = 128
        OUT_DIM = 128
        NUM_EXPERTS = 16
        TOP_K = 2
        ROUTER_TEMP = 1.0
        LN_EPS = 1e-05

        def _layernorm(h, g, b):
            mu = jnp.mean(h, axis=-1, keepdims=True)
            var = jnp.mean(jnp.square(h - mu), axis=-1, keepdims=True)
            return (h - mu) * jax.lax.rsqrt(var + LN_EPS) * g + b
        key = jax.random.key(seed)
        ks = jax.random.split(key, 8)
        s_in = 1.0 / np.sqrt(IN_DIM)
        s_h = 1.0 / np.sqrt(HIDDEN)
        x = jax.random.normal(ks[0], (4, 256, IN_DIM), dtype=jnp.float32)
        Wr = jax.random.uniform(ks[1], (IN_DIM, NUM_EXPERTS), jnp.float32, -s_in, s_in)
        br = jax.random.uniform(ks[2], (NUM_EXPERTS,), jnp.float32, -s_in, s_in)
        W1 = jax.random.uniform(ks[3], (NUM_EXPERTS, IN_DIM, HIDDEN), jnp.float32, -s_in, s_in)
        b1 = jax.random.uniform(ks[4], (NUM_EXPERTS, HIDDEN), jnp.float32, -s_in, s_in)
        g1 = jnp.ones((NUM_EXPERTS, HIDDEN), jnp.float32)
        be1 = jnp.zeros((NUM_EXPERTS, HIDDEN), jnp.float32)
        W2 = jax.random.uniform(ks[5], (NUM_EXPERTS, HIDDEN, OUT_DIM), jnp.float32, -s_h, s_h)
        b2 = jax.random.uniform(ks[6], (NUM_EXPERTS, OUT_DIM), jnp.float32, -s_h, s_h)
        return {'x': x, 'Wr': Wr, 'br': br, 'W1': W1, 'b1': b1, 'g1': g1, 'be1': be1, 'W2': W2, 'b2': b2}
    _L0_ffn_in = _L0_ffn_setup()

    def _L1_attn_setup():
        import jax, jax.numpy as jnp
        import numpy as np
        NEG_FILL = jnp.finfo(jnp.float32).min
        key = jax.random.key(seed)
        k0, k1, k2, k3, k4 = jax.random.split(key, 5)
        B, N, E, D = (4, 512, 128, 32)
        STD = 0.05
        inputs = jax.random.normal(k0, (B, N, E), dtype=jnp.float32)
        Wq = STD * jax.random.normal(k1, (E, D), dtype=jnp.float32)
        Wk = STD * jax.random.normal(k2, (E, D), dtype=jnp.float32)
        Wvdown = STD * jax.random.normal(k3, (E, D), dtype=jnp.float32)
        Wvup = STD * jax.random.normal(k4, (D, E), dtype=jnp.float32)
        return {'inputs': inputs, 'Wq': Wq, 'Wk': Wk, 'Wvdown': Wvdown, 'Wvup': Wvup}
    _L1_attn_in = _L1_attn_setup()

    def _L1_ffn_setup():
        import jax, jax.numpy as jnp
        import numpy as np
        B, S, H, E = (4, 256, 128, 8)
        key = jax.random.key(seed)
        k1, k2, k3 = jax.random.split(key, 3)
        scale_w = 1.0 / np.sqrt(H)
        return {'x': jax.random.normal(k1, (B, S, H), dtype=jnp.float32), 'router_w': jax.random.normal(k2, (H, E), dtype=jnp.float32) * scale_w, 'router_b': jnp.zeros((E,), dtype=jnp.float32), 'expert_w': jax.random.normal(k3, (E, H, H), dtype=jnp.float32) * scale_w, 'expert_b': jnp.zeros((E, H), dtype=jnp.float32)}
    _L1_ffn_in = _L1_ffn_setup()

    def _L2_attn_setup():
        import jax, jax.numpy as jnp
        import numpy as np
        D_MODEL = 128
        D_INNER = 256
        N_STATE = 16
        DT_RANK = 64
        BATCH = 2
        SEQ = 256
        EPS = 1e-05

        def _selective_scan(x_main, dt, Bm, Cm, A):

            def step(h, inp):
                dt_t, B_t, C_t, x_t = inp
                h = jnp.exp(dt_t[..., None] * A) * h + dt_t[..., None] * B_t[:, None, :] * x_t[..., None]
                y = jnp.einsum('ben,bn->be', h, C_t)
                return (h, y)
            h0 = jnp.zeros((x_main.shape[0], D_INNER, N_STATE), x_main.dtype)
            xs = (jnp.swapaxes(dt, 0, 1), jnp.swapaxes(Bm, 0, 1), jnp.swapaxes(Cm, 0, 1), jnp.swapaxes(x_main, 0, 1))
            _, ys = jax.lax.scan(step, h0, xs)
            return jnp.swapaxes(ys, 0, 1)
        key = jax.random.key(seed)
        ks = jax.random.split(key, 8)
        s = 0.02
        x = jax.random.normal(ks[0], (BATCH, SEQ, D_MODEL), jnp.float32)
        W_in = jax.random.normal(ks[1], (2 * D_INNER, D_MODEL), jnp.float32) * s
        conv_w = jax.random.normal(ks[2], (D_INNER, 1, 3), jnp.float32) * s
        conv_b = jnp.zeros((D_INNER,), jnp.float32)
        W_x = jax.random.normal(ks[3], (DT_RANK + 2 * N_STATE, D_INNER), jnp.float32) * s
        W_dt = jax.random.normal(ks[4], (D_INNER, DT_RANK), jnp.float32) * s
        b_dt = jnp.zeros((D_INNER,), jnp.float32)
        A_log = jnp.log(jnp.broadcast_to(jnp.arange(1, N_STATE + 1, dtype=jnp.float32), (D_INNER, N_STATE)))
        D_param = jnp.ones((D_INNER,), jnp.float32)
        W_out = jax.random.normal(ks[5], (D_MODEL, D_INNER), jnp.float32) * s
        gamma = jnp.ones((D_MODEL,), jnp.float32)
        beta = jnp.zeros((D_MODEL,), jnp.float32)
        return {'x': x, 'W_in': W_in, 'conv_w': conv_w, 'conv_b': conv_b, 'W_x': W_x, 'W_dt': W_dt, 'b_dt': b_dt, 'A_log': A_log, 'D_param': D_param, 'W_out': W_out, 'gamma': gamma, 'beta': beta}
    _L2_attn_in = _L2_attn_setup()

    def _L2_ffn_setup():
        import jax, jax.numpy as jnp
        import numpy as np
        B, T, D, E, H, K = (2, 256, 128, 8, 512, 2)
        key = jax.random.key(seed)
        ks = jax.random.split(key, 8)
        s = 0.02
        return {'x': jax.random.normal(ks[0], (B, T, D), jnp.float32), 'rw1': jax.random.normal(ks[1], (D, D), jnp.float32) * s, 'rb1': jnp.zeros((D,), jnp.float32), 'rw2': jax.random.normal(ks[2], (D, E), jnp.float32) * s, 'rb2': jnp.zeros((E,), jnp.float32), 'we1': jax.random.normal(ks[3], (E, D, H), jnp.float32) * s, 'be1': jnp.zeros((E, H), jnp.float32), 'we2': jax.random.normal(ks[4], (E, H, D), jnp.float32) * s, 'be2': jnp.zeros((E, D), jnp.float32)}
    _L2_ffn_in = _L2_ffn_setup()

    def _L3_attn_setup():
        import jax, jax.numpy as jnp
        import numpy as np
        B, S, D = (4, 512, 128)
        CHUNK = 64
        MAX_LR = 0.2
        MIN_DECAY = 0.5
        MAX_NORM = 30.0
        NORM_EPS = 1e-05

        def _forward(x, M_init, eta_w, eta_b, alpha_w, alpha_b, gate_w, gate_b, vg_w1, vg_w2):
            b, s, d = x.shape
            n_ch = s // CHUNK

            def value_gen(y):
                h = jax.nn.silu(y @ vg_w1.T) @ vg_w2.T
                return h + y
            x_chunks = x.reshape(b, n_ch, CHUNK, d).transpose(1, 0, 2, 3)
            M0 = jnp.broadcast_to(M_init, (b, d, d))

            def step(M, chunk):
                eta_tok = jax.nn.sigmoid(chunk @ eta_w + eta_b[0]) * MAX_LR
                alpha_tok = MIN_DECAY + jax.nn.sigmoid(chunk @ alpha_w + alpha_b[0]) * (1.0 - MIN_DECAY)
                eta = eta_tok.mean(axis=1)[:, None, None]
                alpha = alpha_tok.mean(axis=1)[:, None, None]
                outputs = jnp.einsum('bci,boi->bco', chunk, M)
                nrm = jnp.sqrt(jnp.sum(chunk * chunk, axis=-1, keepdims=True))
                keys = chunk / jnp.maximum(nrm, NORM_EPS)
                k_mean = keys.mean(axis=1)
                v_target = value_gen(outputs).mean(axis=1)
                Mk = jnp.einsum('boi,bi->bo', M, k_mean)
                err = v_target - Mk
                update = err[:, :, None] * k_mean[:, None, :]
                M_new = alpha * M + eta * update
                gate = jax.nn.sigmoid(k_mean @ gate_w + gate_b[0])[:, None, None]
                M_new = gate * M_new + (1.0 - gate) * M
                M_norm = jnp.sqrt(jnp.sum(M_new * M_new, axis=(-2, -1), keepdims=True))
                scale = jnp.minimum(MAX_NORM / (M_norm + 1e-06), 1.0)
                return (M_new * scale, outputs)
            M_final, outs = jax.lax.scan(step, M0, x_chunks)
            outs = outs.transpose(1, 0, 2, 3).reshape(b, s, d)
            final_out = value_gen(outs)
            return (final_out, M_final)

        def _reference_tuple_inner(x, M_init, eta_w, eta_b, alpha_w, alpha_b, gate_w, gate_b, vg_w1, vg_w2):
            return _forward(x, M_init, eta_w, eta_b, alpha_w, alpha_b, gate_w, gate_b, vg_w1, vg_w2)
        key = jax.random.key(seed)
        ks = jax.random.split(key, 10)
        return {'x': jax.random.normal(ks[0], (B, S, D), jnp.float32), 'M_init': jax.random.normal(ks[1], (D, D), jnp.float32) * 0.02, 'eta_w': jax.random.normal(ks[2], (D,), jnp.float32) * 0.02, 'eta_b': jax.random.normal(ks[3], (1,), jnp.float32), 'alpha_w': jax.random.normal(ks[4], (D,), jnp.float32) * 0.02, 'alpha_b': jax.random.normal(ks[5], (1,), jnp.float32), 'gate_w': jax.random.normal(ks[6], (D,), jnp.float32) * 0.02, 'gate_b': jax.random.normal(ks[7], (1,), jnp.float32), 'vg_w1': jax.random.normal(ks[8], (D, D), jnp.float32) * 0.02, 'vg_w2': jax.random.normal(ks[9], (D, D), jnp.float32) * 0.02}
    _L3_attn_in = _L3_attn_setup()

    def _L3_ffn_setup():
        import jax, jax.numpy as jnp
        import numpy as np
        TOP_K = 2

        def _mlp(x, w_fc, w_proj):
            return jnp.square(jax.nn.relu(x @ w_fc.T)) @ w_proj.T
        key = jax.random.key(seed)
        ks = jax.random.split(key, 6)
        B, S, D, E = (4, 256, 128, 8)
        d_ff = 4 * D
        x = jax.random.normal(ks[0], (B, S, D), dtype=jnp.float32)
        router_w = jax.random.normal(ks[1], (E, D), dtype=jnp.float32) * 0.02
        w_fc = jax.random.normal(ks[2], (E, d_ff, D), dtype=jnp.float32) * 0.02
        w_proj = jax.random.normal(ks[3], (E, D, d_ff), dtype=jnp.float32) * 0.02
        shared_fc = jax.random.normal(ks[4], (d_ff, D), dtype=jnp.float32) * 0.02
        shared_proj = jax.random.normal(ks[5], (D, d_ff), dtype=jnp.float32) * 0.02
        return {'x': x, 'router_w': router_w, 'w_fc': w_fc, 'w_proj': w_proj, 'shared_fc': shared_fc, 'shared_proj': shared_proj}
    _L3_ffn_in = _L3_ffn_setup()
    _d = {'L0_attn_resid_pre': _L0_attn_in['resid_pre'], 'L0_attn_W_Q': _L0_attn_in['W_Q'], 'L0_attn_b_Q': _L0_attn_in['b_Q'], 'L0_attn_W_K': _L0_attn_in['W_K'], 'L0_attn_b_K': _L0_attn_in['b_K'], 'L0_attn_W_V': _L0_attn_in['W_V'], 'L0_attn_b_V': _L0_attn_in['b_V'], 'L0_attn_W_O': _L0_attn_in['W_O'], 'L0_attn_b_O': _L0_attn_in['b_O'], 'L0_attn_ln1_w': _L0_attn_in['ln1_w'], 'L0_attn_ln1_b': _L0_attn_in['ln1_b'], 'L0_attn_ln2_w': _L0_attn_in['ln2_w'], 'L0_attn_ln2_b': _L0_attn_in['ln2_b'], 'L0_ffn_Wr': _L0_ffn_in['Wr'], 'L0_ffn_br': _L0_ffn_in['br'], 'L0_ffn_W1': _L0_ffn_in['W1'], 'L0_ffn_b1': _L0_ffn_in['b1'], 'L0_ffn_g1': _L0_ffn_in['g1'], 'L0_ffn_be1': _L0_ffn_in['be1'], 'L0_ffn_W2': _L0_ffn_in['W2'], 'L0_ffn_b2': _L0_ffn_in['b2'], 'L1_attn_Wq': _L1_attn_in['Wq'], 'L1_attn_Wk': _L1_attn_in['Wk'], 'L1_attn_Wvdown': _L1_attn_in['Wvdown'], 'L1_attn_Wvup': _L1_attn_in['Wvup'], 'L1_ffn_router_w': _L1_ffn_in['router_w'], 'L1_ffn_router_b': _L1_ffn_in['router_b'], 'L1_ffn_expert_w': _L1_ffn_in['expert_w'], 'L1_ffn_expert_b': _L1_ffn_in['expert_b'], 'L2_attn_W_in': _L2_attn_in['W_in'], 'L2_attn_conv_w': _L2_attn_in['conv_w'], 'L2_attn_conv_b': _L2_attn_in['conv_b'], 'L2_attn_W_x': _L2_attn_in['W_x'], 'L2_attn_W_dt': _L2_attn_in['W_dt'], 'L2_attn_b_dt': _L2_attn_in['b_dt'], 'L2_attn_A_log': _L2_attn_in['A_log'], 'L2_attn_D_param': _L2_attn_in['D_param'], 'L2_attn_W_out': _L2_attn_in['W_out'], 'L2_attn_gamma': _L2_attn_in['gamma'], 'L2_attn_beta': _L2_attn_in['beta'], 'L2_ffn_rw1': _L2_ffn_in['rw1'], 'L2_ffn_rb1': _L2_ffn_in['rb1'], 'L2_ffn_rw2': _L2_ffn_in['rw2'], 'L2_ffn_rb2': _L2_ffn_in['rb2'], 'L2_ffn_we1': _L2_ffn_in['we1'], 'L2_ffn_be1': _L2_ffn_in['be1'], 'L2_ffn_we2': _L2_ffn_in['we2'], 'L2_ffn_be2': _L2_ffn_in['be2'], 'L3_attn_M_init': _L3_attn_in['M_init'], 'L3_attn_eta_w': _L3_attn_in['eta_w'], 'L3_attn_eta_b': _L3_attn_in['eta_b'], 'L3_attn_alpha_w': _L3_attn_in['alpha_w'], 'L3_attn_alpha_b': _L3_attn_in['alpha_b'], 'L3_attn_gate_w': _L3_attn_in['gate_w'], 'L3_attn_gate_b': _L3_attn_in['gate_b'], 'L3_attn_vg_w1': _L3_attn_in['vg_w1'], 'L3_attn_vg_w2': _L3_attn_in['vg_w2'], 'L3_ffn_router_w': _L3_ffn_in['router_w'], 'L3_ffn_w_fc': _L3_ffn_in['w_fc'], 'L3_ffn_w_proj': _L3_ffn_in['w_proj'], 'L3_ffn_shared_fc': _L3_ffn_in['shared_fc'], 'L3_ffn_shared_proj': _L3_ffn_in['shared_proj']}
    _x0 = _d['L0_attn_resid_pre']
    _d['L0_attn_resid_pre'] = jax.random.normal(jax.random.fold_in(jax.random.key(seed), 1), (4, 512, 128), dtype=_x0.dtype)
    del _x0
    return _d

def reference(L0_attn_resid_pre, L0_attn_W_Q, L0_attn_b_Q, L0_attn_W_K, L0_attn_b_K, L0_attn_W_V, L0_attn_b_V, L0_attn_W_O, L0_attn_b_O, L0_attn_ln1_w, L0_attn_ln1_b, L0_attn_ln2_w, L0_attn_ln2_b, L0_ffn_Wr, L0_ffn_br, L0_ffn_W1, L0_ffn_b1, L0_ffn_g1, L0_ffn_be1, L0_ffn_W2, L0_ffn_b2, L1_attn_Wq, L1_attn_Wk, L1_attn_Wvdown, L1_attn_Wvup, L1_ffn_router_w, L1_ffn_router_b, L1_ffn_expert_w, L1_ffn_expert_b, L2_attn_W_in, L2_attn_conv_w, L2_attn_conv_b, L2_attn_W_x, L2_attn_W_dt, L2_attn_b_dt, L2_attn_A_log, L2_attn_D_param, L2_attn_W_out, L2_attn_gamma, L2_attn_beta, L2_ffn_rw1, L2_ffn_rb1, L2_ffn_rw2, L2_ffn_rb2, L2_ffn_we1, L2_ffn_be1, L2_ffn_we2, L2_ffn_be2, L3_attn_M_init, L3_attn_eta_w, L3_attn_eta_b, L3_attn_alpha_w, L3_attn_alpha_b, L3_attn_gate_w, L3_attn_gate_b, L3_attn_vg_w1, L3_attn_vg_w2, L3_ffn_router_w, L3_ffn_w_fc, L3_ffn_w_proj, L3_ffn_shared_fc, L3_ffn_shared_proj):

    def _L0_attn_ref(resid_pre, W_Q, b_Q, W_K, b_K, W_V, b_V, W_O, b_O, ln1_w, ln1_b, ln2_w, ln2_b):
        import jax, jax.numpy as jnp
        import numpy as np
        LN_EPS = 1e-05
        D_HEAD = 64

        def _layernorm(x, w, b):
            x = x - jnp.mean(x, axis=-1, keepdims=True)
            scale = jnp.sqrt(jnp.mean(x * x, axis=-1, keepdims=True) + LN_EPS)
            return x / scale * w + b
        x = _layernorm(resid_pre, ln1_w, ln1_b)
        q = jnp.einsum('hdk,bsd->bshk', W_Q, x) + b_Q
        k = jnp.einsum('hdk,bsd->bshk', W_K, x) + b_K
        v = jnp.einsum('hdk,bsd->bshk', W_V, x) + b_V
        scores = jnp.einsum('bqhk,bphk->bhqp', q, k) / jnp.sqrt(jnp.asarray(D_HEAD, dtype=q.dtype))
        S = scores.shape[-1]
        causal = jnp.tril(jnp.ones((S, S), dtype=bool))
        scores = jnp.where(causal, scores, jnp.asarray(0.0, dtype=scores.dtype))
        pattern = jax.nn.softmax(scores, axis=-1)
        z = jnp.einsum('bhqp,bphk->bqhk', pattern, v)
        attn_out = jnp.einsum('bqhk,hkd->bqd', z, W_O) + b_O
        resid_mid = resid_pre + attn_out
        resid_post = resid_mid + _layernorm(resid_mid, ln2_w, ln2_b)
        return resid_post

    def _L0_ffn_ref(x, Wr, br, W1, b1, g1, be1, W2, b2):
        import jax, jax.numpy as jnp
        import numpy as np
        IN_DIM = 128
        HIDDEN = 128
        OUT_DIM = 128
        NUM_EXPERTS = 16
        TOP_K = 2
        ROUTER_TEMP = 1.0
        LN_EPS = 1e-05

        def _layernorm(h, g, b):
            mu = jnp.mean(h, axis=-1, keepdims=True)
            var = jnp.mean(jnp.square(h - mu), axis=-1, keepdims=True)
            return (h - mu) * jax.lax.rsqrt(var + LN_EPS) * g + b
        orig_shape = x.shape[:-1]
        x_flat = x.reshape(-1, x.shape[-1])
        logits = (x_flat @ Wr + br) / max(ROUTER_TEMP, 1e-06)
        probs = jax.nn.softmax(logits, axis=-1)
        topk_w, topk_idx = jax.lax.top_k(probs, TOP_K)
        topk_w = topk_w / jnp.clip(jnp.sum(topk_w, axis=-1, keepdims=True), 1e-09)
        h = jnp.einsum('nc,ech->neh', x_flat, W1) + b1
        h = _layernorm(h, g1, be1)
        h = jax.nn.gelu(h, approximate=False)
        expert_out = jnp.einsum('neh,eho->neo', h, W2) + b2
        sel = jnp.take_along_axis(expert_out, topk_idx[:, :, None], axis=1)
        y_flat = jnp.sum(sel * topk_w[:, :, None], axis=1)
        return y_flat.reshape(*orig_shape, y_flat.shape[-1])

    def _L1_attn_ref(inputs, Wq, Wk, Wvdown, Wvup):
        import jax, jax.numpy as jnp
        import numpy as np
        NEG_FILL = jnp.finfo(jnp.float32).min
        B, N, E = inputs.shape
        D = Wq.shape[1]
        Q = inputs @ Wq
        K = inputs @ Wk
        score = jnp.einsum('bqd,bkd->bqk', Q, K)
        score = score / jnp.sqrt(jnp.float32(D))
        causal = jnp.tril(jnp.ones((N, N), dtype=bool))
        score = jnp.where(causal, score, 0.0)
        score = jnp.where(score != 0, score, NEG_FILL)
        attn = jax.nn.softmax(score, axis=-1)
        V = inputs @ (Wvdown @ Wvup)
        return attn @ V

    def _L1_ffn_ref(x, router_w, router_b, expert_w, expert_b):
        import jax, jax.numpy as jnp
        import numpy as np
        B, S, H, E = (4, 256, 128, 8)
        b, s, h = x.shape
        xt = x.reshape(b * s, h)
        logits = xt @ router_w + router_b
        probs = jax.nn.softmax(logits, axis=-1)
        gate = jnp.max(probs, axis=-1)
        idx = jnp.argmax(probs, axis=-1)
        out_all = jnp.einsum('th,ehd->ted', xt, expert_w) + expert_b[None, :, :]
        e_out = jnp.take_along_axis(out_all, idx[:, None, None], axis=1)[:, 0, :]
        y = gate[:, None] * e_out
        return y.reshape(b, s, h)

    def _L2_attn_ref(x, W_in, conv_w, conv_b, W_x, W_dt, b_dt, A_log, D_param, W_out, gamma, beta):
        import jax, jax.numpy as jnp
        import numpy as np
        D_MODEL = 128
        D_INNER = 256
        N_STATE = 16
        DT_RANK = 64
        BATCH = 2
        SEQ = 256
        EPS = 1e-05

        def _selective_scan(x_main, dt, Bm, Cm, A):

            def step(h, inp):
                dt_t, B_t, C_t, x_t = inp
                h = jnp.exp(dt_t[..., None] * A) * h + dt_t[..., None] * B_t[:, None, :] * x_t[..., None]
                y = jnp.einsum('ben,bn->be', h, C_t)
                return (h, y)
            h0 = jnp.zeros((x_main.shape[0], D_INNER, N_STATE), x_main.dtype)
            xs = (jnp.swapaxes(dt, 0, 1), jnp.swapaxes(Bm, 0, 1), jnp.swapaxes(Cm, 0, 1), jnp.swapaxes(x_main, 0, 1))
            _, ys = jax.lax.scan(step, h0, xs)
            return jnp.swapaxes(ys, 0, 1)
        residual = x
        xz = jnp.einsum('bld,ed->ble', x, W_in)
        x_main, z = jnp.split(xz, 2, axis=-1)
        xc = jnp.transpose(x_main, (0, 2, 1))
        xc = jax.lax.conv_general_dilated(xc, conv_w, window_strides=(1,), padding=[(1, 1)], feature_group_count=D_INNER, dimension_numbers=('NCH', 'OIH', 'NCH'))
        xc = xc + conv_b[None, :, None]
        x_main = jax.nn.silu(jnp.transpose(xc, (0, 2, 1)))
        dbc = jnp.einsum('ble,fe->blf', x_main, W_x)
        dt_raw = dbc[..., :DT_RANK]
        Bm = dbc[..., DT_RANK:DT_RANK + N_STATE]
        Cm = dbc[..., DT_RANK + N_STATE:]
        dt = jax.nn.softplus(jnp.einsum('blr,er->ble', dt_raw, W_dt) + b_dt)
        A = -jnp.exp(A_log)
        y = _selective_scan(x_main, dt, Bm, Cm, A)
        y = (y + x_main * D_param) * jax.nn.silu(z)
        y = jnp.einsum('ble,de->bld', y, W_out)
        out = y + residual
        mu = out.mean(-1, keepdims=True)
        var = jnp.mean(jnp.square(out - mu), -1, keepdims=True)
        return (out - mu) / jnp.sqrt(var + EPS) * gamma + beta

    def _L2_ffn_ref(x, rw1, rb1, rw2, rb2, we1, be1, we2, be2):
        import jax, jax.numpy as jnp
        import numpy as np
        B, T, D, E, H, K = (2, 256, 128, 8, 512, 2)
        b, t, d = x.shape
        xt = x.reshape(b * t, d)
        n = xt.shape[0]
        logits = jax.nn.silu(xt @ rw1 + rb1) @ rw2 + rb2
        _, idx = jax.lax.top_k(logits, K)
        mask = jnp.zeros((n, E), bool).at[jnp.arange(n)[:, None], idx].set(True)
        w = jax.nn.softmax(jnp.where(mask, logits, -jnp.inf), axis=1)
        h = jax.nn.silu(jnp.einsum('nd,edh->enh', xt, we1) + be1[:, None, :])
        eo = jnp.einsum('enh,ehd->end', h, we2) + be2[:, None, :]
        y = xt + jnp.einsum('ne,end->nd', w, eo)
        return y.reshape(b, t, d)

    def _L3_attn_ref(x, M_init, eta_w, eta_b, alpha_w, alpha_b, gate_w, gate_b, vg_w1, vg_w2):
        import jax, jax.numpy as jnp
        import numpy as np
        B, S, D = (4, 512, 128)
        CHUNK = 64
        MAX_LR = 0.2
        MIN_DECAY = 0.5
        MAX_NORM = 30.0
        NORM_EPS = 1e-05

        def _forward(x, M_init, eta_w, eta_b, alpha_w, alpha_b, gate_w, gate_b, vg_w1, vg_w2):
            b, s, d = x.shape
            n_ch = s // CHUNK

            def value_gen(y):
                h = jax.nn.silu(y @ vg_w1.T) @ vg_w2.T
                return h + y
            x_chunks = x.reshape(b, n_ch, CHUNK, d).transpose(1, 0, 2, 3)
            M0 = jnp.broadcast_to(M_init, (b, d, d))

            def step(M, chunk):
                eta_tok = jax.nn.sigmoid(chunk @ eta_w + eta_b[0]) * MAX_LR
                alpha_tok = MIN_DECAY + jax.nn.sigmoid(chunk @ alpha_w + alpha_b[0]) * (1.0 - MIN_DECAY)
                eta = eta_tok.mean(axis=1)[:, None, None]
                alpha = alpha_tok.mean(axis=1)[:, None, None]
                outputs = jnp.einsum('bci,boi->bco', chunk, M)
                nrm = jnp.sqrt(jnp.sum(chunk * chunk, axis=-1, keepdims=True))
                keys = chunk / jnp.maximum(nrm, NORM_EPS)
                k_mean = keys.mean(axis=1)
                v_target = value_gen(outputs).mean(axis=1)
                Mk = jnp.einsum('boi,bi->bo', M, k_mean)
                err = v_target - Mk
                update = err[:, :, None] * k_mean[:, None, :]
                M_new = alpha * M + eta * update
                gate = jax.nn.sigmoid(k_mean @ gate_w + gate_b[0])[:, None, None]
                M_new = gate * M_new + (1.0 - gate) * M
                M_norm = jnp.sqrt(jnp.sum(M_new * M_new, axis=(-2, -1), keepdims=True))
                scale = jnp.minimum(MAX_NORM / (M_norm + 1e-06), 1.0)
                return (M_new * scale, outputs)
            M_final, outs = jax.lax.scan(step, M0, x_chunks)
            outs = outs.transpose(1, 0, 2, 3).reshape(b, s, d)
            final_out = value_gen(outs)
            return (final_out, M_final)

        def _reference_tuple_inner(x, M_init, eta_w, eta_b, alpha_w, alpha_b, gate_w, gate_b, vg_w1, vg_w2):
            return _forward(x, M_init, eta_w, eta_b, alpha_w, alpha_b, gate_w, gate_b, vg_w1, vg_w2)
        return _reference_tuple_inner(x, M_init, eta_w, eta_b, alpha_w, alpha_b, gate_w, gate_b, vg_w1, vg_w2)[0]

    def _L3_ffn_ref(x, router_w, w_fc, w_proj, shared_fc, shared_proj):
        import jax, jax.numpy as jnp
        import numpy as np
        TOP_K = 2

        def _mlp(x, w_fc, w_proj):
            return jnp.square(jax.nn.relu(x @ w_fc.T)) @ w_proj.T
        B, S, D = x.shape
        E = router_w.shape[0]
        T = B * S
        flat = x.reshape(T, D)
        logits = flat @ router_w.T
        probs = jax.nn.softmax(logits.astype(jnp.float32), axis=-1)
        topk_p, topk_i = jax.lax.top_k(probs, TOP_K)
        topk_w = (topk_p / jnp.maximum(topk_p.sum(-1, keepdims=True), 1e-09)).astype(flat.dtype)
        combine = jnp.zeros((T, E), dtype=flat.dtype)
        combine = combine.at[jnp.arange(T)[:, None], topk_i].add(topk_w)
        out = jnp.zeros_like(flat)
        for e in range(E):
            out = out + _mlp(flat, w_fc[e], w_proj[e]) * combine[:, e:e + 1]
        out = out + _mlp(flat, shared_fc, shared_proj)
        return out.reshape(B, S, D)
    x = L0_attn_resid_pre
    xn = _layernorm(x, axis=-1)
    s = _L0_attn_ref(xn, L0_attn_W_Q, L0_attn_b_Q, L0_attn_W_K, L0_attn_b_K, L0_attn_W_V, L0_attn_b_V, L0_attn_W_O, L0_attn_b_O, L0_attn_ln1_w, L0_attn_ln1_b, L0_attn_ln2_w, L0_attn_ln2_b)
    g = _silu(_L0_ffn_ref(xn, L0_ffn_Wr, L0_ffn_br, L0_ffn_W1, L0_ffn_b1, L0_ffn_g1, L0_ffn_be1, L0_ffn_W2, L0_ffn_b2))
    x = x + s * g
    xn = _layernorm(x, axis=-1)
    s = _L1_attn_ref(xn, L1_attn_Wq, L1_attn_Wk, L1_attn_Wvdown, L1_attn_Wvup)
    g = _silu(_L1_ffn_ref(xn, L1_ffn_router_w, L1_ffn_router_b, L1_ffn_expert_w, L1_ffn_expert_b))
    x = x + s * g
    xn = _layernorm(x, axis=-1)
    s = _L2_attn_ref(xn, L2_attn_W_in, L2_attn_conv_w, L2_attn_conv_b, L2_attn_W_x, L2_attn_W_dt, L2_attn_b_dt, L2_attn_A_log, L2_attn_D_param, L2_attn_W_out, L2_attn_gamma, L2_attn_beta)
    g = _silu(_L2_ffn_ref(xn, L2_ffn_rw1, L2_ffn_rb1, L2_ffn_rw2, L2_ffn_rb2, L2_ffn_we1, L2_ffn_be1, L2_ffn_we2, L2_ffn_be2))
    x = x + s * g
    xn = _layernorm(x, axis=-1)
    s = _L3_attn_ref(xn, L3_attn_M_init, L3_attn_eta_w, L3_attn_eta_b, L3_attn_alpha_w, L3_attn_alpha_b, L3_attn_gate_w, L3_attn_gate_b, L3_attn_vg_w1, L3_attn_vg_w2)
    g = _silu(_L3_ffn_ref(xn, L3_ffn_router_w, L3_ffn_w_fc, L3_ffn_w_proj, L3_ffn_shared_fc, L3_ffn_shared_proj))
    x = x + s * g
    return x

_drawn_inputs = setup_inputs


def setup_inputs(seed=0):
    import zlib

    import numpy as np

    out = dict(_drawn_inputs(seed))
    spreads = {'L0_attn_b_Q': (0.0, 0.8),
     'L0_attn_b_K': (0.0, 0.8),
     'L0_attn_b_V': (0.0, 0.337),
     'L0_attn_b_O': (0.0, 0.1),
     'L0_attn_ln1_w': (1.0, 0.6),
     'L0_attn_ln1_b': (0.0, 0.8),
     'L0_attn_ln2_w': (1.0, 0.2),
     'L0_attn_ln2_b': (0.0, 0.46),
     'L0_ffn_g1': (1.0, 0.2),
     'L0_ffn_be1': (0.0, 0.1),
     'L1_ffn_router_b': (0.0, 0.8),
     'L1_ffn_expert_b': (0.0, 0.8),
     'L2_attn_conv_b': (0.0, 0.8),
     'L2_attn_b_dt': (0.0, 2.0),
     'L2_attn_D_param': (1.0, 0.6),
     'L2_attn_gamma': (1.0, 0.6),
     'L2_attn_beta': (0.0, 1.653),
     'L2_ffn_rb1': (0.0, 1.91),
     'L2_ffn_rb2': (0.0, 0.621),
     'L2_ffn_be1': (0.0, 2.0),
     'L2_ffn_be2': (0.0, 2.0)}
    factors = {'L0_attn_W_Q': 8.0,
     'L0_attn_W_K': 8.0,
     'L0_attn_W_V': 8.0,
     'L1_attn_Wq': 8.0,
     'L1_attn_Wk': 8.0,
     'L1_attn_Wvdown': 8.0,
     'L1_attn_Wvup': 8.0,
     'L1_ffn_router_w': 8.0,
     'L1_ffn_expert_w': 8.0,
     'L2_attn_W_in': 8.0,
     'L2_attn_conv_w': 8.0,
     'L2_attn_W_x': 8.0,
     'L2_attn_W_dt': 8.0,
     'L2_attn_A_log': 33.036,
     'L2_attn_W_out': 8.0,
     'L2_ffn_rw1': 3.744,
     'L2_ffn_rw2': 3.67,
     'L2_ffn_we1': 4.345,
     'L2_ffn_we2': 3.859,
     'L3_attn_M_init': 8.0,
     'L3_attn_eta_w': 64.0,
     'L3_attn_alpha_w': 8.0,
     'L3_attn_gate_w': 64.0,
     'L3_attn_vg_w1': 8.0,
     'L3_attn_vg_w2': 8.0,
     'L3_ffn_router_w': 8.0,
     'L3_ffn_w_fc': 8.0,
     'L3_ffn_w_proj': 8.0,
     'L3_ffn_shared_fc': 8.0,
     'L3_ffn_shared_proj': 8.0}
    for name, (base, spread) in spreads.items():
        noise = np.random.default_rng([zlib.crc32(name.encode()), seed]).standard_normal(out[name].shape)
        drawn = base * np.exp(spread * noise) if base else spread * noise
        out[name] = jnp.asarray(drawn.astype(out[name].dtype))
    for name, factor in factors.items():
        out[name] = (out[name] * factor).astype(out[name].dtype)
    return out
```

```python
from contextlib import ExitStack

import concourse.bass as bass
from concourse import mybir

F32 = mybir.dt.float32
U32 = mybir.dt.uint32
ALU = mybir.AluOpType
ACT = mybir.ActivationFunctionType
AX = mybir.AxisListType

P = 128
D = 128
B, S = 4, 512
T = S // P
EPS = 1e-5
A_LOG_MAX = 80.0
NEG = -3.4028234663852886e38


def build(nc, I, out, layers=4):
    ctx = ExitStack()
    with ctx:
        def sb(name, shape, dt=F32, c=ctx):
            return c.enter_context(nc.sbuf_tensor(name, shape, dt))

        names = []

        def sem(name):
            names.append(name)
            return ctx.enter_context(nc.semaphore(name))

        def linker(eng, chain):
            n = [0]

            def link(ins):
                n[0] += 1
                ins.then_inc(chain, 1)
                eng.wait_ge(chain, n[0])
            return link

        PS = ctx.enter_context(nc.psum_tensor("banks", [P, 8, 512], F32))

        ident = sb("ident", [P, P])
        ones = sb("ones", [P, P])
        tri = sb("tri", [P, P])
        causal = sb("causal", [P, 7 * P])
        iota = sb("iota", [P, T, 16])
        headsel = sb("headsel", [P, 8, 16])
        neg_half = sb("neg_half", [P, 16])
        half_pow = sb("half_pow", [P, 4])
        halfsel = sb("halfsel", [P, 2])

        WQ = sb("WQ", [P, 8, P])
        WK = sb("WK", [P, 8, P])
        WV = sb("WV", [P, 8 * P])
        WO = sb("WO", [P, 8, D])
        bQ = sb("bQ", [P, 8])
        bK = sb("bK", [P, 8])
        bV = sb("bV", [P, 8])
        bO = sb("bO", [P, D])
        ln1w = sb("ln1w", [P, 1])
        ln1b = sb("ln1b", [P, 1])
        ln2w = sb("ln2w", [P, D])
        ln2b = sb("ln2b", [P, D])
        Wr0 = sb("Wr0", [P, 16])
        br0 = sb("br0", [P, 16])
        W1 = sb("W1", [P, 16, P])
        b1 = sb("b1", [P, 16, P])
        g1 = sb("g1", [P, 16])
        be1 = sb("be1", [P, 16])
        W2 = sb("W2", [P, 16, D])
        b2 = sb("b2", [P, D])
        wqp = sb("wqp", [P, P])
        wkp = sb("wkp", [P, P])
        wv1 = sb("wv1", [P, D])
        Wr1 = sb("Wr1", [P, 8])
        br1 = sb("br1", [P, 8])
        EW = sb("EW", [P, 8, D])
        Eb = sb("Eb", [P, D])
        WinT = sb("WinT", [P, 4, P])
        convw = sb("convw", [P, 2, 3])
        convb = sb("convb", [P, 2])
        WxT = sb("WxT", [P, 2, 96])
        WdtT = sb("WdtT", [P, 2, P])
        bdt = sb("bdt", [P, 2])
        Aneg = sb("Aneg", [P, 2, 16])
        Dp = sb("Dp", [P, 2])
        WoutT = sb("WoutT", [P, 2, D])
        gamma = sb("gamma", [P, D])
        beta = sb("beta", [P, D])
        rw1 = sb("rw1", [P, P])
        rb1 = sb("rb1", [P, 1])
        rw2 = sb("rw2", [P, 8])
        rb2 = sb("rb2", [P, 8])
        we1 = sb("we1", [P, 8, 512])
        be1f = sb("be1f", [P, 8, 4])
        we2 = sb("we2", [P, 8, 4, D])
        be2f = sb("be2f", [P, D])
        M0T = sb("M0T", [P, P])
        eaw = sb("eaw", [P, 2])
        eab = sb("eab", [P, 2])
        gw = sb("gw", [P, 1])
        gb = sb("gb", [P, 1])
        vg1T = sb("vg1T", [P, P])
        vg2T = sb("vg2T", [P, P])
        WrT3 = sb("WrT3", [P, 8])
        fcT = sb("fcT", [P, 9, 512])
        pjT = sb("pjT", [P, 9, 4, D])

        s_load = sem("s_load")
        s_const = sem("s_const")
        s_stage = sem("s_stage")
        s_tr = sem("s_tr")
        s_cp = sem("s_cp")
        s_zero = sem("s_zero")
        s_set = sem("s_set")
        s_cp2 = sem("s_cp2")

        def col(ap):
            return ap.rearrange("(p a) -> p a", a=1)

        def bcast(ap, n):
            return ap.rearrange("(a n) -> a n", a=1).to_broadcast([P, n])

        with ExitStack() as c:
            stage = sb("stage", [P, 40, P], c=c)
            plan = []
            loads = []
            n_st = 0

            def st(src, rows, dst, cols=P):
                nonlocal n_st
                plan.append((n_st, rows, cols, dst))
                loads.append((stage[0:rows, n_st, 0:cols], src))
                n_st += 1
            Win = I["L2_attn_W_in"]
            for m in range(4):
                st(Win[m * P:(m + 1) * P, :], P, WinT[:, m, :])
            for m in range(2):
                st(I["L2_attn_W_x"][:, m * P:(m + 1) * P], 96, WxT[:, m, :])
                st(I["L2_attn_W_dt"][m * P:(m + 1) * P, :], P, WdtT[0:64, m, :], 64)
                st(I["L2_attn_W_out"][:, m * P:(m + 1) * P], P, WoutT[:, m, :])
            st(I["L3_attn_M_init"], P, M0T[:, :])
            st(I["L3_attn_vg_w1"], P, vg1T[:, :])
            st(I["L3_attn_vg_w2"], P, vg2T[:, :])
            wvdT = sb("wvdT", [32, P], c=c)
            st(I["L1_attn_Wvdown"], P, wvdT[:, :], 32)
            st(I["L3_ffn_router_w"], 8, WrT3[:, :])
            for name, dst in (("L0_attn_b_Q", bQ), ("L0_attn_b_K", bK), ("L0_attn_b_V", bV)):
                st(I[name].rearrange("(j s) k -> j (s k)", s=2), 8, dst[:, :])
            st(I["L0_ffn_g1"], 16, g1[:, :])
            st(I["L0_ffn_be1"], 16, be1[:, :])
            for name, dst in (("L2_attn_conv_b", convb), ("L2_attn_b_dt", bdt), ("L2_attn_D_param", Dp)):
                st(I[name].rearrange("(m p) -> m p", p=P), 2, dst[:, :])
            st(I["L2_ffn_be1"].rearrange("e (c p) -> (e c) p", p=P), 32, be1f[:, :, :].rearrange("p e c -> p (e c)"))
            n_first = n_st
            big = [[], []]
            big_stage = sb("big_stage", [P, 36, P], c=c)
            wup = sb("wup", [32, D], c=c)
            cen = sb("cen", [P, 16], c=c)

            direct = [
                (WQ[:, :, :].rearrange("p j (s k) -> p (j s) k", s=2), I["L0_attn_W_Q"].rearrange("h d k -> d h k")),
                (WK[:, :, :].rearrange("p j (s k) -> p (j s) k", s=2), I["L0_attn_W_K"].rearrange("h d k -> d h k")),
                (WV[:, :].rearrange("p (h k) -> p h k", k=64), I["L0_attn_W_V"].rearrange("h d k -> d h k")),
                (WO[:, :, :], I["L0_attn_W_O"].rearrange("(j s) k d -> (s k) j d", s=2)),
                (bO[:, :], bcast(I["L0_attn_b_O"], D)),
                (ln1w[:, :], col(I["L0_attn_ln1_w"])),
                (ln1b[:, :], col(I["L0_attn_ln1_b"])),
                (ln2w[:, :], bcast(I["L0_attn_ln2_w"], D)),
                (ln2b[:, :], bcast(I["L0_attn_ln2_b"], D)),
                (Wr0[:, :], I["L0_ffn_Wr"]),
                (br0[:, :], bcast(I["L0_ffn_br"], 16)),
                (W1[:, :, :], I["L0_ffn_W1"].rearrange("e c h -> c e h")),
                (b1[:, :, :].rearrange("p e h -> p (e h)"), bcast(I["L0_ffn_b1"].rearrange("e h -> (e h)"), 2048)),
                (W2[:, :, :], I["L0_ffn_W2"].rearrange("e h o -> h e o")),
                (wup[:, :], I["L1_attn_Wvup"]),
                (Wr1[:, :], I["L1_ffn_router_w"]),
                (br1[:, :], bcast(I["L1_ffn_router_b"], 8)),
                (EW[:, :, :], I["L1_ffn_expert_w"].rearrange("e h d -> h e d")),
                (convw[:, :, :], I["L2_attn_conv_w"].rearrange("(m p) a k -> p m (a k)", p=P)),
                (Aneg[:, :, :], I["L2_attn_A_log"].rearrange("(m p) n -> p m n", p=P)),
                (gamma[:, :], bcast(I["L2_attn_gamma"], D)),
                (beta[:, :], bcast(I["L2_attn_beta"], D)),
                (rw1[:, :], I["L2_ffn_rw1"]),
                (rb1[:, :], col(I["L2_ffn_rb1"])),
                (rw2[:, :], I["L2_ffn_rw2"]),
                (rb2[:, :], bcast(I["L2_ffn_rb2"], 8)),
                (we1[:, :, :], I["L2_ffn_we1"].rearrange("e d h -> d e h")),
                (we2[:, :, :, :].rearrange("p e c d -> p (e c) d"), I["L2_ffn_we2"].rearrange("e (c p) d -> p (e c) d", p=P)),
                (eaw[:, 0:1], col(I["L3_attn_eta_w"])),
                (eaw[:, 1:2], col(I["L3_attn_alpha_w"])),
                (eab[:, 0:1], bcast(I["L3_attn_eta_b"], 1)),
                (eab[:, 1:2], bcast(I["L3_attn_alpha_b"], 1)),
                (gw[:, :], col(I["L3_attn_gate_w"])),
                (gb[:, :], bcast(I["L3_attn_gate_b"], 1)),
            ]
            padded = [
                (b2[0:16, :], I["L0_ffn_b2"]),
                (wqp[:, 0:32], I["L1_attn_Wq"]),
                (wkp[:, 0:32], I["L1_attn_Wk"]),
                (Eb[0:8, :], I["L1_ffn_expert_b"]),
                (be2f[0:8, :], I["L2_ffn_be2"]),
            ]
            fc = I["L3_ffn_w_fc"].rearrange("e (c p) d -> p (e c) d", p=P)
            sfc = I["L3_ffn_shared_fc"].rearrange("(c p) d -> p c d", p=P)
            pj = I["L3_ffn_w_proj"].rearrange("e o f -> o e f")
            spj = I["L3_ffn_shared_proj"].rearrange("o (a f) -> o a f", a=1)

            n_direct = len(direct)
            block = nc.Block()
            with block:
                @block.sync
                def _(sp):
                    for dst, src in loads:
                        sp.dma_start(dst, src).then_inc(s_stage, 16)
                    sp.dma_start(big_stage[:, 0:32, :], fc).then_inc(s_stage, 16)
                    sp.dma_start(big_stage[:, 32:36, :], sfc).then_inc(s_stage, 16)
                    sp.wait_ge(s_zero, 9)
                    for dst, src in padded:
                        sp.dma_start(dst, src).then_inc(s_load, 16)
                    sp.wait_ge(s_cp, n_first + 9)
                    sp.dma_start(big_stage[:, 0:32, :].rearrange("p (e c) f -> p e (c f)", c=4), pj).then_inc(s_stage, 16)
                    sp.dma_start(big_stage[:, 32:36, :].rearrange("p (e c) f -> p e (c f)", c=4), spj).then_inc(s_stage, 16)
                    sp.wait_ge(s_load, 16 * len(padded))
                    sp.wait_ge(s_set, 16 * n_direct)

                @block.scalar
                def _(act):
                    for dst, src in direct:
                        act.dma_start(dst, src).then_inc(s_set, 16)
                    act.wait_ge(s_cp2, 1)
                    nc.scalar.activation(Aneg[:, :, :], Aneg[:, :, :], ACT.Exp).then_inc(s_load, 16)

                @block.gpsimd
                def _(g):
                    for tile in (b2, wqp, wkp, Eb, be2f, WdtT):
                        ap = tile[:, :, :] if len(tile.shape) == 3 else tile[:, :]
                        nc.gpsimd.memset(ap, 0.0).then_inc(s_zero, 1)
                    nc.gpsimd.memset(neg_half[:, :], -0.5).then_inc(s_zero, 1)
                    nc.gpsimd.memset(half_pow[:, :], 0.5).then_inc(s_zero, 1)
                    nc.gpsimd.memset(ones[:, :], 1.0).then_inc(s_zero, 1)
                    nc.gpsimd.memset(ident[:, :], 0.0).then_inc(s_const, 1)
                    nc.gpsimd.memset(tri[:, :], 1.0).then_inc(s_const, 1)
                    nc.gpsimd.memset(causal[:, :], 1.0).then_inc(s_const, 1)
                    nc.gpsimd.memset(headsel[:, :, :], 0.0).then_inc(s_const, 1)
                    nc.gpsimd.memset(halfsel[:, :], 0.0).then_inc(s_const, 1)
                    nc.gpsimd.iota(iota[:, :, :], pattern=[[0, T], [1, 16]], base=0, channel_multiplier=0,
                                   allow_small_or_imprecise_dtypes=True).then_inc(s_const, 1)
                    g.wait_ge(s_const, 6)
                    nc.gpsimd.affine_select(out=ident[:, :], in_=ident[:, :], compare_op=ALU.not_equal, fill=1.0,
                                            base=0, pattern=[[-1, P]], channel_multiplier=1).then_inc(s_const, 1)
                    nc.gpsimd.affine_select(out=tri[:, :], in_=tri[:, :], compare_op=ALU.is_ge, fill=0.0,
                                            base=0, pattern=[[-1, P]], channel_multiplier=1).then_inc(s_const, 1)
                    nc.gpsimd.affine_select(out=causal[:, :], in_=causal[:, :], compare_op=ALU.is_ge, fill=0.0,
                                            base=3 * P, pattern=[[-1, 7 * P]], channel_multiplier=1).then_inc(s_const, 1)
                    g.wait_ge(s_const, 9)
                    for half in range(2):
                        rows = slice(64 * half, 64 * half + 64)
                        nc.gpsimd.affine_select(out=headsel[rows, :, :], in_=headsel[rows, :, :],
                                                compare_op=ALU.not_equal, fill=1.0, base=half,
                                                pattern=[[2, 8], [-1, 16]], channel_multiplier=0).then_inc(s_const, 1)
                        g.wait_ge(s_const, 10 + 2 * half)
                        nc.gpsimd.memset(halfsel[rows, half:half + 1], 1.0).then_inc(s_const, 1)
                        g.wait_ge(s_const, 11 + 2 * half)

                @block.vector
                def _(v):
                    v.wait_ge(s_set, 16 * n_direct)
                    link = linker(v, s_cp2)
                    link(nc.vector.tensor_scalar(Aneg[:, :, :], Aneg[:, :, :], A_LOG_MAX, None, ALU.min))
                    for w in (W1, b1):
                        link(nc.vector.reduce_sum(cen[:, :], w[:, :, :], AX.X))
                        link(nc.vector.tensor_scalar(cen[:, :], cen[:, :], 1.0 / P, None, ALU.mult))
                        link(nc.vector.tensor_tensor(w[:, :, :], w[:, :, :],
                                                     cen[:, :].unsqueeze(2).to_broadcast([P, 16, P]), ALU.subtract))
                    v.wait_ge(s_load, 16 * (len(padded) + 1))
                    link(nc.vector.tensor_scalar(Aneg[:, :, :], Aneg[:, :, :], -1.0, None, ALU.mult))
                    v.wait_ge(s_zero, 9)
                    for n, (slot, rows, cols, dst) in enumerate(plan):
                        v.wait_ge(s_tr, n + 1)
                        nc.vector.tensor_copy(dst, PS[0:cols, n % 2, 0:rows]).then_inc(s_cp, 1)
                    for r in range(18):
                        n = n_first + r
                        v.wait_ge(s_tr, n + 1)
                        dst = fcT[:, r, :] if r < 9 else pjT[:, r - 9, :, :].rearrange("p c d -> p (c d)")
                        nc.vector.tensor_copy(dst, PS[:, n % 2, :]).then_inc(s_cp, 1)
                    v.wait_ge(s_tr, n_first + 19)
                    nc.vector.tensor_copy(wv1[:, :], PS[:, 2, 0:D]).then_inc(s_cp, 1)

                @block.tensor
                def _(pe):
                    pe.wait_ge(s_const, 13)
                    pe.wait_ge(s_stage, 16 * (n_first + 2))
                    for n, (slot, rows, cols, dst) in enumerate(plan):
                        if n >= 2:
                            pe.wait_ge(s_cp, n - 1)
                        nc.tensor.transpose(PS[0:cols, n % 2, 0:rows], stage[0:rows, slot, 0:cols],
                                            ident[0:rows, 0:rows]).then_inc(s_tr, 1)
                    for r in range(18):
                        n = n_first + r
                        pe.wait_ge(s_cp, n - 1)
                        if r == 9:
                            pe.wait_ge(s_stage, 16 * (n_first + 4))
                        for k in range(4):
                            last = nc.tensor.transpose(PS[:, n % 2, k * P:(k + 1) * P],
                                                       big_stage[:, 4 * (r % 9) + k, :], ident[:, :])
                        last.then_inc(s_tr, 1)
                    pe.wait_ge(s_set, 16 * n_direct)
                    nc.tensor.matmul(PS[:, 2, 0:D], wvdT[:, :], wup[:, :], start=True, stop=True).then_inc(s_tr, 1)

        X = sb("X", [P, T, D])
        XN = sb("XN", [P, T, D])
        XNT = sb("XNT", [P, S])
        SA = sb("SA", [P, T, D])
        stats = sb("stats", [P, T, 6])
        mv = sb("mv", [P, T, 2])
        rstd = sb("rstd", [P, T])
        flat = "p t d -> p (t d)"
        loop_sems = len(names)

        def norm_pool(plink, var, rs):
            plink(nc.gpsimd.tensor_scalar(rs, var, EPS, None, ALU.add))
            return nc.gpsimd.tensor_tensor(rs, rs, neg_half[:, 0:rs.shape[1]], ALU.pow)

        def norm_stats(link, src):
            for t in range(T):
                last = nc.vector.bn_stats(stats[:, t, :], src[:, t, :])
            link(last)
            for t in range(T):
                last = nc.vector.bn_aggr(mv[:, t, :], stats[:, t, :])
            return last

        def norm_apply(dst, src):
            for t in range(T):
                last = nc.vector.tensor_scalar(dst[:, t, :], src[:, t, :], mv[:, t, 0:1], rstd[:, t:t + 1],
                                               ALU.subtract, ALU.mult)
            return last

        def transpose_tiles(bank, src):
            for t in range(T):
                last = nc.tensor.transpose(PS[:, bank, t * P:(t + 1) * P], src[:, t, :], ident[:, :])
            return last

        def mm(o, l, r, start=True, stop=True):
            return nc.tensor.matmul(o, l, r, start=start, stop=stop)


        lsems = []

        scope = [ExitStack()]

        def lsem(name):
            h = scope[0].enter_context(nc.semaphore(name))
            lsems.append(h)
            return h

        def end_stage():
            nums = sorted(h.num for h in lsems)
            starts = [n for n in nums if n - 1 not in nums]
            ends = [n for n in nums if n + 1 not in nums]
            for first, last in zip(starts, ends):
                nc.all_engine_barrier(sems_to_clear=range(first, last + 1))
            lsems.clear()
            scope[0].close()
            scope[0] = ExitStack()

        def gate_logits(pe, lhs, w, E, bank):
            for t in range(T):
                last = mm(PS[:, bank, t * E:(t + 1) * E], lhs[:, t * P:(t + 1) * P], w[:, 0:E])
            return last

        LG = sb("LG", [P, T, 16])
        PR = sb("PR", [P, T, 16])
        OH = sb("OH", [P, T, 16])
        OH2 = sb("OH2", [P, T, 16])
        WG = sb("WG", [P, T, P])
        WGT = sb("WGT", [P, S])
        top8 = sb("top8", [P, T, 8])
        idx8 = sb("idx8", [P, T, 8], U32)
        idxf = sb("idxf", [P, T, 8])
        rt = sb("rt", [P, T, 4])

        def rep(ap, n):
            return ap.unsqueeze(2).to_broadcast([P, T, n])

        def route(link, act_exp, bank, bias, E, k, on_logits, renorm):
            lg, pr, oh, oh2 = LG[:, :, 0:E], PR[:, :, 0:E], OH[:, :, 0:E], OH2[:, :, 0:E]
            psv = PS[:, bank, 0:T * E].rearrange("p (t e) -> p t e", e=E)
            if bias is None:
                link(nc.vector.tensor_copy(lg, psv))
            else:
                link(nc.vector.tensor_tensor(lg, psv, bias[:, 0:E].unsqueeze(1).to_broadcast([P, T, E]), ALU.add))
            link(nc.vector.reduce_max(rt[:, :, 0], lg, AX.X))
            act_exp[0](nc.vector.tensor_tensor(pr, lg, rep(rt[:, :, 0], E), ALU.subtract))
            act_exp[1]()
            link(nc.vector.reduce_sum(rt[:, :, 1], pr, AX.X))
            link(nc.vector.reciprocal(rt[:, :, 2], rt[:, :, 1]))
            link(nc.vector.tensor_tensor(pr, pr, rep(rt[:, :, 2], E), ALU.mult))
            pick = lg if on_logits else pr
            for t in range(T):
                last = nc.vector.max(top8[:, t, :], pick[:, t, :])
            link(last)
            for t in range(T):
                last = nc.vector.max_index(idx8[:, t, :], top8[:, t, :], pick[:, t, :])
            link(last)
            link(nc.vector.tensor_copy(idxf[:, :, :], idx8[:, :, :]))
            link(nc.vector.tensor_tensor(oh, iota[:, :, 0:E], rep(idxf[:, :, 0], E), ALU.is_equal))
            if k == 2:
                link(nc.vector.tensor_tensor(oh2, iota[:, :, 0:E], rep(idxf[:, :, 1], E), ALU.is_equal))
                link(nc.vector.tensor_tensor(oh, oh, oh2, ALU.add))
            link(nc.vector.tensor_tensor(pr, pr, oh, ALU.mult))
            if renorm:
                link(nc.vector.reduce_sum(rt[:, :, 3], pr, AX.X))
                link(nc.vector.tensor_scalar(rt[:, :, 3], rt[:, :, 3], 1e-9, None, ALU.max))
                link(nc.vector.reciprocal(rt[:, :, 3], rt[:, :, 3]))
                link(nc.vector.tensor_tensor(pr, pr, rep(rt[:, :, 3], E), ALU.mult))
            link(nc.vector.memset(WG[:, :, :], 0.0))
            return nc.vector.tensor_copy(WG[:, :, 0:E], pr)

        def layer0_attention():
            xn_ok, xt_ok, xt_sb = lsem("a0_xn"), lsem("a0_xt"), lsem("a0_xt_sb")
            var, rs = lsem("a0_var"), lsem("a0_rs")
            dv = lsem("a0_dve_steps")
            vp, vs = lsem("a0_v_products"), lsem("a0_v_stored")
            qk, qks = lsem("a0_qk_products"), lsem("a0_qk_stored")
            sc, nm, ex, ee = lsem("a0_scores"), lsem("a0_neg_max"), lsem("a0_exps"), lsem("a0_tail_exps")
            rc, pn = lsem("a0_inv_sums"), lsem("a0_probs")
            trA, trB, ptA, ptB = lsem("a0_trA"), lsem("a0_trB"), lsem("a0_ptA"), lsem("a0_ptB")
            pv, zs = lsem("a0_pv"), lsem("a0_z_stored")
            tl, tls, cts, ao = lsem("a0_tail"), lsem("a0_tail_stored"), lsem("a0_ct_stored"), lsem("a0_out")
            tz = lsem("a0_zeroed")
            OFF = [0, P, 3 * P, 6 * P]
            NG = 8 * T
            with ExitStack() as c:
                X1 = sb("X1", [P, T, D], c=c)
                X1T = sb("X1T", [P, S], c=c)
                QT = sb("QT", [P, 2, S], c=c)
                KZ = sb("KZ", [P, 2, 2, S], c=c)
                V = sb("V", [P, 8, T, P], c=c)
                PR0 = sb("PR0", [P, 2, 2, 10 * P], c=c)
                PTS = sb("PTS", [P, 2, 2, S], c=c)
                NM = sb("NM", [P, NG, 2], c=c)
                MX = sb("MX", [P, NG, 2], c=c)
                L = sb("L", [P, NG, 2], c=c)
                E0 = sb("E0", [P, NG, 2], c=c)
                R = sb("R", [P, NG, 2], c=c)
                CC = sb("CC", [P, 3, 3, 16], c=c)
                CT = WGT[:, 0:3 * P].rearrange("p (t q) -> p t q", t=3)
                xtail = sb("xtail", [P, 4], c=c)
                xsum = sb("xsum", [P, 4], c=c)
                VT = sb("VT", [P, 8, 3], c=c)
                VTS = PTS[:, 0, 0, 0:384].rearrange("p (j a h) -> p j a h", j=8, a=3)
                G = WG[:, 0, :]

                def ps2(g):
                    b0 = 2 * (g % 2)
                    return PS[:, b0:b0 + 2, :]

                with nc.Block() as block:
                    @block.gpsimd
                    def _(g):
                        plink = linker(g, lsem("a0_pool_steps"))
                        nc.gpsimd.memset(KZ[:, :, :, :], 0.0).then_inc(tz, 1)
                        nc.gpsimd.memset(CC[:, :, :, :], 0.0).then_inc(tz, 1)
                        nc.gpsimd.memset(CT, 0.0).then_inc(tz, 1)
                        nc.gpsimd.memset(G, 0.0).then_inc(tz, 1)
                        for k in range(2):
                            g.wait_ge(var, k + 1)
                            norm_pool(plink, mv[:, :, 1], rstd[:, :]).then_inc(rs, 1)
                        for n in range(NG):
                            j, t = divmod(n, T)
                            w = (t + 1) * P
                            g.wait_ge(rc, n + 1)
                            p = PR0[:, j % 2, :, OFF[t]:OFF[t] + w]
                            nc.gpsimd.tensor_tensor(p, p, R[:, n, :].unsqueeze(2).to_broadcast([P, 2, w]),
                                                    ALU.mult).then_inc(pn, 1)
                        g.wait_ge(var, 3)
                        norm_pool(plink, mv[:, :, 1], rstd[:, :]).then_inc(rs, 1)

                    @block.tensor
                    def _(pe):
                        pe.wait_ge(xn_ok, 1)
                        transpose_tiles(0, XN).then_inc(xt_ok, 1)
                        pe.wait_ge(xn_ok, 2)
                        transpose_tiles(1, X1).then_inc(xt_ok, 1)
                        pe.wait_ge(xt_sb, 2)
                        for i in range(8):
                            t, half = divmod(i, 2)
                            if i >= 2:
                                pe.wait_ge(vs, i - 1)
                            mm(PS[:, 2 + i % 2, :], X1T[:, t * P:(t + 1) * P],
                               WV[:, half * 512:(half + 1) * 512]).then_inc(vp, 1)
                        pe.wait_ge(tls, 1)
                        for j in range(8):
                            last = mm(PS[:, 0, 3 * j:3 * j + 3], WV[:, j * P:(j + 1) * P], xtail[:, 0:3])
                        last.then_inc(tl, 1)
                        pe.wait_ge(tls, 3)
                        for j in range(8):
                            last = mm(PS[0:48, 1, 0:P], PTS[:, 0, 0, 48 * j:48 * j + 48], WO[:, j, :],
                                      start=j == 0, stop=j == 7)
                        last.then_inc(tl, 1)

                        def project(j, which):
                            pe.wait_ge(qks, 3 * j + which)
                            w = (WQ, WK)[which]
                            mm(PS[:, 7, :], w[:, j, :], X1T[:, :]).then_inc(qk, 1)

                        def scores(n):
                            j, t = divmod(n, T)
                            if t == 0:
                                pe.wait_ge(qks, 3 * j + 3)
                            if n >= 2:
                                pe.wait_ge(ex, 2 * (n - 1))
                            for s in range(2):
                                last = mm(ps2(n)[:, s, 0:(t + 1) * P], QT[:, j % 2, t * P:(t + 1) * P],
                                          KZ[:, j % 2, s, 0:(t + 1) * P])
                            last.then_inc(sc, 1)

                        def transposes(j, kt):
                            if kt == 0:
                                pe.wait_ge(pn, T * j + T)
                            for s, (tr, pt) in enumerate(((trA, ptA), (trB, ptB))):
                                if T * j + kt >= 1:
                                    pe.wait_ge(pt, T * j + kt)
                                for t in range(kt, T):
                                    a = OFF[t] + kt * P
                                    last = nc.tensor.transpose(PS[:, 4 + s, t * P:(t + 1) * P],
                                                               PR0[:, j % 2, s, a:a + P], ident[:, :])
                                last.then_inc(tr, 1)

                        def values(j, kt):
                            pe.wait_ge(ptA, T * j + kt + 1)
                            pe.wait_ge(ptB, T * j + kt + 1)
                            if kt == 0 and j:
                                pe.wait_ge(zs, j)
                            for s in range(2):
                                last = mm(PS[64 * s:64 * s + 64, 6, kt * P:S], V[:, j, kt, 64 * s:64 * s + 64],
                                          PTS[:, kt % 2, s, kt * P:S], start=kt == 0, stop=kt == T - 1)
                            last.then_inc(pv, 1)

                        pe.wait_ge(vs, 8)
                        pe.wait_ge(tls, 4)
                        for j in range(2):
                            project(j, 0)
                            project(j, 1)
                            if j == 0:
                                for t in range(T):
                                    scores(t)
                        for j in range(8):
                            for k in range(T):
                                if j + 1 < 8:
                                    scores(T * (j + 1) + k)
                                if j + 2 < 8 and k in (0, 2):
                                    project(j + 2, k // 2)
                                transposes(j, k)
                                if k:
                                    values(j, k - 1)
                            values(j, T - 1)
                        for t in range(3):
                            last = nc.tensor.transpose(PS[0:48, 1, t * P:(t + 1) * P],
                                                       CC[:, t, :, :].rearrange("p a h -> p (a h)"), ident[:, :])
                        last.then_inc(tl, 1)
                        pe.wait_ge(zs, 8)
                        pe.wait_ge(cts, 1)
                        for t in range(T):
                            for j in range(8):
                                last = mm(PS[:, 0, t * P:(t + 1) * P], V[:, j, t, :], WO[:, j, :],
                                          start=j == 0, stop=j == 7 and t == 3)
                            if t < 3:
                                last = mm(PS[:, 0, t * P:(t + 1) * P], CT[:, t, :], G, start=False, stop=True)
                        last.then_inc(ao, 1)

                    @block.scalar
                    def _(act):
                        act.wait_ge(xt_ok, 1)
                        nc.scalar.activation(XNT[:, :], PS[:, 0, :], ACT.Copy).then_inc(xt_sb, 1)
                        act.wait_ge(xt_ok, 2)
                        nc.scalar.activation(X1T[:, :], PS[:, 1, :], ACT.Identity, bias=ln1b[:, :],
                                             scale=ln1w[:, :]).then_inc(xt_sb, 1)
                        for i in range(8):
                            t, half = divmod(i, 2)
                            act.wait_ge(vp, i + 1)
                            nc.scalar.activation(V[:, 4 * half:4 * half + 4, t, :],
                                                 PS[:, 2 + i % 2, :].rearrange("p (j d) -> p j d", j=4),
                                                 ACT.Copy).then_inc(vs, 1)

                        def qk_evac(j, which):
                            act.wait_ge(qk, 2 * j + which + 1)
                            if which == 0:
                                nc.scalar.activation(QT[:, j % 2, :], PS[:, 7, :], ACT.Identity,
                                                     bias=bQ[:, j:j + 1]).then_inc(qks, 1)
                            else:
                                for s in range(2):
                                    r = slice(64 * s, 64 * s + 64)
                                    nc.scalar.activation(KZ[r, j % 2, s, :], PS[r, 7, :], ACT.Identity,
                                                         bias=bK[r, j:j + 1]).then_inc(qks, 1)

                        def exps(n):
                            j, t = divmod(n, T)
                            w = (t + 1) * P
                            act.wait_ge(nm, n + 1)
                            for s in range(2):
                                nc.scalar.activation(PR0[:, j % 2, s, OFF[t]:OFF[t] + w], ps2(n)[:, s, 0:w], ACT.Exp,
                                                     bias=NM[:, n, s:s + 1], scale=0.125,
                                                     accum_out=L[:, n, s:s + 1]).then_inc(ex, 1)
                            nc.scalar.activation(E0[:, n, :], NM[:, n, :], ACT.Exp).then_inc(ee, 1)

                        act.wait_ge(tz, 4)
                        for j in range(2):
                            qk_evac(j, 0)
                            qk_evac(j, 1)
                            if j == 0:
                                for t in range(T):
                                    exps(t)
                        for j in range(8):
                            for k in range(T):
                                if j + 1 < 8:
                                    exps(T * (j + 1) + k)
                                if j + 2 < 8 and k in (0, 2):
                                    qk_evac(j + 2, k // 2)
                                act.wait_ge(trA, T * j + k + 1)
                                if T * j + k >= 2:
                                    act.wait_ge(pv, T * j + k - 1)
                                nc.scalar.activation(PTS[:, k % 2, 0, k * P:S], PS[:, 4, k * P:S],
                                                     ACT.Copy).then_inc(ptA, 1)

                    @block.vector
                    def _(v):
                        link = linker(v, dv)
                        norm_stats(link, X).then_inc(var, 1)
                        v.wait_ge(rs, 1)
                        norm_apply(XN, X).then_inc(xn_ok, 1)
                        v.wait_ge(xn_ok, 1)
                        norm_stats(link, XN).then_inc(var, 1)
                        v.wait_ge(rs, 2)
                        norm_apply(X1, XN).then_inc(xn_ok, 1)
                        v.wait_ge(xt_sb, 2)
                        link(nc.vector.reduce_sum(xsum[:, 0:T], X1T[:, :].rearrange("p (t q) -> p t q", t=T), AX.X))
                        link(nc.vector.tensor_copy(xtail[:, 2:3], xsum[:, 3:4]))
                        link(nc.vector.tensor_tensor(xtail[:, 1:2], xtail[:, 2:3], xsum[:, 2:3], ALU.add))
                        nc.vector.tensor_tensor(xtail[:, 0:1], xtail[:, 1:2], xsum[:, 1:2], ALU.add).then_inc(tls, 1)
                        v.wait_ge(tl, 1)
                        nc.vector.tensor_copy(VT[:, :, :], PS[:, 0, 0:24].rearrange("p (j a) -> p j a", a=3)).then_inc(tls, 1)
                        v.wait_ge(tls, 2)
                        nc.vector.tensor_tensor(VTS, VT[:, :, :].unsqueeze(3).to_broadcast([P, 8, 3, 16]),
                                                headsel[:, :, :].unsqueeze(2).to_broadcast([P, 8, 3, 16]),
                                                ALU.mult).then_inc(tls, 1)
                        v.wait_ge(tl, 2)
                        v.wait_ge(tz, 4)
                        nc.vector.tensor_copy(G[0:48, :], PS[0:48, 1, 0:P]).then_inc(tls, 1)

                        def row_max(n):
                            t = n % T
                            v.wait_ge(sc, n + 1)
                            d = ps2(n)[:, :, t * P:(t + 1) * P]
                            link(nc.vector.tensor_tensor(d, d, tri[:, :].unsqueeze(1).to_broadcast([P, 2, P]), ALU.mult))
                            link(nc.vector.reduce_max(MX[:, n, :], ps2(n)[:, :, 0:(t + 1) * P], AX.X))
                            if t < T - 1:
                                nc.vector.tensor_scalar(NM[:, n, :], MX[:, n, :], 0.0, -0.125, ALU.max,
                                                        ALU.mult).then_inc(nm, 1)
                            else:
                                nc.vector.tensor_scalar(NM[:, n, :], MX[:, n, :], -0.125, None, ALU.mult).then_inc(nm, 1)

                        def row_sum(n):
                            j, t = divmod(n, T)
                            v.wait_ge(ex, 2 * n + 2)
                            v.wait_ge(ee, n + 1)
                            link(nc.vector.scalar_tensor_tensor(L[:, n, :], E0[:, n, :], float((T - 1 - t) * P),
                                                                L[:, n, :], ALU.mult, ALU.add))
                            nc.vector.reciprocal(R[:, n, :], L[:, n, :]).then_inc(rc, 1)
                            if t < T - 1:
                                v.wait_ge(rc, n + 1)
                                nc.vector.tensor_tensor(CC[:, t, t, 2 * j:2 * j + 2], E0[:, n, :], R[:, n, :],
                                                        ALU.mult).then_inc(tls, 1)

                        for t in range(T):
                            row_max(t)
                            if t:
                                row_sum(t - 1)
                        for j in range(8):
                            for k in range(T):
                                n = T * (j + 1) + k
                                row_sum(n - 1)
                                if j + 1 < 8:
                                    row_max(n)
                                v.wait_ge(trB, T * j + k + 1)
                                if T * j + k >= 2:
                                    v.wait_ge(pv, T * j + k - 1)
                                nc.vector.tensor_copy(PTS[:, k % 2, 1, k * P:S], PS[:, 5, k * P:S]).then_inc(ptB, 1)
                                if j + 1 == 8:
                                    break
                            if j + 1 == 8:
                                for k in range(1, T):
                                    v.wait_ge(trB, T * j + k + 1)
                                    v.wait_ge(pv, T * j + k - 1)
                                    nc.vector.tensor_copy(PTS[:, k % 2, 1, k * P:S], PS[:, 5, k * P:S]).then_inc(ptB, 1)
                            v.wait_ge(pv, T * (j + 1))
                            nc.vector.tensor_scalar(V[:, j, :, :].rearrange("p t d -> p (t d)"), PS[:, 6, :],
                                                    bV[:, j:j + 1], None, ALU.add).then_inc(zs, 1)
                        v.wait_ge(tl, 3)
                        nc.vector.tensor_copy(CT[0:48, :, :], PS[0:48, 1, 0:3 * P].rearrange("p (t q) -> p t q", t=3)).then_inc(cts, 1)
                        v.wait_ge(ao, 1)
                        sa = SA[:, :, :]
                        link(nc.vector.tensor_tensor(sa, PS[:, 0, :].rearrange("p (t d) -> p t d", t=T),
                                                     XN[:, :, :], ALU.add))
                        link(nc.vector.tensor_tensor(sa, sa, bO[:, :].unsqueeze(1).to_broadcast([P, T, D]), ALU.add))
                        norm_stats(link, SA).then_inc(var, 1)
                        v.wait_ge(rs, 3)
                        link(norm_apply(X1, SA))
                        link(nc.vector.tensor_tensor(X1[:, :, :], X1[:, :, :], ln2w[:, :].unsqueeze(1).to_broadcast([P, T, D]), ALU.mult))
                        link(nc.vector.tensor_tensor(X1[:, :, :], X1[:, :, :], ln2b[:, :].unsqueeze(1).to_broadcast([P, T, D]), ALU.add))
                        link(nc.vector.tensor_tensor(sa, sa, X1[:, :, :], ALU.add))

        def gate_and_add(link, silu_out, s_ap):
            link(nc.vector.tensor_tensor(silu_out, silu_out, s_ap, ALU.mult))
            link(nc.vector.tensor_tensor(X[:, :, :], X[:, :, :], silu_out, ALU.add))

        def layer0_experts():
            r = {k: lsem(f"f0_{k}") for k in ("logits", "shifted", "expd", "weights", "wT", "wT_stored", "bias")}
            dv, pl = lsem("f0_dve_steps"), lsem("f0_pool_steps")
            hp, hb, sq, hn, ht = (lsem(f"f0_{k}") for k in ("hidden", "biased", "squares", "normed", "hiddenT"))
            gl, yp, ac, gt = (lsem(f"f0_{k}") for k in ("gelus", "outs", "added", "gate"))
            NU = 16
            with ExitStack() as c:
                HB = sb("HB", [P, 2, 4, P], c=c)
                SQ = sb("SQ", [P, 2, 4, P], c=c)
                SS = sb("SS", [P, NU, 4], c=c)
                HN = sb("HN", [P, 2, 4, P], c=c)
                GT = sb("GT", [P, 2, 4, P], c=c)
                ACC = sb("ACC", [P, T, D], c=c)
                GS = sb("GS", [P, T, D], c=c)

                def bank(k, i):
                    return PS[:, k + i % 2, :].rearrange("p (e d) -> p e d", e=4)

                with nc.Block() as block:
                    @block.tensor
                    def _(pe):
                        gate_logits(pe, XNT, Wr0, 16, 6).then_inc(r["logits"], 1)
                        for i in range(NU + 2):
                            if i < NU:
                                t, g = divmod(i, 4)
                                if i >= 2:
                                    pe.wait_ge(hb, i - 1)
                                mm(PS[:, i % 2, :], XNT[:, t * P:(t + 1) * P],
                                   W1[:, 4 * g:4 * g + 4, :].rearrange("p e h -> p (e h)")).then_inc(hp, 1)
                            if i == 0:
                                pe.wait_ge(r["weights"], 1)
                                transpose_tiles(7, WG).then_inc(r["wT"], 1)
                                pe.wait_ge(r["wT_stored"], 1)
                                for t in range(T):
                                    last = mm(PS[:, 7, t * P:(t + 1) * P], WGT[:, t * P:(t + 1) * P], b2[:, :])
                                last.then_inc(r["bias"], 1)
                            u = i - 1
                            if 0 <= u < NU:
                                pe.wait_ge(hn, u + 1)
                                if u >= 2:
                                    pe.wait_ge(gl, u - 1)
                                for e in range(4):
                                    last = nc.tensor.transpose(bank(2, u)[:, e, :], HN[:, u % 2, e, :], ident[:, :])
                                last.then_inc(ht, 1)
                            u = i - 2
                            if 0 <= u:
                                g = u % 4
                                pe.wait_ge(gl, u + 1)
                                if u >= 2:
                                    pe.wait_ge(ac, u - 1)
                                for e in range(4):
                                    last = mm(bank(4, u)[:, e, :], GT[:, u % 2, e, :], W2[:, 4 * g + e, :])
                                last.then_inc(yp, 1)

                    @block.scalar
                    def _(act):
                        act.wait_ge(r["shifted"], 1)
                        nc.scalar.activation(PR[:, :, :], PR[:, :, :], ACT.Exp).then_inc(r["expd"], 1)
                        for i in range(NU + 1):
                            if i < NU:
                                act.wait_ge(hb, i + 1)
                                if i >= 2:
                                    act.wait_ge(sq, i - 1)
                                for e in range(4):
                                    last = nc.scalar.activation(SQ[:, i % 2, e, :], HB[:, i % 2, e, :], ACT.Square,
                                                                scale=float(P) ** -0.5, accum_out=SS[:, i, e:e + 1])
                                last.then_inc(sq, 1)
                            u = i - 1
                            if u >= 0:
                                g = u % 4
                                act.wait_ge(ht, u + 1)
                                if u >= 2:
                                    act.wait_ge(yp, u - 1)
                                for e in range(4):
                                    n = 4 * g + e
                                    last = nc.scalar.activation(GT[:, u % 2, e, :], bank(2, u)[:, e, :], ACT.Gelu,
                                                                bias=be1[:, n:n + 1], scale=g1[:, n:n + 1])
                                last.then_inc(gl, 1)
                        act.wait_ge(ac, NU)
                        nc.scalar.activation(GS[:, :, :], ACC[:, :, :], ACT.Silu).then_inc(gt, 1)

                    @block.gpsimd
                    def _(g):
                        plink = linker(g, pl)
                        for i in range(NU):
                            g.wait_ge(sq, i + 1)
                            plink(norm_pool(plink, SS[:, i, :], SS[:, i, :]))
                            if i >= 2:
                                g.wait_ge(ht, i - 1)
                            nc.gpsimd.tensor_tensor(HN[:, i % 2, :, :], HB[:, i % 2, :, :],
                                                    SS[:, i, :].unsqueeze(2).to_broadcast([P, 4, P]),
                                                    ALU.mult).then_inc(hn, 1)

                    @block.vector
                    def _(v):
                        link = linker(v, dv)

                        def hidden_bias(i):
                            g = i % 4
                            v.wait_ge(hp, i + 1)
                            if i >= 2:
                                v.wait_ge(hn, i - 1)
                                v.wait_ge(sq, i - 1)
                            nc.vector.tensor_tensor(HB[:, i % 2, :, :], bank(0, i), b1[:, 4 * g:4 * g + 4, :],
                                                    ALU.add).then_inc(hb, 1)

                        v.wait_ge(r["logits"], 1)
                        route(link, (lambda ins: ins.then_inc(r["shifted"], 1),
                                        lambda: v.wait_ge(r["expd"], 1)), 6, br0, 16, 2, False, True)\
                            .then_inc(r["weights"], 1)
                        v.wait_ge(r["wT"], 1)
                        nc.vector.tensor_copy(WGT[:, :], PS[:, 7, :]).then_inc(r["wT_stored"], 1)
                        v.wait_ge(r["bias"], 1)
                        link(nc.vector.tensor_copy(ACC[:, :, :].rearrange(flat), PS[:, 7, :]))
                        for i in range(NU + 2):
                            if i < NU:
                                hidden_bias(i)
                            u = i - 2
                            if u >= 0:
                                t, g = divmod(u, 4)
                                v.wait_ge(yp, u + 1)
                                for e in range(4):
                                    ins = nc.vector.scalar_tensor_tensor(ACC[:, t, :], bank(4, u)[:, e, :],
                                                                         WG[:, t, 4 * g + e:4 * g + e + 1],
                                                                         ACC[:, t, :], ALU.mult, ALU.add)
                                    if e < 3:
                                        link(ins)
                                ins.then_inc(ac, 1)
                                v.wait_ge(ac, u + 1)
                        v.wait_ge(gt, 1)
                        gate_and_add(link, GS[:, :, :], SA[:, :, :])

        def layer1_attention():
            dv = lsem("a1_dve_steps")
            var, rs, xn, xt, xts = (lsem(f"a1_{k}") for k in ("var", "rstd", "xn", "xT", "xT_stored"))
            qk, qks, vp, vs, sc, nm, ex = (lsem(f"a1_{k}") for k in ("qk", "qk_stored", "v", "v_stored", "scores", "neg_max", "exps"))
            tr, pt, pv, ou, pl = (lsem(f"a1_{k}") for k in ("transposes", "pT", "pv", "scaled", "pool_steps"))
            with ExitStack() as c:
                Q = sb("Q", [P, S], c=c)
                K = sb("K", [P, S], c=c)
                V = sb("V1", [P, T, D], c=c)
                SC = sb("SC", [P, T, S], c=c)
                FI = sb("FI", [P, 2, S], c=c)
                PB = sb("PB", [P, T, S], c=c)
                PT = sb("PT", [P, T, S], c=c)
                NM = sb("NM1", [P, T], c=c)
                MX = sb("MX1", [P, T], c=c)
                L = sb("L1", [P, T], c=c)
                R = sb("R1", [P, T], c=c)
                sc_scale = 32.0 ** -0.5
                with nc.Block() as block:
                    @block.gpsimd
                    def _(g):
                        plink = linker(g, pl)
                        g.wait_ge(var, 1)
                        norm_pool(plink, mv[:, :, 1], rstd[:, :]).then_inc(rs, 1)

                    @block.tensor
                    def _(pe):
                        pe.wait_ge(xn, 1)
                        transpose_tiles(0, XN).then_inc(xt, 1)
                        pe.wait_ge(xts, 1)
                        for i, w in enumerate((wqp, wkp)):
                            mm(PS[:, 1 + i, :], w[:, :], XNT[:, :]).then_inc(qk, 1)
                        for t in range(T):
                            last = mm(PS[:, 3, t * P:(t + 1) * P], XNT[:, t * P:(t + 1) * P], wv1[:, :])
                        last.then_inc(vp, 1)
                        pe.wait_ge(qks, 2)
                        for t in range(T):
                            mm(PS[:, 4 + t, :], Q[:, t * P:(t + 1) * P], K[:, :]).then_inc(sc, 1)
                        pe.wait_ge(vs, 1)
                        for t in range(T):
                            pe.wait_ge(ex, t + 1)
                            for kt in range(T):
                                last = nc.tensor.transpose(PS[:, kt, t * P:(t + 1) * P],
                                                           PB[:, t, kt * P:(kt + 1) * P], ident[:, :])
                        last.then_inc(tr, 1)
                        pe.wait_ge(pt, 4)
                        for t in range(T):
                            for kt in range(T):
                                last = mm(PS[:, 4, t * P:(t + 1) * P], PT[:, kt, t * P:(t + 1) * P], V[:, kt, :],
                                          start=kt == 0, stop=kt == T - 1)
                        last.then_inc(pv, 1)

                    @block.scalar
                    def _(act):
                        act.wait_ge(xt, 1)
                        nc.scalar.activation(XNT[:, :], PS[:, 0, :], ACT.Copy).then_inc(xts, 1)
                        for i, dst in enumerate((Q, K)):
                            act.wait_ge(qk, i + 1)
                            nc.scalar.activation(dst[:, :], PS[:, 1 + i, :], ACT.Copy).then_inc(qks, 1)
                        act.wait_ge(vp, 1)
                        nc.scalar.activation(V[:, :, :].rearrange(flat), PS[:, 3, :], ACT.Copy).then_inc(vs, 1)
                        for t in range(T):
                            act.wait_ge(nm, t + 1)
                            nc.scalar.activation(PB[:, t, :], SC[:, t, :], ACT.Exp, bias=NM[:, t:t + 1],
                                                 accum_out=L[:, t:t + 1]).then_inc(ex, 1)
                        act.wait_ge(tr, 1)
                        for kt in range(2):
                            nc.scalar.activation(PT[:, kt, :], PS[:, kt, :], ACT.Copy).then_inc(pt, 1)

                    @block.vector
                    def _(v):
                        link = linker(v, dv)
                        norm_stats(link, X).then_inc(var, 1)
                        v.wait_ge(rs, 1)
                        norm_apply(XN, X).then_inc(xn, 1)
                        for t in range(T):
                            v.wait_ge(sc, t + 1)
                            a = (T - 1 - t) * P
                            link(nc.vector.scalar_tensor_tensor(SC[:, t, :], PS[:, 4 + t, :], sc_scale,
                                                                causal[:, a:a + S], ALU.mult, ALU.mult))
                            link(nc.vector.tensor_scalar(FI[:, t % 2, :], SC[:, t, :], 0.0, NEG, ALU.is_equal, ALU.mult))
                            link(nc.vector.tensor_tensor(SC[:, t, :], SC[:, t, :], FI[:, t % 2, :], ALU.add))
                            link(nc.vector.reduce_max(MX[:, t:t + 1], SC[:, t, :], AX.X))
                            nc.vector.tensor_scalar(NM[:, t:t + 1], MX[:, t:t + 1], -1.0, None, ALU.mult).then_inc(nm, 1)
                        v.wait_ge(ex, T)
                        link(nc.vector.reciprocal(R[:, :], L[:, :]))
                        v.wait_ge(tr, 1)
                        for kt in range(2, T):
                            nc.vector.tensor_copy(PT[:, kt, :], PS[:, kt, :]).then_inc(pt, 1)
                        v.wait_ge(pv, 1)
                        for t in range(T):
                            last = nc.vector.tensor_scalar(SA[:, t, :], PS[:, 4, t * P:(t + 1) * P], R[:, t:t + 1],
                                                           None, ALU.mult)
                        last.then_inc(ou, 1)

        def layer1_experts():
            r = {k: lsem(f"f1_{k}") for k in ("logits", "shifted", "expd", "weights", "wT", "wT_stored", "bias")}
            dv, yp, ac, gt = (lsem(f"f1_{k}") for k in ("dve_steps", "outs", "added", "gate"))
            NU = 8
            with ExitStack() as c:
                ACC = sb("ACC1", [P, T, D], c=c)
                GS = sb("GS1", [P, T, D], c=c)
                with nc.Block() as block:
                    @block.tensor
                    def _(pe):
                        gate_logits(pe, XNT, Wr1, 8, 6).then_inc(r["logits"], 1)

                        def unit(u):
                            t, g = divmod(u, 2)
                            if u >= 4:
                                pe.wait_ge(ac, u - 3)
                            mm(PS[:, u % 4, :], XNT[:, t * P:(t + 1) * P],
                               EW[:, 4 * g:4 * g + 4, :].rearrange("p e d -> p (e d)")).then_inc(yp, 1)
                        for u in range(4):
                            unit(u)
                        pe.wait_ge(r["weights"], 1)
                        transpose_tiles(7, WG).then_inc(r["wT"], 1)
                        pe.wait_ge(r["wT_stored"], 1)
                        for t in range(T):
                            last = mm(PS[:, 7, t * P:(t + 1) * P], WGT[:, t * P:(t + 1) * P], Eb[:, :])
                        last.then_inc(r["bias"], 1)
                        for u in range(4, NU):
                            unit(u)

                    @block.scalar
                    def _(act):
                        act.wait_ge(r["shifted"], 1)
                        nc.scalar.activation(PR[:, :, 0:8], PR[:, :, 0:8], ACT.Exp).then_inc(r["expd"], 1)
                        act.wait_ge(ac, NU)
                        nc.scalar.activation(GS[:, :, :], ACC[:, :, :], ACT.Silu).then_inc(gt, 1)

                    @block.vector
                    def _(v):
                        link = linker(v, dv)
                        v.wait_ge(r["logits"], 1)
                        route(link, (lambda ins: ins.then_inc(r["shifted"], 1),
                                        lambda: v.wait_ge(r["expd"], 1)), 6, br1, 8, 1, False, False)\
                            .then_inc(r["weights"], 1)
                        v.wait_ge(r["wT"], 1)
                        nc.vector.tensor_copy(WGT[:, :], PS[:, 7, :]).then_inc(r["wT_stored"], 1)
                        v.wait_ge(r["bias"], 1)
                        link(nc.vector.tensor_copy(ACC[:, :, :].rearrange(flat), PS[:, 7, :]))
                        for u in range(NU):
                            t, g = divmod(u, 2)
                            v.wait_ge(yp, u + 1)
                            for e in range(4):
                                ins = nc.vector.scalar_tensor_tensor(ACC[:, t, :], PS[:, u % 4, e * P:(e + 1) * P],
                                                                     WG[:, t, 4 * g + e:4 * g + e + 1],
                                                                     ACC[:, t, :], ALU.mult, ALU.add)
                                if e < 3:
                                    link(ins)
                            ins.then_inc(ac, 1)
                            v.wait_ge(ac, u + 1)
                        v.wait_ge(gt, 1)
                        gate_and_add(link, GS[:, :, :], SA[:, :, :])

        def layer2_mixer():
            dv, pl, ac = lsem("a2_dve_steps"), lsem("a2_pool_steps"), lsem("a2_act_steps")
            var, rs, xn, xt, xts = (lsem(f"a2_{k}") for k in ("var", "rstd", "xn", "xT", "xT_stored"))
            zr, xz, xm, cv, si = (lsem(f"a2_{k}") for k in ("zeroed", "xz", "x_stored", "conv", "silus"))
            db, dbs, dtp, dtr, dtx = (lsem(f"a2_{k}") for k in ("dbc", "dbc_stored", "dt_raw", "dt_parts", "dt_x"))
            bc, ex, scn, hc, yk = (lsem(f"a2_{k}") for k in ("bc", "decays", "scans", "outs", "y"))
            yg, wo = lsem("a2_gated"), lsem("a2_projected")
            NS = 16
            with ExitStack() as c:
                XP = sb("XP", [P, 2, S + 2], c=c)
                XM = sb("XM", [P, 2, S], c=c)
                ZS = sb("ZS", [P, 2, S], c=c)
                DT = sb("DT", [P, 2, S], c=c)
                DTX = sb("DTX", [P, 2, S], c=c)
                DBC = sb("DBC", [P, S], c=c)
                DA = sb("DA", [P, 2, 2, S], c=c)
                H = sb("H", [P, 2, 2, S], c=c)
                with nc.Block() as block:
                    @block.gpsimd
                    def _(g):
                        plink = linker(g, pl)
                        nc.gpsimd.memset(XP[:, :, :], 0.0).then_inc(zr, 1)
                        nc.gpsimd.memset(DBC[:, :], 0.0).then_inc(zr, 1)
                        for k in range(2):
                            g.wait_ge(var, k + 1)
                            norm_pool(plink, mv[:, :, 1], rstd[:, :]).then_inc(rs, 1)

                    @block.tensor
                    def _(pe):
                        pe.wait_ge(xn, 1)
                        transpose_tiles(7, XN).then_inc(xt, 1)
                        pe.wait_ge(xts, 1)
                        for m in range(4):
                            mm(PS[:, m, :], WinT[:, m, :], XNT[:, :]).then_inc(xz, 1)
                        pe.wait_ge(si, 4)
                        for m in range(2):
                            last = mm(PS[0:96, 4, :], WxT[:, m, :], XM[:, m, :], start=m == 0, stop=m == 1)
                        last.then_inc(db, 1)
                        pe.wait_ge(dbs, 1)
                        for m in range(2):
                            mm(PS[:, 6 + m, :], WdtT[:, m, :], DBC[:, :]).then_inc(dtp, 1)

                        def bc_rows(n):
                            if n >= 2:
                                pe.wait_ge(hc, n - 1)
                            for k in range(2):
                                r = 64 + 16 * k + n
                                last = mm(PS[:, 2 * k + n % 2, :], ident[:, r:r + 1].to_broadcast([P, P]), DBC[:, :])
                            last.then_inc(bc, 1)
                        bc_rows(0)
                        for n in range(NS):
                            if n + 1 < NS:
                                bc_rows(n + 1)
                            pe.wait_ge(hc, n + 1)
                            for m in range(2):
                                last = mm(PS[:, 4 + m, :], ident[:, :], H[:, n % 2, m, :], start=n == 0, stop=n == NS - 1)
                            last.then_inc(yk, 1)
                        pe.wait_ge(yg, 1)
                        for t in range(T):
                            for m in range(2):
                                last = mm(PS[:, 6, t * P:(t + 1) * P], H[:, 0, m, t * P:(t + 1) * P], WoutT[:, m, :],
                                          start=m == 0, stop=m == 1)
                        last.then_inc(wo, 1)

                    @block.scalar
                    def _(act):
                        alink = linker(act, ac)
                        act.wait_ge(xt, 1)
                        nc.scalar.activation(XNT[:, :], PS[:, 7, :], ACT.Copy).then_inc(xts, 1)
                        act.wait_ge(zr, 2)
                        for m in range(2):
                            act.wait_ge(xz, m + 1)
                            nc.scalar.activation(XP[:, m, 1:S + 1], PS[:, m, :], ACT.Copy).then_inc(xm, 1)
                        for m in range(2):
                            act.wait_ge(xz, m + 3)
                            nc.scalar.activation(ZS[:, m, :], PS[:, 2 + m, :], ACT.Silu).then_inc(si, 1)
                        for m in range(2):
                            act.wait_ge(cv, m + 1)
                            nc.scalar.activation(XM[:, m, :], H[:, 0, m, :], ACT.Silu,
                                                 bias=convb[:, m:m + 1]).then_inc(si, 1)
                        act.wait_ge(db, 1)
                        nc.scalar.activation(DBC[0:96, :], PS[0:96, 4, :], ACT.Copy).then_inc(dbs, 1)
                        act.wait_ge(dtp, 2)
                        for m in range(2):
                            nc.scalar.activation(DT[:, m, :], PS[:, 6 + m, :], ACT.Relu, bias=bdt[:, m:m + 1])
                            alink(nc.scalar.activation(DA[:, 0, m, :], PS[:, 6 + m, :], ACT.Abs, bias=bdt[:, m:m + 1]))
                        alink(nc.scalar.activation(DA[:, 0, :, :], DA[:, 0, :, :], ACT.Exp, scale=-1.0))
                        nc.scalar.activation(DA[:, 1, :, :], DA[:, 0, :, :], ACT.Ln, bias=1.0).then_inc(dtr, 1)
                        act.wait_ge(dtx, 1)
                        for n in range(NS):
                            if n >= 2:
                                act.wait_ge(scn, n - 1)
                            for m in range(2):
                                last = nc.scalar.activation(DA[:, n % 2, m, :], DT[:, m, :], ACT.Exp,
                                                            scale=Aneg[:, m, n:n + 1])
                            last.then_inc(ex, 1)

                    @block.vector
                    def _(v):
                        link = linker(v, dv)
                        norm_stats(link, X).then_inc(var, 1)
                        v.wait_ge(rs, 1)
                        norm_apply(XN, X).then_inc(xn, 1)
                        for m in range(2):
                            v.wait_ge(xm, m + 1)
                            o = H[:, 0, m, :]
                            link(nc.vector.tensor_scalar(o, XP[:, m, 0:S], convw[:, m, 0:1], None, ALU.mult))
                            link(nc.vector.scalar_tensor_tensor(o, XP[:, m, 1:S + 1], convw[:, m, 1:2], o, ALU.mult, ALU.add))
                            nc.vector.scalar_tensor_tensor(o, XP[:, m, 2:S + 2], convw[:, m, 2:3], o, ALU.mult,
                                                           ALU.add).then_inc(cv, 1)
                        v.wait_ge(dtr, 1)
                        e, t1 = DA[:, 0, :, :], DTX[:, :, :]
                        link(nc.vector.tensor_scalar(t1, e, 1.0, -1.0, ALU.add, ALU.add))
                        link(nc.vector.tensor_tensor(t1, e, t1, ALU.subtract))
                        link(nc.vector.tensor_tensor(DT[:, :, :], DT[:, :, :], DA[:, 1, :, :], ALU.add))
                        link(nc.vector.tensor_tensor(DT[:, :, :], DT[:, :, :], t1, ALU.add))
                        v.wait_ge(si, 4)
                        nc.vector.tensor_tensor(DTX[:, :, :], DT[:, :, :], XM[:, :, :], ALU.mult).then_inc(dtx, 1)
                        v.wait_ge(dtx, 1)
                        for n in range(NS):
                            h = H[:, n % 2, :, :]
                            v.wait_ge(bc, n + 1)
                            if n >= 2:
                                v.wait_ge(yk, n - 1)
                            link(nc.vector.tensor_tensor(h, DTX[:, :, :], PS[:, n % 2, :].unsqueeze(1).to_broadcast([P, 2, S]),
                                                         ALU.mult))
                            v.wait_ge(ex, n + 1)
                            for m in range(2):
                                last = nc.vector.tensor_tensor_scan(H[:, n % 2, m, :], DA[:, n % 2, m, :],
                                                                    H[:, n % 2, m, :], 0.0, ALU.mult, ALU.add)
                            last.then_inc(scn, 1)
                            v.wait_ge(scn, n + 1)
                            nc.vector.tensor_tensor(h, h, PS[:, 2 + n % 2, :].unsqueeze(1).to_broadcast([P, 2, S]),
                                                    ALU.mult).then_inc(hc, 1)
                        v.wait_ge(yk, NS)
                        for m in range(2):
                            last = nc.vector.scalar_tensor_tensor(H[:, 0, m, :], XM[:, m, :], Dp[:, m:m + 1], PS[:, 4 + m, :],
                                                                  ALU.mult, ALU.add)
                        link(last)
                        nc.vector.tensor_tensor(H[:, 0, :, :], H[:, 0, :, :], ZS[:, :, :], ALU.mult).then_inc(yg, 1)
                        v.wait_ge(wo, 1)
                        sa = SA[:, :, :]
                        link(nc.vector.tensor_tensor(sa, PS[:, 6, :].rearrange("p (t d) -> p t d", t=T), XN[:, :, :], ALU.add))
                        norm_stats(link, SA).then_inc(var, 1)
                        v.wait_ge(rs, 2)
                        link(norm_apply(SA, SA))
                        link(nc.vector.tensor_tensor(sa, sa, gamma[:, :].unsqueeze(1).to_broadcast([P, T, D]), ALU.mult))
                        link(nc.vector.tensor_tensor(sa, sa, beta[:, :].unsqueeze(1).to_broadcast([P, T, D]), ALU.add))

        def layer2_experts():
            r = {k: lsem(f"f2_{k}") for k in ("logits", "shifted", "expd", "weights", "wT", "wT_stored", "bias")}
            dv, r1, r1s, hp, hs, yp, ad, gt = (lsem(f"f2_{k}") for k in (
                "dve_steps", "router", "router_stored", "hidden", "silus", "outs", "added", "gate"))
            with ExitStack() as c:
                ACC = sb("ACC2", [P, T, D], c=c)
                GS = sb("GS2", [P, T, D], c=c)
                H1 = sb("H1", [P, S], c=c)
                HH = sb("HH", [P, 2, 4, S], c=c)
                with nc.Block() as block:
                    @block.tensor
                    def _(pe):
                        mm(PS[:, 6, :], rw1[:, :], XNT[:, :]).then_inc(r1, 1)
                        pe.wait_ge(r1s, 1)
                        gate_logits(pe, H1, rw2, 8, 7).then_inc(r["logits"], 1)
                        for e in range(9):
                            if e < 8:
                                for k in range(4):
                                    n = 4 * e + k
                                    if n >= 4:
                                        pe.wait_ge(hs, n - 3)
                                    mm(PS[:, n % 4, :], we1[:, e, k * P:(k + 1) * P], XNT[:, :]).then_inc(hp, 1)
                            if e == 0:
                                pe.wait_ge(r["weights"], 1)
                                transpose_tiles(6, WG).then_inc(r["wT"], 1)
                                pe.wait_ge(r["wT_stored"], 1)
                                for t in range(T):
                                    last = mm(PS[:, 6, t * P:(t + 1) * P], WGT[:, t * P:(t + 1) * P], be2f[:, :])
                                last.then_inc(r["bias"], 1)
                            u = e - 1
                            if u >= 0:
                                pe.wait_ge(hs, 4 * u + 4)
                                if u >= 2:
                                    pe.wait_ge(ad, u - 1)
                                for t in range(T):
                                    for k in range(4):
                                        last = mm(PS[:, 4 + u % 2, t * P:(t + 1) * P], HH[:, u % 2, k, t * P:(t + 1) * P],
                                                  we2[:, u, k, :], start=k == 0, stop=k == 3)
                                last.then_inc(yp, 1)

                    @block.scalar
                    def _(act):
                        act.wait_ge(r1, 1)
                        nc.scalar.activation(H1[:, :], PS[:, 6, :], ACT.Silu, bias=rb1[:, :]).then_inc(r1s, 1)
                        act.wait_ge(r["shifted"], 1)
                        nc.scalar.activation(PR[:, :, 0:8], PR[:, :, 0:8], ACT.Exp).then_inc(r["expd"], 1)
                        for n in range(32):
                            e, k = divmod(n, 4)
                            act.wait_ge(hp, n + 1)
                            if e >= 2 and k == 0:
                                act.wait_ge(yp, e - 1)
                            nc.scalar.activation(HH[:, e % 2, k, :], PS[:, n % 4, :], ACT.Silu,
                                                 bias=be1f[:, e, k:k + 1]).then_inc(hs, 1)
                        act.wait_ge(ad, 8)
                        nc.scalar.activation(GS[:, :, :], ACC[:, :, :], ACT.Silu).then_inc(gt, 1)

                    @block.vector
                    def _(v):
                        link = linker(v, dv)
                        v.wait_ge(r["logits"], 1)
                        route(link, (lambda ins: ins.then_inc(r["shifted"], 1),
                                        lambda: v.wait_ge(r["expd"], 1)), 7, rb2, 8, 2, True, True)\
                            .then_inc(r["weights"], 1)
                        v.wait_ge(r["wT"], 1)
                        nc.vector.tensor_copy(WGT[:, :], PS[:, 6, :]).then_inc(r["wT_stored"], 1)
                        v.wait_ge(r["bias"], 1)
                        link(nc.vector.tensor_tensor(ACC[:, :, :].rearrange(flat), PS[:, 6, :], XN[:, :, :].rearrange(flat),
                                                     ALU.add))
                        for e in range(8):
                            v.wait_ge(yp, e + 1)
                            for t in range(T):
                                last = nc.vector.scalar_tensor_tensor(ACC[:, t, :], PS[:, 4 + e % 2, t * P:(t + 1) * P],
                                                                      WG[:, t, e:e + 1], ACC[:, t, :], ALU.mult, ALU.add)
                            last.then_inc(ad, 1)
                            v.wait_ge(ad, e + 1)
                        v.wait_ge(gt, 1)
                        gate_and_add(link, GS[:, :, :], SA[:, :, :])

        def layer3():
            dv, pl = lsem("a3_dve_steps"), lsem("a3_pool_steps")
            var, rs, xn, xt, xts = (lsem(f"a3_{k}") for k in ("var", "rstd", "xn", "xT", "xT_stored"))
            ns, kr, km, kms, ea, eas, sg, sm, co, gp, gs_, gate = (lsem(f"a3_{k}") for k in (
                "norms", "key_scales", "key_means", "key_means_stored", "rates", "rates_shifted", "sigmoids",
                "masked", "rate_sums", "gate_parts", "gate_shifted", "gates"))
            gsum = lsem("a3_gate_sums")
            ready, op, ot, h1, hs, vt, dg, eb, nq, nn, nrm, srt = (lsem(f"a3_{k}") for k in (
                "ready", "outs", "outs_stored", "hidden", "silus", "targets", "diag", "err_rows", "squares",
                "norm_sum", "norm_stored", "norm_root"))
            fo, fos = lsem("a3_final"), lsem("a3_final_stored")
            r = {k: lsem(f"f3_{k}") for k in ("logits", "shifted", "expd")}
            hp, rl, sqs, yp, ad, gt = (lsem(f"f3_{k}") for k in (
                "hidden", "relus", "squares", "outs", "added", "gate"))
            NE = 9
            CH = 64
            NC = S // CH
            with ExitStack() as c:
                XK = sb("XK", [P, NC, CH + 1], c=c)
                KM = sb("KM", [P, NC], c=c)
                NSQ = sb("NSQ", [P, T], c=c)
                KR = sb("KR", [P, T, 2], c=c)
                SQJ = sb("SQJ", [P, T, D], c=c)
                SG = sb("SG", [P, T, 2], c=c)
                SM = sb("SM", [P, 2, T, 2], c=c)
                EA = sb("EA", [P, 2, NC], c=c)
                GK = sb("GK", [P, NC], c=c)
                CA = sb("CA", [P, NC], c=c)
                KB = sb("KB", [P, NC], c=c)
                N = sb("N", [P, P], c=c)
                NA = sb("NA", [P, P], c=c)
                N2 = sb("N2", [P, P], c=c)
                NJ = sb("NJ", [P, P], c=c)
                DG = sb("DG", [P, P], c=c)
                OT = sb("OT", [P, S], c=c)
                HS = sb("HS", [P, S], c=c)
                OS = sb("OS", [P, NC], c=c)
                HA = sb("HA", [P, NC], c=c)
                ER = sb("ER", [P, 2], c=c)
                NQ = sb("NQ", [P, NC], c=c)
                NR = sb("NR", [P, NC], c=c)
                ACC = sb("ACC3", [P, T, D], c=c)
                GS = sb("GS3", [P, T, D], c=c)
                RL = sb("RL", [P, 2, S], c=c)
                HH = sb("HH3", [P, 2, 4, S], c=c)
                STEPS = 5
                assert STEPS * NC == 4 * (NE + 1)
                with nc.Block() as block:
                    @block.gpsimd
                    def _(g):
                        plink = linker(g, pl)
                        g.wait_ge(var, 1)
                        norm_pool(plink, mv[:, :, 1], rstd[:, :]).then_inc(rs, 1)
                        g.wait_ge(ns, T)
                        nc.gpsimd.tensor_tensor(NSQ[:, :], NSQ[:, :], half_pow[:, 0:T], ALU.pow).then_inc(ns, 1)
                        for k in range(NC):
                            g.wait_ge(nrm, k + 1)
                            nc.gpsimd.tensor_tensor(NR[:, k:k + 1], NR[:, k:k + 1], half_pow[:, 0:1], ALU.pow).then_inc(srt, 1)

                    @block.tensor
                    def _(pe):
                        pe.wait_ge(xn, 1)
                        transpose_tiles(0, XN).then_inc(xt, 1)
                        pe.wait_ge(xts, 1)
                        for t in range(T):
                            last = mm(PS[:, 2, 2 * t:2 * t + 2], XNT[:, t * P:(t + 1) * P], eaw[:, :])
                        last.then_inc(ea, 1)
                        gate_logits(pe, XNT, WrT3, 8, 7).then_inc(r["logits"], 1)
                        pe.wait_ge(kr, 1)
                        for t in range(T):
                            last = mm(PS[:, 1, 2 * t:2 * t + 2], XN[:, t, :], KR[:, t, :])
                        last.then_inc(km, 1)
                        pe.wait_ge(sm, 1)
                        mm(PS[:, 3, 0:2 * NC], ones[:, :], SM[:, :, :, :].rearrange("p w t h -> p (w t h)")).then_inc(co, 1)
                        pe.wait_ge(gp, 1)
                        mm(PS[:, 4, 0:NC], ones[:, :], GK[:, :]).then_inc(gsum, 1)
                        def experts(i):
                            e, k = divmod(i, 4)
                            if e < NE:
                                if i >= 4:
                                    pe.wait_ge(sqs, i - 3)
                                mm(PS[:, i % 4, :], fcT[:, e, k * P:(k + 1) * P], XNT[:, :]).then_inc(hp, 1)
                            u = e - 1
                            if u >= 0:
                                if k == 0:
                                    pe.wait_ge(sqs, 4 * u + 4)
                                    if u >= 2:
                                        pe.wait_ge(ad, u - 1)
                                for q in range(4):
                                    last = mm(PS[:, 4 + u % 2, k * P:(k + 1) * P], HH[:, u % 2, q, k * P:(k + 1) * P],
                                              pjT[:, u, q, :], start=q == 0, stop=q == 3)
                                if k == 3:
                                    last.then_inc(yp, 1)

                        for k in range(NC):
                            pe.wait_ge(ready, k + 1)
                            mm(PS[:, 7, 0:CH + 1], N[:, :], XK[:, k, :]).then_inc(op, 1)
                            experts(STEPS * k)
                            pe.wait_ge(ot, k + 1)
                            mm(PS[:, 6, 0:CH], vg1T[:, :], OT[:, k * CH:(k + 1) * CH]).then_inc(h1, 1)
                            experts(STEPS * k + 1)
                            pe.wait_ge(hs, k + 1)
                            mm(PS[:, 6, 0:1], vg2T[:, :], HA[:, k:k + 1]).then_inc(vt, 1)
                            experts(STEPS * k + 2)
                            pe.wait_ge(dg, k + 1)
                            mm(PS[:, 6, 0:P], ones[:, :], DG[:, :]).then_inc(eb, 1)
                            experts(STEPS * k + 3)
                            pe.wait_ge(nq, k + 1)
                            mm(PS[:, 6, 0:1], ones[:, :], NQ[:, k:k + 1]).then_inc(nn, 1)
                            experts(STEPS * k + 4)
                        pe.wait_ge(nrm, NC)
                        for t in range(T):
                            mm(PS[:, 6, t * P:(t + 1) * P], HS[:, t * P:(t + 1) * P], vg2T[:, :], start=True, stop=False)
                            last = mm(PS[:, 6, t * P:(t + 1) * P], OT[:, t * P:(t + 1) * P], ident[:, :], start=False, stop=True)
                        last.then_inc(fo, 1)

                    @block.scalar
                    def _(act):
                        act.wait_ge(xt, 1)
                        nc.scalar.activation(XNT[:, :], PS[:, 0, :], ACT.Copy).then_inc(xts, 1)
                        for t in range(T):
                            nc.scalar.activation(SQJ[:, t, :], XN[:, t, :], ACT.Square,
                                                 accum_out=NSQ[:, t:t + 1]).then_inc(ns, 1)
                        act.wait_ge(eas, 1)
                        nc.scalar.activation(SG[:, :, :], SG[:, :, :], ACT.Sigmoid).then_inc(sg, 1)
                        act.wait_ge(gs_, 1)
                        nc.scalar.activation(GK[:, :], GK[:, :], ACT.Sigmoid).then_inc(gate, 1)
                        act.wait_ge(r["shifted"], 1)
                        nc.scalar.activation(PR[:, :, 0:8], PR[:, :, 0:8], ACT.Exp).then_inc(r["expd"], 1)

                        def experts(i):
                            if i < 4 * NE:
                                act.wait_ge(hp, i + 1)
                                if i >= 2:
                                    act.wait_ge(sqs, i - 1)
                                nc.scalar.activation(RL[:, i % 2, :], PS[:, i % 4, :], ACT.Relu).then_inc(rl, 1)

                        for k in range(NC):
                            act.wait_ge(op, k + 1)
                            nc.scalar.activation(OT[:, k * CH:(k + 1) * CH], PS[:, 7, 0:CH], ACT.Copy,
                                                 accum_out=OS[:, k:k + 1]).then_inc(ot, 1)
                            experts(STEPS * k)
                            act.wait_ge(h1, k + 1)
                            nc.scalar.activation(HS[:, k * CH:(k + 1) * CH], PS[:, 6, 0:CH], ACT.Silu,
                                                 accum_out=HA[:, k:k + 1]).then_inc(hs, 1)
                            for i in range(1, STEPS):
                                experts(STEPS * k + i)
                        act.wait_ge(fo, 1)
                        nc.scalar.activation(SA[:, :, :].rearrange(flat), PS[:, 6, :], ACT.Copy).then_inc(fos, 1)
                        act.wait_ge(ad, NE)
                        nc.scalar.activation(GS[:, :, :], ACC[:, :, :], ACT.Silu).then_inc(gt, 1)

                    @block.vector
                    def _(v):
                        link = linker(v, dv)
                        norm_stats(link, X).then_inc(var, 1)
                        v.wait_ge(rs, 1)
                        norm_apply(XN, X).then_inc(xn, 1)
                        v.wait_ge(ns, T + 1)
                        link(nc.vector.tensor_scalar(NSQ[:, :], NSQ[:, :], 1e-5, None, ALU.max))
                        link(nc.vector.reciprocal(NSQ[:, :], NSQ[:, :]))
                        link(nc.vector.tensor_scalar(NSQ[:, :], NSQ[:, :], 1.0 / CH, None, ALU.mult))
                        nc.vector.tensor_tensor(KR[:, :, :], rep(NSQ[:, :], 2),
                                                halfsel[:, :].unsqueeze(1).to_broadcast([P, T, 2]), ALU.mult).then_inc(kr, 1)
                        v.wait_ge(ea, 1)
                        nc.vector.tensor_tensor(SG[:, :, :], PS[:, 2, 0:2 * T].rearrange("p (t w) -> p t w", w=2),
                                                eab[:, :].unsqueeze(1).to_broadcast([P, T, 2]), ALU.add).then_inc(eas, 1)
                        v.wait_ge(km, 1)
                        link(nc.vector.tensor_copy(KM[:, :], PS[:, 1, 0:NC]))
                        nc.vector.tensor_scalar(GK[:, :], KM[:, :], gw[:, :], None, ALU.mult).then_inc(gp, 1)
                        v.wait_ge(sg, 1)
                        for w in range(2):
                            last = nc.vector.tensor_tensor(SM[:, w, :, :], rep(SG[:, :, w], 2),
                                                           halfsel[:, :].unsqueeze(1).to_broadcast([P, T, 2]), ALU.mult)
                        last.then_inc(sm, 1)
                        v.wait_ge(gsum, 1)
                        nc.vector.tensor_scalar(GK[:, :], PS[:, 4, 0:NC], gb[:, :], None, ALU.add).then_inc(gs_, 1)
                        link(nc.vector.tensor_copy(XK[:, :, CH], KM[:, :]))
                        v.wait_ge(xts, 1)
                        link(nc.vector.tensor_copy(XK[:, :, 0:CH], XNT[:, :].rearrange("p (k c) -> p k c", c=CH)))
                        link(nc.vector.tensor_copy(N[:, :], M0T[:, :]))
                        v.wait_ge(co, 1)
                        link(nc.vector.tensor_scalar(EA[:, 0, :], PS[:, 3, 0:NC], 0.2 / CH, None, ALU.mult))
                        link(nc.vector.tensor_scalar(EA[:, 1, :], PS[:, 3, NC:2 * NC], 0.5 / CH, -0.5, ALU.mult, ALU.add))
                        v.wait_ge(gate, 1)
                        link(nc.vector.tensor_tensor(CA[:, :], EA[:, 1, :], GK[:, :], ALU.mult))
                        link(nc.vector.tensor_scalar(CA[:, :], CA[:, :], 1.0, None, ALU.add))
                        link(nc.vector.tensor_tensor(KB[:, :], EA[:, 0, :], GK[:, :], ALU.mult))
                        link(nc.vector.tensor_tensor(KB[:, :], KB[:, :], KM[:, :], ALU.mult))
                        v.wait_ge(r["logits"], 1)
                        link(route(link, (lambda ins: ins.then_inc(r["shifted"], 1),
                                             lambda: v.wait_ge(r["expd"], 1)), 7, None, 8, 2, False, True))
                        link(nc.vector.memset(WG[:, :, 8:9], 1.0))
                        nc.vector.memset(ACC[:, :, :], 0.0).then_inc(ready, 1)
                        v.wait_ge(ready, 1)

                        def experts(i):
                            e, k = divmod(i, 4)
                            if e < NE:
                                v.wait_ge(rl, i + 1)
                                if e >= 2 and k == 0:
                                    v.wait_ge(yp, e - 1)
                                nc.vector.tensor_tensor(HH[:, e % 2, k, :], RL[:, i % 2, :], PS[:, i % 4, :],
                                                        ALU.mult).then_inc(sqs, 1)
                            if e >= 2 and k == 0:
                                add_expert(e - 2)

                        def add_expert(u):
                            v.wait_ge(yp, u + 1)
                            if u:
                                v.wait_ge(ad, u)
                            for t in range(T):
                                last = nc.vector.scalar_tensor_tensor(ACC[:, t, :], PS[:, 4 + u % 2, t * P:(t + 1) * P],
                                                                      WG[:, t, u:u + 1], ACC[:, t, :], ALU.mult, ALU.add)
                            last.then_inc(ad, 1)

                        for k in range(NC):
                            link(nc.vector.tensor_scalar(NA[:, :], N[:, :], CA[:, k:k + 1], None, ALU.mult))
                            experts(STEPS * k)
                            experts(STEPS * k + 1)
                            v.wait_ge(vt, k + 1)
                            v.wait_ge(hs, k + 1)
                            link(nc.vector.tensor_tensor(ER[:, 0:1], PS[:, 6, 0:1], OS[:, k:k + 1], ALU.add))
                            link(nc.vector.scalar_tensor_tensor(ER[:, 1:2], ER[:, 0:1], 1.0 / CH, PS[:, 7, CH:CH + 1],
                                                                ALU.mult, ALU.subtract))
                            nc.vector.tensor_scalar(DG[:, :], ident[:, :], ER[:, 1:2], None, ALU.mult).then_inc(dg, 1)
                            experts(STEPS * k + 2)
                            v.wait_ge(eb, k + 1)
                            link(nc.vector.scalar_tensor_tensor(N2[:, :], PS[:, 6, 0:P], KB[:, k:k + 1], NA[:, :],
                                                                ALU.mult, ALU.add))
                            nc.vector.scalar_tensor_tensor(NJ[:, :], N2[:, :], 1.0, N2[:, :], ALU.mult, ALU.mult,
                                                           accum_out=NQ[:, k:k + 1]).then_inc(nq, 1)
                            experts(STEPS * k + 3)
                            v.wait_ge(nn, k + 1)
                            nc.vector.tensor_copy(NR[:, k:k + 1], PS[:, 6, 0:1]).then_inc(nrm, 1)
                            experts(STEPS * k + 4)
                            v.wait_ge(srt, k + 1)
                            nr = NR[:, k:k + 1]
                            link(nc.vector.tensor_scalar(nr, nr, 1e-6, None, ALU.add))
                            link(nc.vector.reciprocal(nr, nr))
                            link(nc.vector.tensor_scalar(nr, nr, 30.0, 1.0, ALU.mult, ALU.min))
                            nc.vector.tensor_scalar(N[:, :], N2[:, :], nr, None, ALU.mult).then_inc(ready, 1)
                            v.wait_ge(ready, k + 2)
                        add_expert(NE - 1)
                        v.wait_ge(gt, 1)
                        v.wait_ge(fos, 1)
                        gate_and_add(link, GS[:, :, :], SA[:, :, :])
        out_t = out.rearrange("b (t p) d -> b p t d", p=P)
        x_t = I["L0_attn_resid_pre"].rearrange("b (t p) d -> b p t d", p=P)
        with nc.Fori(0, B) as b:
            x_in = lsem("x_in")
            with nc.Block() as block:
                @block.sync
                def _(sp):
                    sp.dma_start(X[:, :, :], x_t[bass.ds(b, 1)].rearrange("a p t d -> (a p) t d")).then_inc(x_in, 16)
                    sp.wait_ge(x_in, 16)
            end_stage()
            layer0_attention()
            end_stage()
            layer0_experts()
            end_stage()
            layer1_attention()
            end_stage()
            layer1_experts()
            end_stage()
            layer2_mixer()
            end_stage()
            layer2_experts()
            end_stage()
            layer3()
            end_stage()
            x_out = lsem("x_out")
            with nc.Block() as block:
                @block.sync
                def _(sp):
                    sp.dma_start(out_t[bass.ds(b, 1)].rearrange("a p t d -> (a p) t d"), X[:, :, :]).then_inc(x_out, 16)
                    sp.wait_ge(x_out, 16)
            end_stage()


def kernel(**inputs):
    import numpy as _np
    import concourse.bacc as _bacc
    from concourse import mybir as _mybir
    from concourse.bass_utils import run_bass_kernel_spmd as _run

    nc = _bacc.Bacc("TRN2", target_bir_lowering=False, num_devices=1)
    arrays, aps = {}, {}
    for name in inputs:
        a = _np.ascontiguousarray(inputs[name])
        arrays[f"in_{name}"] = a
        aps[name] = nc.dram_tensor(f"in_{name}", a.shape, _mybir.dt.from_np(a.dtype), kind="ExternalInput").ap()
    out = nc.dram_tensor("out_0", (B, S, D), F32, kind="ExternalOutput").ap()
    build(nc, aps, out)
    r = _run(nc, [arrays], core_ids=[0])
    return r.results[0]["out_0"]
```

```python
from contextlib import ExitStack

import concourse.bass as bass
from concourse import mybir

F32 = mybir.dt.float32
F32R = mybir.dt.float32r
U32 = mybir.dt.uint32
ALU = mybir.AluOpType
ACT = mybir.ActivationFunctionType
AX = mybir.AxisListType

P = 128
D = 128
B, S = 4, 512
T = S // P
EPS = 1e-5
A_LOG_MAX = 80.0
NEG = -3.4028234663852886e38


def build(nc, I, out, layers=4):
    ctx = ExitStack()
    with ctx:
        def sb(name, shape, dt=F32, c=ctx):
            return c.enter_context(nc.sbuf_tensor(name, shape, dt))

        names = []

        def sem(name):
            names.append(name)
            return ctx.enter_context(nc.semaphore(name))

        def linker(eng, chain):
            n = [0]

            def link(ins):
                n[0] += 1
                ins.then_inc(chain, 1)
                eng.wait_ge(chain, n[0])
            return link

        PS = ctx.enter_context(nc.psum_tensor("banks", [P, 8, 512], F32))

        ident = sb("ident", [P, P])
        identR = sb("identR", [P, P], F32R)
        ones = sb("ones", [P, P])
        tri = sb("tri", [P, P])
        causal = sb("causal", [P, 7 * P])
        iota = sb("iota", [P, T, 16])
        headsel = sb("headsel", [P, 8, 16])
        neg_half = sb("neg_half", [P, 16])
        half_pow = sb("half_pow", [P, 4])
        halfsel = sb("halfsel", [P, 2])

        WQ = sb("WQ", [P, 8, P])
        WK = sb("WK", [P, 8, P])
        WV = sb("WV", [P, 8 * P])
        WO = sb("WO", [P, 8, D])
        bQ = sb("bQ", [P, 8])
        bK = sb("bK", [P, 8])
        bV = sb("bV", [P, 8])
        bO = sb("bO", [P, D])
        ln1w = sb("ln1w", [P, 1])
        ln1b = sb("ln1b", [P, 1])
        ln2w = sb("ln2w", [P, D])
        ln2b = sb("ln2b", [P, D])
        Wr0 = sb("Wr0", [P, 16])
        br0 = sb("br0", [P, 16])
        W1 = sb("W1", [P, 16, P])
        b1 = sb("b1", [P, 16, P])
        g1 = sb("g1", [P, 16])
        be1 = sb("be1", [P, 16])
        W2 = sb("W2", [P, 16, D])
        b2 = sb("b2", [P, D])
        wqp = sb("wqp", [P, P])
        wkp = sb("wkp", [P, P])
        wv1 = sb("wv1", [P, D])
        Wr1 = sb("Wr1", [P, 8])
        br1 = sb("br1", [P, 8])
        EW = sb("EW", [P, 8, D])
        Eb = sb("Eb", [P, D])
        WinT = sb("WinT", [P, 4, P])
        convw = sb("convw", [P, 2, 3])
        convb = sb("convb", [P, 2])
        WxT = sb("WxT", [P, 2, 96])
        WdtT = sb("WdtT", [P, 2, P])
        bdt = sb("bdt", [P, 2])
        Aneg = sb("Aneg", [P, 2, 16])
        Dp = sb("Dp", [P, 2])
        WoutT = sb("WoutT", [P, 2, D])
        gamma = sb("gamma", [P, D])
        beta = sb("beta", [P, D])
        rw1 = sb("rw1", [P, P])
        rb1 = sb("rb1", [P, 1])
        rw2 = sb("rw2", [P, 8])
        rb2 = sb("rb2", [P, 8])
        we1 = sb("we1", [P, 8, 512])
        be1f = sb("be1f", [P, 8, 4])
        we2 = sb("we2", [P, 8, 4, D])
        be2f = sb("be2f", [P, D])
        M0T = sb("M0T", [P, P])
        eaw = sb("eaw", [P, 2])
        eab = sb("eab", [P, 2])
        gw = sb("gw", [P, 1])
        gb = sb("gb", [P, 1])
        vg1T = sb("vg1T", [P, P])
        vg2T = sb("vg2T", [P, P])
        WrT3 = sb("WrT3", [P, 8])
        fcT = sb("fcT", [P, 9, 512])
        pjT = sb("pjT", [P, 9, 4, D])

        s_load = sem("s_load")
        s_const = sem("s_const")
        s_stage = sem("s_stage")
        s_tr = sem("s_tr")
        s_cp = sem("s_cp")
        s_zero = sem("s_zero")
        s_set = sem("s_set")
        s_cp2 = sem("s_cp2")

        def col(ap):
            return ap.rearrange("(p a) -> p a", a=1)

        def bcast(ap, n):
            return ap.rearrange("(a n) -> a n", a=1).to_broadcast([P, n])

        with ExitStack() as c:
            stage = sb("stage", [P, 40, P], c=c)
            plan = []
            loads = []
            n_st = 0

            def st(src, rows, dst, cols=P):
                nonlocal n_st
                plan.append((n_st, rows, cols, dst))
                loads.append((stage[0:rows, n_st, 0:cols], src))
                n_st += 1
            Win = I["L2_attn_W_in"]
            for m in range(4):
                st(Win[m * P:(m + 1) * P, :], P, WinT[:, m, :])
            for m in range(2):
                st(I["L2_attn_W_x"][:, m * P:(m + 1) * P], 96, WxT[:, m, :])
                st(I["L2_attn_W_dt"][m * P:(m + 1) * P, :], P, WdtT[0:64, m, :], 64)
                st(I["L2_attn_W_out"][:, m * P:(m + 1) * P], P, WoutT[:, m, :])
            st(I["L3_attn_M_init"], P, M0T[:, :])
            st(I["L3_attn_vg_w1"], P, vg1T[:, :])
            st(I["L3_attn_vg_w2"], P, vg2T[:, :])
            wvdT = sb("wvdT", [32, P], c=c)
            st(I["L1_attn_Wvdown"], P, wvdT[:, :], 32)
            st(I["L3_ffn_router_w"], 8, WrT3[:, :])
            for name, dst in (("L0_attn_b_Q", bQ), ("L0_attn_b_K", bK), ("L0_attn_b_V", bV)):
                st(I[name].rearrange("(j s) k -> j (s k)", s=2), 8, dst[:, :])
            st(I["L0_ffn_g1"], 16, g1[:, :])
            st(I["L0_ffn_be1"], 16, be1[:, :])
            for name, dst in (("L2_attn_conv_b", convb), ("L2_attn_b_dt", bdt), ("L2_attn_D_param", Dp)):
                st(I[name].rearrange("(m p) -> m p", p=P), 2, dst[:, :])
            st(I["L2_ffn_be1"].rearrange("e (c p) -> (e c) p", p=P), 32, be1f[:, :, :].rearrange("p e c -> p (e c)"))
            n_first = n_st
            big = [[], []]
            big_stage = sb("big_stage", [P, 36, P], c=c)
            wup = sb("wup", [32, D], c=c)
            cen = sb("cen", [P, 16], c=c)

            direct = [
                (WQ[:, :, :].rearrange("p j (s k) -> p (j s) k", s=2), I["L0_attn_W_Q"].rearrange("h d k -> d h k")),
                (WK[:, :, :].rearrange("p j (s k) -> p (j s) k", s=2), I["L0_attn_W_K"].rearrange("h d k -> d h k")),
                (WV[:, :].rearrange("p (h k) -> p h k", k=64), I["L0_attn_W_V"].rearrange("h d k -> d h k")),
                (WO[:, :, :], I["L0_attn_W_O"].rearrange("(j s) k d -> (s k) j d", s=2)),
                (bO[:, :], bcast(I["L0_attn_b_O"], D)),
                (ln1w[:, :], col(I["L0_attn_ln1_w"])),
                (ln1b[:, :], col(I["L0_attn_ln1_b"])),
                (ln2w[:, :], bcast(I["L0_attn_ln2_w"], D)),
                (ln2b[:, :], bcast(I["L0_attn_ln2_b"], D)),
                (Wr0[:, :], I["L0_ffn_Wr"]),
                (br0[:, :], bcast(I["L0_ffn_br"], 16)),
                (W1[:, :, :], I["L0_ffn_W1"].rearrange("e c h -> c e h")),
                (b1[:, :, :].rearrange("p e h -> p (e h)"), bcast(I["L0_ffn_b1"].rearrange("e h -> (e h)"), 2048)),
                (W2[:, :, :], I["L0_ffn_W2"].rearrange("e h o -> h e o")),
                (wup[:, :], I["L1_attn_Wvup"]),
                (Wr1[:, :], I["L1_ffn_router_w"]),
                (br1[:, :], bcast(I["L1_ffn_router_b"], 8)),
                (EW[:, :, :], I["L1_ffn_expert_w"].rearrange("e h d -> h e d")),
                (convw[:, :, :], I["L2_attn_conv_w"].rearrange("(m p) a k -> p m (a k)", p=P)),
                (Aneg[:, :, :], I["L2_attn_A_log"].rearrange("(m p) n -> p m n", p=P)),
                (gamma[:, :], bcast(I["L2_attn_gamma"], D)),
                (beta[:, :], bcast(I["L2_attn_beta"], D)),
                (rw1[:, :], I["L2_ffn_rw1"]),
                (rb1[:, :], col(I["L2_ffn_rb1"])),
                (rw2[:, :], I["L2_ffn_rw2"]),
                (rb2[:, :], bcast(I["L2_ffn_rb2"], 8)),
                (we1[:, :, :], I["L2_ffn_we1"].rearrange("e d h -> d e h")),
                (we2[:, :, :, :].rearrange("p e c d -> p (e c) d"), I["L2_ffn_we2"].rearrange("e (c p) d -> p (e c) d", p=P)),
                (eaw[:, 0:1], col(I["L3_attn_eta_w"])),
                (eaw[:, 1:2], col(I["L3_attn_alpha_w"])),
                (eab[:, 0:1], bcast(I["L3_attn_eta_b"], 1)),
                (eab[:, 1:2], bcast(I["L3_attn_alpha_b"], 1)),
                (gw[:, :], col(I["L3_attn_gate_w"])),
                (gb[:, :], bcast(I["L3_attn_gate_b"], 1)),
            ]
            padded = [
                (b2[0:16, :], I["L0_ffn_b2"]),
                (wqp[:, 0:32], I["L1_attn_Wq"]),
                (wkp[:, 0:32], I["L1_attn_Wk"]),
                (Eb[0:8, :], I["L1_ffn_expert_b"]),
                (be2f[0:8, :], I["L2_ffn_be2"]),
            ]
            fc = I["L3_ffn_w_fc"].rearrange("e (c p) d -> p (e c) d", p=P)
            sfc = I["L3_ffn_shared_fc"].rearrange("(c p) d -> p c d", p=P)
            pj = I["L3_ffn_w_proj"].rearrange("e o f -> o e f")
            spj = I["L3_ffn_shared_proj"].rearrange("o (a f) -> o a f", a=1)

            n_direct = len(direct)
            block = nc.Block()
            with block:
                @block.sync
                def _(sp):
                    for dst, src in loads:
                        sp.dma_start(dst, src).then_inc(s_stage, 16)
                    sp.dma_start(big_stage[:, 0:32, :], fc).then_inc(s_stage, 16)
                    sp.dma_start(big_stage[:, 32:36, :], sfc).then_inc(s_stage, 16)
                    sp.wait_ge(s_zero, 9)
                    for dst, src in padded:
                        sp.dma_start(dst, src).then_inc(s_load, 16)
                    sp.wait_ge(s_cp, n_first + 9)
                    sp.dma_start(big_stage[:, 0:32, :].rearrange("p (e c) f -> p e (c f)", c=4), pj).then_inc(s_stage, 16)
                    sp.dma_start(big_stage[:, 32:36, :].rearrange("p (e c) f -> p e (c f)", c=4), spj).then_inc(s_stage, 16)
                    sp.wait_ge(s_load, 16 * len(padded))
                    sp.wait_ge(s_set, 16 * n_direct)

                @block.scalar
                def _(act):
                    for dst, src in direct:
                        act.dma_start(dst, src).then_inc(s_set, 16)
                    act.wait_ge(s_cp2, 1)
                    nc.scalar.activation(Aneg[:, :, :], Aneg[:, :, :], ACT.Exp).then_inc(s_load, 16)

                @block.gpsimd
                def _(g):
                    for tile in (b2, wqp, wkp, Eb, be2f, WdtT):
                        ap = tile[:, :, :] if len(tile.shape) == 3 else tile[:, :]
                        nc.gpsimd.memset(ap, 0.0).then_inc(s_zero, 1)
                    nc.gpsimd.memset(neg_half[:, :], -0.5).then_inc(s_zero, 1)
                    nc.gpsimd.memset(half_pow[:, :], 0.5).then_inc(s_zero, 1)
                    nc.gpsimd.memset(ones[:, :], 1.0).then_inc(s_zero, 1)
                    nc.gpsimd.memset(ident[:, :], 0.0).then_inc(s_const, 1)
                    nc.gpsimd.memset(tri[:, :], 1.0).then_inc(s_const, 1)
                    nc.gpsimd.memset(causal[:, :], 1.0).then_inc(s_const, 1)
                    nc.gpsimd.memset(headsel[:, :, :], 0.0).then_inc(s_const, 1)
                    nc.gpsimd.memset(halfsel[:, :], 0.0).then_inc(s_const, 1)
                    nc.gpsimd.iota(iota[:, :, :], pattern=[[0, T], [1, 16]], base=0, channel_multiplier=0,
                                   allow_small_or_imprecise_dtypes=True).then_inc(s_const, 1)
                    g.wait_ge(s_const, 6)
                    nc.gpsimd.affine_select(out=ident[:, :], in_=ident[:, :], compare_op=ALU.not_equal, fill=1.0,
                                            base=0, pattern=[[-1, P]], channel_multiplier=1).then_inc(s_const, 1)
                    nc.gpsimd.affine_select(out=tri[:, :], in_=tri[:, :], compare_op=ALU.is_ge, fill=0.0,
                                            base=0, pattern=[[-1, P]], channel_multiplier=1).then_inc(s_const, 1)
                    nc.gpsimd.affine_select(out=causal[:, :], in_=causal[:, :], compare_op=ALU.is_ge, fill=0.0,
                                            base=3 * P, pattern=[[-1, 7 * P]], channel_multiplier=1).then_inc(s_const, 1)
                    g.wait_ge(s_const, 9)
                    for half in range(2):
                        rows = slice(64 * half, 64 * half + 64)
                        nc.gpsimd.affine_select(out=headsel[rows, :, :], in_=headsel[rows, :, :],
                                                compare_op=ALU.not_equal, fill=1.0, base=half,
                                                pattern=[[2, 8], [-1, 16]], channel_multiplier=0).then_inc(s_const, 1)
                        g.wait_ge(s_const, 10 + 2 * half)
                        nc.gpsimd.memset(halfsel[rows, half:half + 1], 1.0).then_inc(s_const, 1)
                        g.wait_ge(s_const, 11 + 2 * half)

                @block.vector
                def _(v):
                    v.wait_ge(s_set, 16 * n_direct)
                    link = linker(v, s_cp2)
                    link(nc.vector.tensor_scalar(Aneg[:, :, :], Aneg[:, :, :], A_LOG_MAX, None, ALU.min))
                    for w in (W1, b1):
                        link(nc.vector.reduce_sum(cen[:, :], w[:, :, :], AX.X))
                        link(nc.vector.tensor_scalar(cen[:, :], cen[:, :], 1.0 / P, None, ALU.mult))
                        link(nc.vector.tensor_tensor(w[:, :, :], w[:, :, :],
                                                     cen[:, :].unsqueeze(2).to_broadcast([P, 16, P]), ALU.subtract))
                    v.wait_ge(s_const, 13)
                    link(nc.vector.tensor_copy(identR[:, :], ident[:, :]))
                    v.wait_ge(s_load, 16 * (len(padded) + 1))
                    link(nc.vector.tensor_scalar(Aneg[:, :, :], Aneg[:, :, :], -1.0, None, ALU.mult))
                    v.wait_ge(s_zero, 9)
                    for n, (slot, rows, cols, dst) in enumerate(plan):
                        v.wait_ge(s_tr, n + 1)
                        nc.vector.tensor_copy(dst, PS[0:cols, n % 2, 0:rows]).then_inc(s_cp, 1)
                    for r in range(18):
                        n = n_first + r
                        v.wait_ge(s_tr, n + 1)
                        dst = fcT[:, r, :] if r < 9 else pjT[:, r - 9, :, :].rearrange("p c d -> p (c d)")
                        nc.vector.tensor_copy(dst, PS[:, n % 2, :]).then_inc(s_cp, 1)
                    v.wait_ge(s_tr, n_first + 19)
                    nc.vector.tensor_copy(wv1[:, :], PS[:, 2, 0:D]).then_inc(s_cp, 1)

                @block.tensor
                def _(pe):
                    pe.wait_ge(s_const, 13)
                    pe.wait_ge(s_stage, 16 * (n_first + 2))
                    for n, (slot, rows, cols, dst) in enumerate(plan):
                        if n >= 2:
                            pe.wait_ge(s_cp, n - 1)
                        nc.tensor.transpose(PS[0:cols, n % 2, 0:rows], stage[0:rows, slot, 0:cols],
                                            ident[0:rows, 0:rows]).then_inc(s_tr, 1)
                    for r in range(18):
                        n = n_first + r
                        pe.wait_ge(s_cp, n - 1)
                        if r == 9:
                            pe.wait_ge(s_stage, 16 * (n_first + 4))
                        for k in range(4):
                            last = nc.tensor.transpose(PS[:, n % 2, k * P:(k + 1) * P],
                                                       big_stage[:, 4 * (r % 9) + k, :], ident[:, :])
                        last.then_inc(s_tr, 1)
                    pe.wait_ge(s_set, 16 * n_direct)
                    nc.tensor.matmul(PS[:, 2, 0:D], wvdT[:, :], wup[:, :], start=True, stop=True).then_inc(s_tr, 1)

        X = sb("X", [P, T, D])
        XN = sb("XN", [P, T, D])
        XNT = sb("XNT", [P, S])
        SA = sb("SA", [P, T, D])
        stats = sb("stats", [P, T, 6])
        mv = sb("mv", [P, T, 2])
        rstd = sb("rstd", [P, T])
        flat = "p t d -> p (t d)"
        loop_sems = len(names)

        def norm_pool(plink, var, rs):
            plink(nc.gpsimd.tensor_scalar(rs, var, EPS, None, ALU.add))
            return nc.gpsimd.tensor_tensor(rs, rs, neg_half[:, 0:rs.shape[1]], ALU.pow)

        def norm_stats(link, src):
            for t in range(T):
                last = nc.vector.bn_stats(stats[:, t, :], src[:, t, :])
            link(last)
            for t in range(T):
                last = nc.vector.bn_aggr(mv[:, t, :], stats[:, t, :])
            return last

        def norm_apply(dst, src):
            for t in range(T):
                last = nc.vector.tensor_scalar(dst[:, t, :], src[:, t, :], mv[:, t, 0:1], rstd[:, t:t + 1],
                                               ALU.subtract, ALU.mult)
            return last

        def transpose_tiles(bank, src):
            for t in range(T):
                last = nc.tensor.transpose(PS[:, bank, t * P:(t + 1) * P], src[:, t, :], ident[:, :])
            return last

        def mm(o, l, r, start=True, stop=True):
            return nc.tensor.matmul(o, l, r, start=start, stop=stop)


        lsems = []

        scope = [ExitStack()]

        def lsem(name):
            h = scope[0].enter_context(nc.semaphore(name))
            lsems.append(h)
            return h

        def end_stage():
            nums = sorted(h.num for h in lsems)
            starts = [n for n in nums if n - 1 not in nums]
            ends = [n for n in nums if n + 1 not in nums]
            for first, last in zip(starts, ends):
                nc.all_engine_barrier(sems_to_clear=range(first, last + 1))
            lsems.clear()
            scope[0].close()
            scope[0] = ExitStack()

        def gate_logits(pe, lhs, w, E, bank):
            for t in range(T):
                last = mm(PS[:, bank, t * E:(t + 1) * E], lhs[:, t * P:(t + 1) * P], w[:, 0:E])
            return last

        LG = sb("LG", [P, T, 16])
        PR = sb("PR", [P, T, 16])
        OH = sb("OH", [P, T, 16])
        OH2 = sb("OH2", [P, T, 16])
        WG = sb("WG", [P, T, 16])
        WGT = sb("WGT", [P, S])
        top8 = sb("top8", [P, T, 8])
        idx8 = sb("idx8", [P, T, 8], U32)
        idxf = sb("idxf", [P, T, 8])
        rt = sb("rt", [P, T, 4])

        def rep(ap, n):
            return ap.unsqueeze(2).to_broadcast([P, T, n])

        def best(link, pick, E, k):
            oh, oh2 = OH[:, :, 0:E], OH2[:, :, 0:E]
            for t in range(T):
                last = nc.vector.max(top8[:, t, :], pick[:, t, :])
            link(last)
            for t in range(T):
                last = nc.vector.max_index(idx8[:, t, :], top8[:, t, :], pick[:, t, :])
            link(last)
            link(nc.vector.tensor_copy(idxf[:, :, :], idx8[:, :, :]))
            if k == 2:
                nc.vector.tensor_tensor(oh2, iota[:, :, 0:E], rep(idxf[:, :, 1], E), ALU.is_equal)
            link(nc.vector.tensor_tensor(oh, iota[:, :, 0:E], rep(idxf[:, :, 0], E), ALU.is_equal))
            if k == 2:
                link(nc.vector.tensor_tensor(oh, oh, oh2, ALU.add))

        def shifted_logits(link, bank, bias, E):
            lg, pr = LG[:, :, 0:E], PR[:, :, 0:E]
            psv = PS[:, bank, 0:T * E].rearrange("p (t e) -> p t e", e=E)
            if bias is None:
                link(nc.vector.tensor_copy(lg, psv))
            else:
                link(nc.vector.tensor_tensor(lg, psv, bias[:, 0:E].unsqueeze(1).to_broadcast([P, T, E]), ALU.add))
            link(nc.vector.reduce_max(rt[:, :, 0], lg, AX.X))
            return nc.vector.tensor_tensor(pr, lg, rep(rt[:, :, 0], E), ALU.subtract)

        def route_share(link, E):
            pr = PR[:, :, 0:E]
            link(nc.vector.tensor_tensor(pr, pr, OH[:, :, 0:E], ALU.mult))
            link(nc.vector.reduce_sum(rt[:, :, 3], pr, AX.X))
            link(nc.vector.reciprocal(rt[:, :, 3], rt[:, :, 3]))
            return nc.vector.tensor_tensor(WG[:, :, 0:E], pr, rep(rt[:, :, 3], E), ALU.mult)

        def route_top(link, E, k, renorm):
            pr, oh = PR[:, :, 0:E], OH[:, :, 0:E]
            link(nc.vector.reduce_sum(rt[:, :, 1], pr, AX.X))
            link(nc.vector.reciprocal(rt[:, :, 2], rt[:, :, 1]))
            link(nc.vector.tensor_tensor(pr, pr, rep(rt[:, :, 2], E), ALU.mult))
            best(link, pr, E, k)
            if not renorm:
                return nc.vector.tensor_tensor(WG[:, :, 0:E], pr, oh, ALU.mult)
            link(nc.vector.tensor_tensor(pr, pr, oh, ALU.mult))
            link(nc.vector.reduce_sum(rt[:, :, 3], pr, AX.X))
            link(nc.vector.tensor_scalar(rt[:, :, 3], rt[:, :, 3], 1e-9, None, ALU.max))
            link(nc.vector.reciprocal(rt[:, :, 3], rt[:, :, 3]))
            return nc.vector.tensor_tensor(WG[:, :, 0:E], pr, rep(rt[:, :, 3], E), ALU.mult)

        def transpose_weights(bank, E):
            for t in range(T):
                last = nc.tensor.transpose(PS[0:E, bank, t * P:(t + 1) * P], WG[:, t, 0:E], ident[:, :])
            return last

        def weighted_biases(bank, E, b):
            for t in range(T):
                last = mm(PS[:, bank, t * P:(t + 1) * P], WGT[0:E, t * P:(t + 1) * P], b[0:E, :])
            return last



        def gate_and_add(link, silu_out, s_ap):
            link(nc.vector.tensor_tensor(silu_out, silu_out, s_ap, ALU.mult))
            link(nc.vector.tensor_tensor(X[:, :, :], X[:, :, :], silu_out, ALU.add))

        def layer0():
            xn_ok, xt_ok, xt_sb = lsem("a0_xn"), lsem("a0_xt"), lsem("a0_xt_sb")
            var, rs = lsem("a0_var"), lsem("a0_rs")
            dv = lsem("a0_dve_steps")
            vp, vs = lsem("a0_v_products"), lsem("a0_v_stored")
            qk, qks = lsem("a0_qk_products"), lsem("a0_qk_stored")
            sc, nm, ex, ee = lsem("a0_scores"), lsem("a0_neg_max"), lsem("a0_exps"), lsem("a0_tail_exps")
            rc, pn, pnB = lsem("a0_inv_sums"), lsem("a0_probsA"), lsem("a0_probsB")
            trA, trB, ptA, ptB = lsem("a0_trA"), lsem("a0_trB"), lsem("a0_ptA"), lsem("a0_ptB")
            pv, zs = lsem("a0_pv"), lsem("a0_z_stored")
            tl, tls, cts, ao = lsem("a0_tail"), lsem("a0_tail_stored"), lsem("a0_ct_stored"), lsem("a0_out")
            tz = lsem("a0_zeroed")
            OFF = [0, P, 3 * P, 6 * P]
            NG = 8 * T
            LAG = 4
            QK_AT = (0, 1)
            r = {k: lsem(f"f0_{k}") for k in ("logits", "shifted", "expd", "weights", "wT", "wT_stored", "bias")}
            hp, hb, sq, hn, ht = (lsem(f"f0_{k}") for k in ("hidden", "biased", "squares", "normed", "hiddenT"))
            gl, yp, ac, gt = (lsem(f"f0_{k}") for k in ("gelus", "outs", "added", "gate"))
            NU = 16
            with ExitStack() as c:
                X1 = sb("X1", [P, T, D], c=c)
                X1T = sb("X1T", [P, S], c=c)
                QT = sb("QT", [P, 2, S], c=c)
                KZ = sb("KZ", [P, 2, 2, S], c=c)
                V = sb("V", [P, 8, T, P], c=c)
                PR0 = sb("PR0", [P, 2, 2, 10 * P], c=c)
                PTS = sb("PTS", [P, 2, 2, S], c=c)
                NM = sb("NM", [P, NG, 2], c=c)
                MX = sb("MX", [P, NG, 2], c=c)
                L = sb("L", [P, NG, 2], c=c)
                E0 = sb("E0", [P, NG, 2], c=c)
                R = sb("R", [P, NG, 2], c=c)
                CC = sb("CC", [P, 3, 3, 16], c=c)
                CT = WGT[:, 0:3 * P].rearrange("p (t q) -> p t q", t=3)
                xtail = sb("xtail", [P, 4], c=c)
                xsum = sb("xsum", [P, 4], c=c)
                VT = sb("VT", [P, 8, 3], c=c)
                VTS = PTS[:, 0, 0, 0:384].rearrange("p (j a h) -> p j a h", j=8, a=3)
                G = sb("G", [P, P], c=c)[:, :]
                four = "p (i e d) -> p i e d"
                HB = KZ[:, :, :, :].rearrange("p a s k -> p (a s k)")[:, 0:3 * S].rearrange(four, i=3, e=4)
                SQ = QT[:, :, :].rearrange("p i (e d) -> p i e d", e=4)
                pair0 = PR0[:, 0, :, :].rearrange("p s k -> p (s k)")
                HN = pair0[:, 0:2 * S].rearrange(four, i=2, e=4)
                GT = pair0[:, 2 * S:4 * S].rearrange(four, i=2, e=4)
                pair1 = PR0[:, 1, :, :].rearrange("p s k -> p (s k)")
                ACC = pair1[:, 0:S].rearrange("p (t d) -> p t d", t=T)
                GS = pair1[:, S:2 * S].rearrange("p (t d) -> p t d", t=T)
                SS = sb("SS", [P, NU, 4], c=c)

                def bank(k, i):
                    return PS[:, k + i % 2, :].rearrange("p (e d) -> p e d", e=4)

                def ps2(g):
                    b0 = 2 * (g % 2)
                    return PS[:, b0:b0 + 2, :]

                with nc.Block() as block:
                    @block.gpsimd
                    def _(g):
                        plink = linker(g, lsem("a0_pool_steps"))
                        nc.gpsimd.memset(KZ[:, :, :, :], 0.0).then_inc(tz, 1)
                        nc.gpsimd.memset(CC[:, :, :, :], 0.0).then_inc(tz, 1)
                        nc.gpsimd.memset(CT, 0.0).then_inc(tz, 1)
                        nc.gpsimd.memset(G, 0.0).then_inc(tz, 1)
                        for k in range(2):
                            g.wait_ge(var, k + 1)
                            norm_pool(plink, mv[:, :, 1], rstd[:, :]).then_inc(rs, 1)
                        for n in range(NG):
                            j, t = divmod(n, T)
                            g.wait_ge(rc, n + 1)
                            p = PR0[:, j % 2, 0, OFF[t]:OFF[t] + (t + 1) * P]
                            nc.gpsimd.tensor_tensor(p, p, R[:, n, 0:1].to_broadcast([P, (t + 1) * P]),
                                                    ALU.mult).then_inc(pn, 1)
                        def unit_norm(i):
                            g.wait_ge(sq, i + 1)
                            plink(norm_pool(plink, SS[:, i, :], SS[:, i, :]))
                            if i >= 2:
                                g.wait_ge(ht, i - 1)
                            else:
                                g.wait_ge(trA, NG)
                                g.wait_ge(trB, NG)
                            nc.gpsimd.tensor_tensor(HN[:, i % 2, :, :], HB[:, i % 3, :, :],
                                                    SS[:, i, :].unsqueeze(2).to_broadcast([P, 4, P]),
                                                    ALU.mult).then_inc(hn, 1)
                        unit_norm(0)
                        unit_norm(1)
                        g.wait_ge(var, 3)
                        norm_pool(plink, mv[:, :, 1], rstd[:, :]).then_inc(rs, 1)
                        for i in range(2, NU):
                            unit_norm(i)

                    @block.tensor
                    def _(pe):
                        pe.wait_ge(xn_ok, 1)
                        transpose_tiles(0, XN).then_inc(xt_ok, 1)
                        pe.wait_ge(xt_sb, 1)
                        gate_logits(pe, XNT, Wr0, 16, 7).then_inc(r["logits"], 1)
                        pe.wait_ge(xn_ok, 2)
                        transpose_tiles(1, X1).then_inc(xt_ok, 1)
                        pe.wait_ge(xt_sb, 2)
                        for i in range(8):
                            t, half = divmod(i, 2)
                            if i >= 2:
                                pe.wait_ge(vs, i - 1)
                            mm(PS[:, 2 + i % 2, :], X1T[:, t * P:(t + 1) * P],
                               WV[:, half * 512:(half + 1) * 512]).then_inc(vp, 1)
                        pe.wait_ge(tls, 1)
                        for j in range(8):
                            last = mm(PS[:, 0, 3 * j:3 * j + 3], WV[:, j * P:(j + 1) * P], xtail[:, 0:3])
                        last.then_inc(tl, 1)
                        pe.wait_ge(tls, 3)
                        for j in range(8):
                            last = mm(PS[0:48, 1, 0:P], PTS[:, 0, 0, 48 * j:48 * j + 48], WO[:, j, :],
                                      start=j == 0, stop=j == 7)
                        last.then_inc(tl, 1)

                        def project(j, which):
                            if j or which:
                                pe.wait_ge(qks, 3 * j + which)
                            w = (WQ, WK)[which]
                            mm(PS[:, 7, :], w[:, j, :], X1T[:, :]).then_inc(qk, 1)

                        def scores(n):
                            j, t = divmod(n, T)
                            if t == 0:
                                pe.wait_ge(qks, 3 * j + 3)
                            if n >= 2:
                                pe.wait_ge(ex, 2 * (n - 1))
                            for s in range(2):
                                last = mm(ps2(n)[:, s, 0:(t + 1) * P], QT[:, j % 2, t * P:(t + 1) * P],
                                          KZ[:, j % 2, s, 0:(t + 1) * P])
                            last.then_inc(sc, 1)

                        def hidden(i):
                            t, g = divmod(i, 4)
                            if i >= 2:
                                pe.wait_ge(hb, i - 1)
                            else:
                                pe.wait_ge(ex, 2 * NG - 2)
                            mm(PS[:, i % 2, :], XNT[:, t * P:(t + 1) * P],
                               W1[:, 4 * g:4 * g + 4, :].rearrange("p e h -> p (e h)")).then_inc(hp, 1)

                        def transposes(n):
                            t = n % T
                            if n >= 1:
                                pe.wait_ge(ptA, n)
                                pe.wait_ge(ptB, n)
                            for s, (tr, done) in enumerate(((trA, pn), (trB, pnB))):
                                pe.wait_ge(done, n + 1)
                                for k in range(t + 1):
                                    a = OFF[t] + k * P
                                    last = nc.tensor.transpose(PS[:, 4 + s, k * P:(k + 1) * P],
                                                               PR0[:, (n // T) % 2, s, a:a + P], ident[:, :])
                                last.then_inc(tr, 1)

                        def values(n):
                            j, t = divmod(n, T)
                            pe.wait_ge(ptA, n + 1)
                            pe.wait_ge(ptB, n + 1)
                            if t == 0 and j:
                                pe.wait_ge(zs, j)
                            for s in range(2):
                                for k in range(t + 1):
                                    last = mm(PS[64 * s:64 * s + 64, 6, t * P:(t + 1) * P],
                                              V[:, j, k, 64 * s:64 * s + 64], PTS[:, n % 2, s, k * P:(k + 1) * P],
                                              start=k == 0, stop=k == t)
                            last.then_inc(pv, 1)

                        pe.wait_ge(vs, 8)
                        pe.wait_ge(tls, 4)
                        pe.wait_ge(r["shifted"], 1)
                        project(0, 0)
                        project(0, 1)
                        for n in range(NG + LAG):
                            if n >= LAG:
                                transposes(n - LAG)
                            if n < NG:
                                scores(n)
                                if n + T < NG and n % T in QK_AT:
                                    project(n // T + 1, QK_AT.index(n % T))
                            if n in (NG, NG + 1):
                                hidden(n - NG)
                            if n >= LAG:
                                values(n - LAG)
                        for t in range(3):
                            last = nc.tensor.transpose(PS[0:48, 3, t * P:(t + 1) * P],
                                                       CC[:, t, :, :].rearrange("p a h -> p (a h)"), ident[:, :])
                        last.then_inc(tl, 1)
                        pe.wait_ge(zs, 8)
                        pe.wait_ge(cts, 1)
                        for t in range(T):
                            for j in range(8):
                                last = mm(PS[:, 2, t * P:(t + 1) * P], V[:, j, t, :], WO[:, j, :],
                                          start=j == 0, stop=j == 7 and t == 3)
                            if t < 3:
                                last = mm(PS[:, 2, t * P:(t + 1) * P], CT[:, t, :], G, start=False, stop=True)
                        last.then_inc(ao, 1)

                        transpose_weights(3, 16).then_inc(r["wT"], 1)
                        for i in range(2, NU + 3):
                            if i < NU:
                                hidden(i)
                            u = i - 2
                            if 0 <= u < NU:
                                pe.wait_ge(hn, u + 1)
                                if u >= 2:
                                    pe.wait_ge(gl, u - 1)
                                for e in range(4):
                                    last = nc.tensor.transpose(bank(4, u)[:, e, :], HN[:, u % 2, e, :], ident[:, :])
                                last.then_inc(ht, 1)
                            if i == 2:
                                pe.wait_ge(r["wT_stored"], 1)
                                weighted_biases(3, 16, b2).then_inc(r["bias"], 1)
                            u = i - 3
                            if 0 <= u:
                                g = u % 4
                                pe.wait_ge(gl, u + 1)
                                if u >= 2:
                                    pe.wait_ge(ac, u - 1)
                                for e in range(4):
                                    last = mm(bank(6, u)[:, e, :], GT[:, u % 2, e, :], W2[:, 4 * g + e, :])
                                last.then_inc(yp, 1)

                    @block.scalar
                    def _(act):
                        act.wait_ge(xt_ok, 1)
                        nc.scalar.activation(XNT[:, :], PS[:, 0, :], ACT.Copy).then_inc(xt_sb, 1)
                        act.wait_ge(xt_ok, 2)
                        nc.scalar.activation(X1T[:, :], PS[:, 1, :], ACT.Identity, bias=ln1b[:, :],
                                             scale=ln1w[:, :]).then_inc(xt_sb, 1)
                        for i in range(8):
                            t, half = divmod(i, 2)
                            act.wait_ge(vp, i + 1)
                            nc.scalar.activation(V[:, 4 * half:4 * half + 4, t, :],
                                                 PS[:, 2 + i % 2, :].rearrange("p (j d) -> p j d", j=4),
                                                 ACT.Copy).then_inc(vs, 1)
                            if i == 2:
                                act.wait_ge(r["shifted"], 1)
                                nc.scalar.activation(PR[:, :, :], PR[:, :, :], ACT.Exp).then_inc(r["expd"], 1)

                        def qk_evac(j, which):
                            act.wait_ge(qk, 2 * j + which + 1)
                            if which == 0:
                                nc.scalar.activation(QT[:, j % 2, :], PS[:, 7, :], ACT.Identity,
                                                     bias=bQ[:, j:j + 1]).then_inc(qks, 1)
                            else:
                                for s in range(2):
                                    r = slice(64 * s, 64 * s + 64)
                                    nc.scalar.activation(KZ[r, j % 2, s, :], PS[r, 7, :], ACT.Identity,
                                                         bias=bK[r, j:j + 1]).then_inc(qks, 1)

                        def exps(n):
                            j, t = divmod(n, T)
                            w = (t + 1) * P
                            act.wait_ge(nm, n + 1)
                            for s in range(2):
                                nc.scalar.activation(PR0[:, j % 2, s, OFF[t]:OFF[t] + w], ps2(n)[:, s, 0:w], ACT.Exp,
                                                     bias=NM[:, n, s:s + 1], scale=0.125,
                                                     accum_out=L[:, n, s:s + 1]).then_inc(ex, 1)
                            nc.scalar.activation(E0[:, n, :], NM[:, n, :], ACT.Exp).then_inc(ee, 1)

                        def squares(i):
                            act.wait_ge(hb, i + 1)
                            if i >= 2:
                                act.wait_ge(sq, i - 1)
                            for e in range(4):
                                last = nc.scalar.activation(SQ[:, i % 2, e, :], HB[:, i % 3, e, :], ACT.Square,
                                                            scale=float(P) ** -0.5, accum_out=SS[:, i, e:e + 1])
                            last.then_inc(sq, 1)

                        act.wait_ge(tz, 4)
                        qk_evac(0, 0)
                        qk_evac(0, 1)
                        for n in range(NG + LAG):
                            if n >= LAG:
                                m = n - LAG
                                act.wait_ge(trA, m + 1)
                                if m >= 2:
                                    act.wait_ge(pv, m - 1)
                                w = (m % T + 1) * P
                                nc.scalar.activation(PTS[:, m % 2, 0, 0:w], PS[:, 4, 0:w], ACT.Copy).then_inc(ptA, 1)
                            if n < NG:
                                exps(n)
                                if n + T < NG and n % T in QK_AT:
                                    qk_evac(n // T + 1, QK_AT.index(n % T))
                            if n in (NG, NG + 1):
                                squares(n - NG)
                        for i in range(2, NU + 2):
                            if i < NU:
                                squares(i)
                            u = i - 2
                            if u >= 0:
                                g = u % 4
                                act.wait_ge(ht, u + 1)
                                if u >= 2:
                                    act.wait_ge(yp, u - 1)
                                for e in range(4):
                                    n = 4 * g + e
                                    last = nc.scalar.activation(GT[:, u % 2, e, :], bank(4, u)[:, e, :], ACT.Gelu,
                                                                bias=be1[:, n:n + 1], scale=g1[:, n:n + 1])
                                last.then_inc(gl, 1)
                        act.wait_ge(ac, NU)
                        nc.scalar.activation(GS, ACC, ACT.Silu).then_inc(gt, 1)


                    @block.vector
                    def _(v):
                        link = linker(v, dv)
                        norm_stats(link, X).then_inc(var, 1)
                        v.wait_ge(rs, 1)
                        norm_apply(XN, X).then_inc(xn_ok, 1)
                        v.wait_ge(xn_ok, 1)
                        norm_stats(link, XN).then_inc(var, 1)
                        v.wait_ge(rs, 2)
                        norm_apply(X1, XN).then_inc(xn_ok, 1)
                        v.wait_ge(xt_sb, 2)
                        link(nc.vector.reduce_sum(xsum[:, 0:T], X1T[:, :].rearrange("p (t q) -> p t q", t=T), AX.X))
                        link(nc.vector.tensor_copy(xtail[:, 2:3], xsum[:, 3:4]))
                        link(nc.vector.tensor_tensor(xtail[:, 1:2], xtail[:, 2:3], xsum[:, 2:3], ALU.add))
                        nc.vector.tensor_tensor(xtail[:, 0:1], xtail[:, 1:2], xsum[:, 1:2], ALU.add).then_inc(tls, 1)
                        v.wait_ge(r["logits"], 1)
                        shifted_logits(link, 7, br0, 16).then_inc(r["shifted"], 1)
                        v.wait_ge(r["expd"], 1)
                        route_top(link, 16, 2, True).then_inc(r["weights"], 1)
                        v.wait_ge(tl, 1)
                        nc.vector.tensor_copy(VT[:, :, :], PS[:, 0, 0:24].rearrange("p (j a) -> p j a", a=3)).then_inc(tls, 1)
                        v.wait_ge(tls, 2)
                        nc.vector.tensor_tensor(VTS, VT[:, :, :].unsqueeze(3).to_broadcast([P, 8, 3, 16]),
                                                headsel[:, :, :].unsqueeze(2).to_broadcast([P, 8, 3, 16]),
                                                ALU.mult).then_inc(tls, 1)
                        v.wait_ge(tl, 2)
                        v.wait_ge(tz, 4)
                        nc.vector.tensor_copy(G[0:48, :], PS[0:48, 1, 0:P]).then_inc(tls, 1)

                        def hidden_bias(i):
                            g = i % 4
                            v.wait_ge(hp, i + 1)
                            if i >= 3:
                                v.wait_ge(hn, i - 2)
                                v.wait_ge(sq, i - 2)
                            else:
                                v.wait_ge(sc, NG)
                            nc.vector.tensor_tensor(HB[:, i % 3, :, :], bank(0, i), b1[:, 4 * g:4 * g + 4, :],
                                                    ALU.add).then_inc(hb, 1)

                        def row_max(n):
                            t = n % T
                            v.wait_ge(sc, n + 1)
                            d = ps2(n)[:, :, t * P:(t + 1) * P]
                            link(nc.vector.tensor_tensor(d, d, tri[:, :].unsqueeze(1).to_broadcast([P, 2, P]), ALU.mult))
                            link(nc.vector.reduce_max(MX[:, n, :], ps2(n)[:, :, 0:(t + 1) * P], AX.X))
                            if t < T - 1:
                                nc.vector.tensor_scalar(NM[:, n, :], MX[:, n, :], 0.0, -0.125, ALU.max,
                                                        ALU.mult).then_inc(nm, 1)
                            else:
                                nc.vector.tensor_scalar(NM[:, n, :], MX[:, n, :], -0.125, None, ALU.mult).then_inc(nm, 1)

                        def z_store(j):
                            v.wait_ge(pv, T * (j + 1))
                            nc.vector.tensor_scalar(V[:, j, :, :].rearrange("p t d -> p (t d)"), PS[:, 6, :],
                                                    bV[:, j:j + 1], None, ALU.add).then_inc(zs, 1)

                        def row_sum(n):
                            j, t = divmod(n, T)
                            v.wait_ge(ex, 2 * n + 2)
                            v.wait_ge(ee, n + 1)
                            link(nc.vector.scalar_tensor_tensor(L[:, n, :], E0[:, n, :], float((T - 1 - t) * P),
                                                                L[:, n, :], ALU.mult, ALU.add))
                            nc.vector.reciprocal(R[:, n, :], L[:, n, :]).then_inc(rc, 1)
                            v.wait_ge(rc, n + 1)
                            p = PR0[:, j % 2, 1, OFF[t]:OFF[t] + (t + 1) * P]
                            nc.vector.tensor_scalar(p, p, R[:, n, 1:2], None, ALU.mult).then_inc(pnB, 1)
                            if t < T - 1:
                                nc.vector.tensor_tensor(CC[:, t, t, 2 * j:2 * j + 2], E0[:, n, :], R[:, n, :],
                                                        ALU.mult).then_inc(tls, 1)

                        for n in range(NG + LAG):
                            if n > LAG and (n - LAG) % T == 0:
                                j = (n - LAG) // T - 1
                                z_store(j)
                            if n >= LAG:
                                m = n - LAG
                                v.wait_ge(trB, m + 1)
                                if m >= 2:
                                    v.wait_ge(pv, m - 1)
                                w = (m % T + 1) * P
                                nc.vector.tensor_copy(PTS[:, m % 2, 1, 0:w], PS[:, 5, 0:w]).then_inc(ptB, 1)
                            if n < NG:
                                row_max(n)
                            if n in (NG, NG + 1):
                                hidden_bias(n - NG)
                            if 1 <= n <= NG:
                                row_sum(n - 1)
                        z_store(7)
                        v.wait_ge(tl, 3)
                        nc.vector.tensor_copy(CT[0:48, :, :], PS[0:48, 3, 0:3 * P].rearrange("p (t q) -> p t q", t=3)).then_inc(cts, 1)
                        v.wait_ge(ao, 1)
                        sa = SA[:, :, :]
                        link(nc.vector.tensor_tensor(sa, PS[:, 2, :].rearrange("p (t d) -> p t d", t=T),
                                                     XN[:, :, :], ALU.add))
                        link(nc.vector.tensor_tensor(sa, sa, bO[:, :].unsqueeze(1).to_broadcast([P, T, D]), ALU.add))
                        norm_stats(link, SA).then_inc(var, 1)
                        hidden_bias(2)
                        v.wait_ge(r["wT"], 1)
                        nc.vector.tensor_copy(WGT[0:16, :], PS[0:16, 3, :]).then_inc(r["wT_stored"], 1)
                        v.wait_ge(rs, 3)
                        link(norm_apply(X1, SA))
                        link(nc.vector.tensor_tensor(X1[:, :, :], X1[:, :, :], ln2w[:, :].unsqueeze(1).to_broadcast([P, T, D]), ALU.mult))
                        link(nc.vector.tensor_tensor(X1[:, :, :], X1[:, :, :], ln2b[:, :].unsqueeze(1).to_broadcast([P, T, D]), ALU.add))
                        link(nc.vector.tensor_tensor(sa, sa, X1[:, :, :], ALU.add))
                        v.wait_ge(r["bias"], 1)
                        v.wait_ge(trA, NG)
                        v.wait_ge(trB, NG)
                        link(nc.vector.tensor_copy(ACC, PS[:, 3, :].rearrange("p (t d) -> p t d", t=T)))
                        for i in range(3, NU + 3):
                            if i < NU:
                                hidden_bias(i)
                            u = i - 3
                            if u >= 0:
                                t, g = divmod(u, 4)
                                v.wait_ge(yp, u + 1)
                                for e in range(4):
                                    ins = nc.vector.scalar_tensor_tensor(ACC[:, t, :], bank(6, u)[:, e, :],
                                                                         WG[:, t, 4 * g + e:4 * g + e + 1],
                                                                         ACC[:, t, :], ALU.mult, ALU.add)
                                    if e < 3:
                                        link(ins)
                                ins.then_inc(ac, 1)
                                v.wait_ge(ac, u + 1)
                        v.wait_ge(gt, 1)
                        gate_and_add(link, GS, SA[:, :, :])

        def layer1():
            dv, pl = lsem("a1_dve_steps"), lsem("a1_pool_steps")
            var, rs, xn, xt, xts = (lsem(f"a1_{k}") for k in ("var", "rstd", "xn", "xT", "xT_stored"))
            qk, qks, vp, vs, sc = (lsem(f"a1_{k}") for k in ("qk", "qk_stored", "v", "v_stored", "scores"))
            sm, fi, fd, nm, ex, inv = (lsem(f"a1_{k}") for k in ("masked", "fills", "filled", "neg_max", "exps", "inv_sums"))
            tr, pt, pv, so = (lsem(f"a1_{k}") for k in ("transposes", "pT", "pv", "s_stored"))
            r = {k: lsem(f"f1_{k}") for k in ("logits", "shifted", "expd", "weights", "wT", "wT_stored", "bias")}
            yp, ad, gt = (lsem(f"f1_{k}") for k in ("outs", "added", "gate"))
            NE = 8
            SCALE = 32.0 ** -0.5
            with ExitStack() as c:
                QK = sb("QK", [P, 2, S], c=c)
                V = sb("V1", [P, T, D], c=c)
                SC = sb("SC", [P, T, S], c=c)
                FI = sb("FI", [P, T, S], c=c)
                PB = sb("PB", [P, T, S], c=c)
                PT = sb("PT", [P, T, S], c=c)
                NM = sb("NM1", [P, T], c=c)
                MX = sb("MX1", [P, T], c=c)
                L = sb("L1", [P, T], c=c)
                R = sb("R1", [P, T], c=c)
                ACC = sb("ACC1", [P, T, D], c=c)
                GS = sb("GS1", [P, T, D], c=c)
                with nc.Block() as block:
                    @block.gpsimd
                    def _(g):
                        plink = linker(g, pl)
                        g.wait_ge(var, 1)
                        norm_pool(plink, mv[:, :, 1], rstd[:, :]).then_inc(rs, 1)
                        for t in range(T):
                            g.wait_ge(fi, t + 1)
                            nc.gpsimd.tensor_tensor(SC[:, t, :], SC[:, t, :], FI[:, t, :], ALU.add).then_inc(fd, 1)

                    @block.tensor
                    def _(pe):
                        pe.wait_ge(xn, 1)
                        transpose_tiles(0, XN).then_inc(xt, 1)
                        pe.wait_ge(xts, 1)
                        for i, w in enumerate((wqp, wkp)):
                            mm(PS[:, 1 + i, :], w[:, :], XNT[:, :]).then_inc(qk, 1)
                        gate_logits(pe, XNT, Wr1, NE, 0).then_inc(r["logits"], 1)
                        for t in range(T):
                            last = mm(PS[:, 3, t * P:(t + 1) * P], XNT[:, t * P:(t + 1) * P], wv1[:, :])
                        last.then_inc(vp, 1)
                        pe.wait_ge(qks, 2)
                        for t in range(T):
                            mm(PS[:, 4 + t, :], QK[:, 0, t * P:(t + 1) * P], QK[:, 1, :]).then_inc(sc, 1)

                        def expert(e):
                            if e == 2:
                                pe.wait_ge(vs, 1)
                            if e >= 3:
                                pe.wait_ge(ad, e - 2)
                            for t in range(T):
                                last = mm(PS[:, 1 + e % 3, t * P:(t + 1) * P], XNT[:, t * P:(t + 1) * P], EW[:, e, :])
                            last.then_inc(yp, 1)

                        for e in range(3):
                            expert(e)
                        pe.wait_ge(r["weights"], 1)
                        transpose_weights(0, NE).then_inc(r["wT"], 1)
                        pe.wait_ge(r["wT_stored"], 1)
                        weighted_biases(0, NE, Eb).then_inc(r["bias"], 1)

                        def transposes(t):
                            pe.wait_ge(ex, t + 1)
                            pe.wait_ge(sm, t + 1)
                            for kt in range(T):
                                last = nc.tensor.transpose(PS[:, 4 + t, kt * P:(kt + 1) * P],
                                                           PB[:, t, kt * P:(kt + 1) * P], ident[:, :])
                            last.then_inc(tr, 1)

                        def values(t):
                            pe.wait_ge(pt, t + 1)
                            for kt in range(T):
                                last = mm(PS[:, 4 + t, 0:P], PT[:, t, kt * P:(kt + 1) * P], V[:, kt, :],
                                          start=kt == 0, stop=kt == T - 1)
                            last.then_inc(pv, 1)
                        for t in range(T):
                            transposes(t)
                            expert(3 + t)
                            values(t)
                        expert(7)

                    @block.scalar
                    def _(act):
                        act.wait_ge(xt, 1)
                        nc.scalar.activation(XNT[:, :], PS[:, 0, :], ACT.Copy).then_inc(xts, 1)
                        for i in range(2):
                            act.wait_ge(qk, i + 1)
                            nc.scalar.activation(QK[:, i, :], PS[:, 1 + i, :], ACT.Copy).then_inc(qks, 1)
                        act.wait_ge(r["shifted"], 1)
                        nc.scalar.activation(PR[:, :, 0:NE], PR[:, :, 0:NE], ACT.Exp).then_inc(r["expd"], 1)
                        act.wait_ge(vp, 1)
                        nc.scalar.activation(V[:, :, :].rearrange(flat), PS[:, 3, :], ACT.Copy).then_inc(vs, 1)

                        def store_s(t):
                            act.wait_ge(pv, t + 1)
                            act.wait_ge(inv, t + 1)
                            nc.scalar.activation(SA[:, t, :], PS[:, 4 + t, 0:P], ACT.Copy,
                                                 scale=R[:, t:t + 1]).then_inc(so, 1)
                        for t in range(T):
                            act.wait_ge(nm, t + 1)
                            nc.scalar.activation(PB[:, t, :], SC[:, t, :], ACT.Exp, bias=NM[:, t:t + 1],
                                                 accum_out=L[:, t:t + 1]).then_inc(ex, 1)
                        for t in range(T):
                            act.wait_ge(tr, t + 1)
                            nc.scalar.activation(PT[:, t, :], PS[:, 4 + t, :], ACT.Copy).then_inc(pt, 1)
                            if t:
                                store_s(t - 1)
                        store_s(T - 1)
                        act.wait_ge(ad, NE)
                        nc.scalar.activation(GS[:, :, :], ACC[:, :, :], ACT.Silu).then_inc(gt, 1)

                    @block.vector
                    def _(v):
                        link = linker(v, dv)
                        norm_stats(link, X).then_inc(var, 1)
                        v.wait_ge(rs, 1)
                        norm_apply(XN, X).then_inc(xn, 1)

                        def expd():
                            for t in range(T):
                                v.wait_ge(sc, t + 1)
                                a = (T - 1 - t) * P
                                nc.vector.scalar_tensor_tensor(SC[:, t, :], PS[:, 4 + t, :], SCALE,
                                                               causal[:, a:a + S], ALU.mult, ALU.mult).then_inc(sm, 1)
                                v.wait_ge(sm, t + 1)
                                nc.vector.tensor_scalar(FI[:, t, :], SC[:, t, :], 0.0, NEG, ALU.is_equal,
                                                        ALU.mult).then_inc(fi, 1)
                            v.wait_ge(r["expd"], 1)

                        def row_max(t):
                            v.wait_ge(fd, t + 1)
                            link(nc.vector.reduce_max(MX[:, t:t + 1], SC[:, t, :], AX.X))
                            nc.vector.tensor_scalar(NM[:, t:t + 1], MX[:, t:t + 1], -1.0, None, ALU.mult).then_inc(nm, 1)

                        v.wait_ge(r["logits"], 1)
                        shifted_logits(link, 0, br1, NE).then_inc(r["shifted"], 1)
                        expd()
                        row_max(0)
                        row_max(1)
                        route_top(link, NE, 1, False).then_inc(r["weights"], 1)
                        row_max(2)
                        v.wait_ge(r["wT"], 1)
                        nc.vector.tensor_copy(WGT[0:NE, :], PS[0:NE, 0, :]).then_inc(r["wT_stored"], 1)
                        row_max(3)
                        v.wait_ge(r["bias"], 1)
                        link(nc.vector.tensor_copy(ACC[:, :, :].rearrange(flat), PS[:, 0, :]))
                        for e in range(NE):
                            v.wait_ge(yp, e + 1)
                            if e:
                                v.wait_ge(ad, e)
                            for t in range(T):
                                last = nc.vector.scalar_tensor_tensor(ACC[:, t, :], PS[:, 1 + e % 3, t * P:(t + 1) * P],
                                                                      WG[:, t, e:e + 1], ACC[:, t, :], ALU.mult, ALU.add)
                            last.then_inc(ad, 1)
                            if e < T:
                                v.wait_ge(ex, e + 1)
                                nc.vector.reciprocal(R[:, e:e + 1], L[:, e:e + 1]).then_inc(inv, 1)
                        v.wait_ge(gt, 1)
                        v.wait_ge(so, T)
                        gate_and_add(link, GS[:, :, :], SA[:, :, :])

        def layer2():
            dv, pl, ac = lsem("a2_dve_steps"), lsem("a2_pool_steps"), lsem("a2_act_steps")
            var, rs, xn, xt, xts = (lsem(f"a2_{k}") for k in ("var", "rstd", "xn", "xT", "xT_stored"))
            zr, xz, xm, cv, zg, xs = (lsem(f"a2_{k}") for k in ("zeroed", "xz", "x_stored", "conv", "z_silus", "x_silus"))
            db, dbs, bcr = (lsem(f"a2_{k}") for k in ("dbc", "dbc_stored", "bc_split"))
            dtp, dta, dte, dtl, dtx = (lsem(f"a2_{k}") for k in ("dt_raw", "dt_abs", "dt_exp", "dt_log", "dt_x"))
            bp, cp = lsem("a2_b_rows"), lsem("a2_c_rows")
            bm, ex, scn, hc, ya = (lsem(f"a2_{k}") for k in ("inputs", "decays", "scans", "outs", "y"))
            yg, wo = lsem("a2_gated"), lsem("a2_projected")
            r = {k: lsem(f"f2_{k}") for k in ("logits", "shifted", "expd", "weights", "wT", "wT_stored", "bias")}
            r1, r1s, hp, hs, yp, ad, gt = (lsem(f"f2_{k}") for k in (
                "router", "router_stored", "hidden", "silus", "outs", "added", "gate"))
            NS, NE = 16, 8
            LEAD = 2
            with ExitStack() as c:
                XM = sb("XM", [P, 2, S], c=c)
                ZS = sb("ZS", [P, 2, S], c=c)
                DT = sb("DT", [P, 2, S], c=c)
                DTX = sb("DTX", [P, 2, S], c=c)
                DAS = sb("DAS", [P, 8 * S + 4], c=c)
                H = sb("H", [P, 2, 2, S], c=c)
                BCR = sb("BCR", [96, 2, S], F32R, c=c)
                ACC = sb("ACC2", [P, T, D], c=c)
                H1 = sb("H1", [P, S], c=c)
                HH = sb("HH", [P, 2, 4, S], c=c)
                DA = DAS[:, 0:8 * S].rearrange("p (i m s) -> p i m s", i=4, m=2)
                XP = DAS[:, 6 * S:8 * S + 4].rearrange("p (m s) -> p m s", m=2)
                DBC = DAS[0:96, 4 * S:5 * S]
                E, LN = DA[:, 0, :, :], DA[:, 1, :, :]
                Y = [SA[:, :, :].rearrange(flat), H1[:, :]]
                GS = H1[:, :].rearrange("p (t d) -> p t d", t=T)
                with nc.Block() as block:
                    @block.gpsimd
                    def _(g):
                        plink = linker(g, pl)
                        nc.gpsimd.memset(XP[:, :, :], 0.0).then_inc(zr, 1)
                        g.wait_ge(var, 1)
                        norm_pool(plink, mv[:, :, 1], rstd[:, :]).then_inc(rs, 1)
                        g.wait_ge(r["logits"], 1)
                        for m in range(2):
                            g.wait_ge(xs, m + 1)
                            nc.gpsimd.tensor_tensor(Y[m], XM[:, m, :], Dp[:, m:m + 1].to_broadcast([P, S]),
                                                    ALU.mult).then_inc(ya, 1)
                        for n in range(NS):
                            for m in range(2):
                                g.wait_ge(hc, 2 * n + m + 1)
                                g.wait_ge(ya, 2 * n + m + 1)
                                nc.gpsimd.tensor_tensor(Y[m], Y[m], H[:, n % 2, m, :], ALU.add).then_inc(ya, 1)
                        g.wait_ge(var, 2)
                        norm_pool(plink, mv[:, :, 1], rstd[:, :]).then_inc(rs, 1)

                    @block.tensor
                    def _(pe):
                        pe.wait_ge(xn, 1)
                        transpose_tiles(7, XN).then_inc(xt, 1)
                        pe.wait_ge(xts, 1)
                        for m in range(4):
                            mm(PS[:, m, :], WinT[:, m, :], XNT[:, :]).then_inc(xz, 1)
                        mm(PS[:, 6, :], rw1[:, :], XNT[:, :]).then_inc(r1, 1)

                        def hidden(n):
                            e, k = divmod(n, 4)
                            if n >= 4:
                                pe.wait_ge(hs, n - 3)
                            elif n < 2:
                                pe.wait_ge(zg, n + 1)
                            mm(PS[:, 2 + n % 4, :], we1[:, e, k * P:(k + 1) * P], XNT[:, :]).then_inc(hp, 1)

                        def outs(n):
                            u, t = divmod(n, 4)
                            if t == 0:
                                pe.wait_ge(hs, 4 * u + 4)
                                if u >= 2:
                                    pe.wait_ge(ad, u - 1)
                            for k in range(4):
                                last = mm(PS[:, 6 + u % 2, t * P:(t + 1) * P], HH[:, u % 2, k, t * P:(t + 1) * P],
                                          we2[:, u, k, :], start=k == 0, stop=k == 3)
                            if t == 3:
                                last.then_inc(yp, 1)

                        def rows(n, k, done):
                            i = 64 + NS * k + n
                            for part in range(2):
                                last = mm(PS[:, k, :], identR[0:96, i:i + 1].to_broadcast([96, P]), BCR[:, part, :],
                                          start=part == 0, stop=part == 1)
                            last.then_inc(done, 1)

                        for n in range(3):
                            hidden(n)
                        pe.wait_ge(r1s, 1)
                        gate_logits(pe, H1, rw2, NE, 7).then_inc(r["logits"], 1)
                        hidden(3)
                        pe.wait_ge(xs, 2)
                        for m in range(2):
                            last = mm(PS[0:96, 0, :], WxT[:, m, :], XM[:, m, :], start=m == 0, stop=m == 1)
                        last.then_inc(db, 1)
                        hidden(4)
                        pe.wait_ge(dbs, 1)
                        for m in range(2):
                            mm(PS[:, m, :], WdtT[0:96, m, :], DBC).then_inc(dtp, 1)
                        for n in range(5, 8):
                            hidden(n)
                        pe.wait_ge(bcr, 1)
                        pe.wait_ge(dta, 2)
                        rows(0, 0, bp)
                        rows(0, 1, cp)
                        pe.wait_ge(r["weights"], 1)
                        transpose_weights(6, NE).then_inc(r["wT"], 1)
                        pe.wait_ge(r["wT_stored"], 1)
                        weighted_biases(6, NE, be2f).then_inc(r["bias"], 1)

                        pe.wait_ge(r["bias"], 2)
                        for n in range(NS):
                            work = [(outs, 2 * n), (outs, 2 * n + 1)]
                            if 2 * n + 4 * LEAD < 4 * NE:
                                if n % 2:
                                    work += [(hidden, 2 * n - 2 + 4 * LEAD + k) for k in range(4)]
                            if n + 1 < NS:
                                pe.wait_ge(bm, 2 * n + 2)
                                rows(n + 1, 0, bp)
                            half = len(work) // 2
                            for f, i in work[:half]:
                                f(i)
                            if n + 1 < NS:
                                pe.wait_ge(hc, 2 * n + 2)
                                rows(n + 1, 1, cp)
                            for f, i in work[half:]:
                                f(i)
                        pe.wait_ge(yg, 1)
                        for t in range(T):
                            for m in range(2):
                                last = mm(PS[:, 0, t * P:(t + 1) * P], H[:, 0, m, t * P:(t + 1) * P], WoutT[:, m, :],
                                          start=m == 0, stop=m == 1)
                        last.then_inc(wo, 1)

                    @block.scalar
                    def _(act):
                        alink = linker(act, ac)
                        act.wait_ge(xt, 1)
                        nc.scalar.activation(XNT[:, :], PS[:, 7, :], ACT.Copy).then_inc(xts, 1)
                        act.wait_ge(zr, 1)
                        for m in range(2):
                            act.wait_ge(xz, m + 1)
                            nc.scalar.activation(XP[:, m, 1:S + 1], PS[:, m, :], ACT.Copy).then_inc(xm, 1)
                        for m in range(2):
                            act.wait_ge(xz, m + 3)
                            nc.scalar.activation(ZS[:, m, :], PS[:, 2 + m, :], ACT.Silu).then_inc(zg, 1)
                        act.wait_ge(r1, 1)
                        nc.scalar.activation(H1[:, :], PS[:, 6, :], ACT.Silu, bias=rb1[:, :]).then_inc(r1s, 1)

                        def hidden(n):
                            e, k = divmod(n, 4)
                            act.wait_ge(hp, n + 1)
                            if e >= 2 and k == 0:
                                act.wait_ge(yp, e - 1)
                            nc.scalar.activation(HH[:, e % 2, k, :], PS[:, 2 + n % 4, :], ACT.Silu,
                                                 bias=be1f[:, e, k:k + 1]).then_inc(hs, 1)

                        hidden(0)
                        for m in range(2):
                            act.wait_ge(cv, m + 1)
                            nc.scalar.activation(XM[:, m, :], H[:, 0, m, :], ACT.Silu,
                                                 bias=convb[:, m:m + 1]).then_inc(xs, 1)
                        hidden(1)
                        hidden(2)
                        act.wait_ge(db, 1)
                        nc.scalar.activation(DBC, PS[0:96, 0, :], ACT.Copy).then_inc(dbs, 1)
                        hidden(3)
                        hidden(4)
                        for m in range(2):
                            act.wait_ge(dtp, m + 1)
                            nc.scalar.activation(DT[:, m, :], PS[:, m, :], ACT.Relu, bias=bdt[:, m:m + 1])
                            nc.scalar.activation(E[:, m, :], PS[:, m, :], ACT.Abs, bias=bdt[:, m:m + 1]).then_inc(dta, 1)
                        act.wait_ge(dta, 2)
                        nc.scalar.activation(E, E, ACT.Exp, scale=-1.0).then_inc(dte, 1)
                        act.wait_ge(r["shifted"], 1)
                        nc.scalar.activation(PR[:, :, 0:NE], PR[:, :, 0:NE], ACT.Exp).then_inc(r["expd"], 1)
                        act.wait_ge(dte, 1)
                        nc.scalar.activation(LN, E, ACT.Ln, bias=1.0).then_inc(dtl, 1)

                        def decays(n):
                            if n >= 4:
                                act.wait_ge(scn, 2 * (n - 3))
                            elif n == 2:
                                act.wait_ge(dtp, 2)
                                act.wait_ge(bcr, 1)
                            for m in range(2):
                                nc.scalar.activation(DA[:, n % 4, m, :], DT[:, m, :], ACT.Exp,
                                                     scale=Aneg[:, m, n:n + 1]).then_inc(ex, 1)
                        act.wait_ge(dtx, 1)
                        decays(0)
                        decays(1)
                        for n in range(0, NS, 2):
                            if n + 2 < NS:
                                decays(n + 2)
                                decays(n + 3)
                            if n == 0:
                                for k in range(5, 4 * LEAD):
                                    hidden(k)
                            if 2 * n + 4 * LEAD < 4 * NE:
                                for k in range(4):
                                    hidden(2 * n + 4 * LEAD + k)
                        act.wait_ge(ad, NE)
                        act.wait_ge(yg, 1)
                        nc.scalar.activation(GS, ACC[:, :, :], ACT.Silu).then_inc(gt, 1)

                    @block.vector
                    def _(v):
                        link = linker(v, dv)
                        norm_stats(link, X).then_inc(var, 1)
                        v.wait_ge(rs, 1)
                        norm_apply(XN, X).then_inc(xn, 1)
                        for m in range(2):
                            v.wait_ge(xm, m + 1)
                            o = H[:, 0, m, :]
                            link(nc.vector.tensor_scalar(o, XP[:, m, 0:S], convw[:, m, 0:1], None, ALU.mult))
                            link(nc.vector.scalar_tensor_tensor(o, XP[:, m, 1:S + 1], convw[:, m, 1:2], o, ALU.mult, ALU.add))
                            nc.vector.scalar_tensor_tensor(o, XP[:, m, 2:S + 2], convw[:, m, 2:3], o, ALU.mult,
                                                           ALU.add).then_inc(cv, 1)
                        v.wait_ge(r["logits"], 1)
                        shifted_logits(link, 7, rb2, NE).then_inc(r["shifted"], 1)
                        best(link, LG[:, :, 0:NE], NE, 2)
                        v.wait_ge(dbs, 1)
                        link(nc.vector.tensor_copy(BCR[:, 0, :], DBC))
                        nc.vector.tensor_tensor(BCR[:, 1, :], DBC, BCR[:, 0, :].bitcast(F32), ALU.subtract).then_inc(bcr, 1)
                        v.wait_ge(dte, 1)
                        link(nc.vector.tensor_scalar(DTX[:, :, :], E, 1.0, -1.0, ALU.add, ALU.add))
                        link(nc.vector.tensor_tensor(DTX[:, :, :], E, DTX[:, :, :], ALU.subtract))
                        v.wait_ge(r["expd"], 1)
                        route_share(link, NE).then_inc(r["weights"], 1)
                        v.wait_ge(dta, 2)
                        link(nc.vector.tensor_tensor(DT[:, :, :], DT[:, :, :], DTX[:, :, :], ALU.add))
                        v.wait_ge(dtl, 1)
                        nc.vector.tensor_tensor(DT[:, :, :], DT[:, :, :], LN, ALU.add).then_inc(dtx, 1)
                        v.wait_ge(r["wT"], 1)
                        nc.vector.tensor_copy(WGT[0:NE, :], PS[0:NE, 6, :]).then_inc(r["wT_stored"], 1)
                        v.wait_ge(dtx, 1)
                        v.wait_ge(xs, 2)
                        nc.vector.tensor_tensor(DTX[:, :, :], DT[:, :, :], XM[:, :, :], ALU.mult).then_inc(dtx, 1)
                        v.wait_ge(r["bias"], 1)
                        nc.vector.tensor_tensor(ACC[:, :, :].rearrange(flat), PS[:, 6, :], XN[:, :, :].rearrange(flat),
                                                ALU.add).then_inc(r["bias"], 1)

                        def add_expert(e):
                            v.wait_ge(yp, e + 1)
                            if e:
                                v.wait_ge(ad, e)
                            else:
                                v.wait_ge(r["bias"], 2)
                            for t in range(T):
                                last = nc.vector.scalar_tensor_tensor(ACC[:, t, :], PS[:, 6 + e % 2, t * P:(t + 1) * P],
                                                                      WG[:, t, e:e + 1], ACC[:, t, :], ALU.mult, ALU.add)
                            last.then_inc(ad, 1)

                        v.wait_ge(dtx, 2)
                        for n in range(NS):
                            v.wait_ge(bp, n + 1)
                            for m in range(2):
                                if n >= 2:
                                    v.wait_ge(ya, 2 * n + m - 1)
                                nc.vector.tensor_tensor(H[:, n % 2, m, :], DTX[:, m, :], PS[:, 0, :], ALU.mult).then_inc(bm, 1)
                            for m in range(2):
                                v.wait_ge(bm, 2 * n + m + 1)
                                v.wait_ge(ex, 2 * n + m + 1)
                                nc.vector.tensor_tensor_scan(H[:, n % 2, m, :], DA[:, n % 4, m, :],
                                                             H[:, n % 2, m, :], 0.0, ALU.mult, ALU.add).then_inc(scn, 1)
                            v.wait_ge(cp, n + 1)
                            for m in range(2):
                                v.wait_ge(scn, 2 * n + m + 1)
                                nc.vector.tensor_tensor(H[:, n % 2, m, :], H[:, n % 2, m, :], PS[:, 1, :],
                                                        ALU.mult).then_inc(hc, 1)
                            if n >= 3 and n % 2:
                                add_expert((n - 3) // 2)
                        for m in range(2):
                            v.wait_ge(ya, 2 * NS + m + 1)
                            last = nc.vector.tensor_tensor(H[:, 0, m, :], Y[m], ZS[:, m, :], ALU.mult)
                        last.then_inc(yg, 1)
                        add_expert(NE - 1)
                        v.wait_ge(wo, 1)
                        sa = SA[:, :, :]
                        link(nc.vector.tensor_tensor(sa, PS[:, 0, :].rearrange("p (t d) -> p t d", t=T), XN[:, :, :], ALU.add))
                        norm_stats(link, SA).then_inc(var, 1)
                        v.wait_ge(rs, 2)
                        link(norm_apply(SA, SA))
                        link(nc.vector.tensor_tensor(sa, sa, gamma[:, :].unsqueeze(1).to_broadcast([P, T, D]), ALU.mult))
                        link(nc.vector.tensor_tensor(sa, sa, beta[:, :].unsqueeze(1).to_broadcast([P, T, D]), ALU.add))
                        v.wait_ge(gt, 1)
                        gate_and_add(link, GS, SA[:, :, :])

        def layer3():
            dv, pl = lsem("a3_dve_steps"), lsem("a3_pool_steps")
            var, rs, xn, xt, xts = (lsem(f"a3_{k}") for k in ("var", "rstd", "xn", "xT", "xT_stored"))
            ns, kr, km, kms, ea, eas, sg, sm, co, gp, gs_, gate = (lsem(f"a3_{k}") for k in (
                "norms", "key_scales", "key_means", "key_means_stored", "rates", "rates_shifted", "sigmoids",
                "masked", "rate_sums", "gate_parts", "gate_shifted", "gates"))
            gsum = lsem("a3_gate_sums")
            ready, op, ot, h1, hs, vt, dg, eb, nq, nn, nrm, srt = (lsem(f"a3_{k}") for k in (
                "ready", "outs", "outs_stored", "hidden", "silus", "targets", "diag", "err_rows", "squares",
                "norm_sum", "norm_stored", "norm_root"))
            fo, fos = lsem("a3_final"), lsem("a3_final_stored")
            r = {k: lsem(f"f3_{k}") for k in ("logits", "shifted", "expd")}
            hp, rl, sqs, yp, ad, gt = (lsem(f"f3_{k}") for k in (
                "hidden", "relus", "squares", "outs", "added", "gate"))
            NE = 9
            CH = 64
            NC = S // CH
            with ExitStack() as c:
                XK = sb("XK", [P, NC, CH + 1], c=c)
                KM = sb("KM", [P, NC], c=c)
                NSQ = sb("NSQ", [P, T], c=c)
                KR = sb("KR", [P, T, 2], c=c)
                SQJ = sb("SQJ", [P, T, D], c=c)
                SG = sb("SG", [P, T, 2], c=c)
                SM = sb("SM", [P, 2, T, 2], c=c)
                EA = sb("EA", [P, 2, NC], c=c)
                GK = sb("GK", [P, NC], c=c)
                CA = sb("CA", [P, NC], c=c)
                KB = sb("KB", [P, NC], c=c)
                N = sb("N", [P, P], c=c)
                NA = sb("NA", [P, P], c=c)
                N2 = sb("N2", [P, P], c=c)
                NJ = sb("NJ", [P, P], c=c)
                DG = sb("DG", [P, P], c=c)
                OT = sb("OT", [P, S], c=c)
                HS = sb("HS", [P, S], c=c)
                OS = sb("OS", [P, NC], c=c)
                HA = sb("HA", [P, NC], c=c)
                ER = sb("ER", [P, 2], c=c)
                NQ = sb("NQ", [P, NC], c=c)
                NR = sb("NR", [P, NC], c=c)
                ACC = sb("ACC3", [P, T, D], c=c)
                GS = sb("GS3", [P, T, D], c=c)
                RL = sb("RL", [P, 2, S], c=c)
                HH = sb("HH3", [P, 2, 4, S], c=c)
                STEPS = 5
                assert STEPS * NC == 4 * (NE + 1)
                with nc.Block() as block:
                    @block.gpsimd
                    def _(g):
                        plink = linker(g, pl)
                        g.wait_ge(var, 1)
                        norm_pool(plink, mv[:, :, 1], rstd[:, :]).then_inc(rs, 1)
                        g.wait_ge(ns, T)
                        nc.gpsimd.tensor_tensor(NSQ[:, :], NSQ[:, :], half_pow[:, 0:T], ALU.pow).then_inc(ns, 1)
                        for k in range(NC):
                            g.wait_ge(nrm, k + 1)
                            nc.gpsimd.tensor_tensor(NR[:, k:k + 1], NR[:, k:k + 1], half_pow[:, 0:1], ALU.pow).then_inc(srt, 1)

                    @block.tensor
                    def _(pe):
                        pe.wait_ge(xn, 1)
                        transpose_tiles(0, XN).then_inc(xt, 1)
                        pe.wait_ge(xts, 1)
                        for t in range(T):
                            last = mm(PS[:, 2, 2 * t:2 * t + 2], XNT[:, t * P:(t + 1) * P], eaw[:, :])
                        last.then_inc(ea, 1)
                        gate_logits(pe, XNT, WrT3, 8, 7).then_inc(r["logits"], 1)
                        pe.wait_ge(kr, 1)
                        for t in range(T):
                            last = mm(PS[:, 1, 2 * t:2 * t + 2], XN[:, t, :], KR[:, t, :])
                        last.then_inc(km, 1)
                        pe.wait_ge(sm, 1)
                        mm(PS[:, 3, 0:2 * NC], ones[:, :], SM[:, :, :, :].rearrange("p w t h -> p (w t h)")).then_inc(co, 1)
                        pe.wait_ge(gp, 1)
                        mm(PS[:, 4, 0:NC], ones[:, :], GK[:, :]).then_inc(gsum, 1)
                        def experts(i):
                            e, k = divmod(i, 4)
                            if e < NE:
                                if i >= 4:
                                    pe.wait_ge(sqs, i - 3)
                                mm(PS[:, i % 4, :], fcT[:, e, k * P:(k + 1) * P], XNT[:, :]).then_inc(hp, 1)
                            u = e - 1
                            if u >= 0:
                                if k == 0:
                                    pe.wait_ge(sqs, 4 * u + 4)
                                    if u >= 2:
                                        pe.wait_ge(ad, u - 1)
                                for q in range(4):
                                    last = mm(PS[:, 4 + u % 2, k * P:(k + 1) * P], HH[:, u % 2, q, k * P:(k + 1) * P],
                                              pjT[:, u, q, :], start=q == 0, stop=q == 3)
                                if k == 3:
                                    last.then_inc(yp, 1)

                        for k in range(NC):
                            pe.wait_ge(ready, k + 1)
                            mm(PS[:, 7, 0:CH + 1], N[:, :], XK[:, k, :]).then_inc(op, 1)
                            experts(STEPS * k)
                            pe.wait_ge(ot, k + 1)
                            mm(PS[:, 6, 0:CH], vg1T[:, :], OT[:, k * CH:(k + 1) * CH]).then_inc(h1, 1)
                            experts(STEPS * k + 1)
                            pe.wait_ge(hs, k + 1)
                            mm(PS[:, 6, 0:1], vg2T[:, :], HA[:, k:k + 1]).then_inc(vt, 1)
                            experts(STEPS * k + 2)
                            pe.wait_ge(dg, k + 1)
                            mm(PS[:, 6, 0:P], ones[:, :], DG[:, :]).then_inc(eb, 1)
                            experts(STEPS * k + 3)
                            pe.wait_ge(nq, k + 1)
                            mm(PS[:, 6, 0:1], ones[:, :], NQ[:, k:k + 1]).then_inc(nn, 1)
                            experts(STEPS * k + 4)
                        pe.wait_ge(nrm, NC)
                        for t in range(T):
                            mm(PS[:, 6, t * P:(t + 1) * P], HS[:, t * P:(t + 1) * P], vg2T[:, :], start=True, stop=False)
                            last = mm(PS[:, 6, t * P:(t + 1) * P], OT[:, t * P:(t + 1) * P], ident[:, :], start=False, stop=True)
                        last.then_inc(fo, 1)

                    @block.scalar
                    def _(act):
                        act.wait_ge(xt, 1)
                        nc.scalar.activation(XNT[:, :], PS[:, 0, :], ACT.Copy).then_inc(xts, 1)
                        for t in range(T):
                            nc.scalar.activation(SQJ[:, t, :], XN[:, t, :], ACT.Square,
                                                 accum_out=NSQ[:, t:t + 1]).then_inc(ns, 1)
                        act.wait_ge(eas, 1)
                        nc.scalar.activation(SG[:, :, :], SG[:, :, :], ACT.Sigmoid).then_inc(sg, 1)
                        act.wait_ge(gs_, 1)
                        nc.scalar.activation(GK[:, :], GK[:, :], ACT.Sigmoid).then_inc(gate, 1)
                        act.wait_ge(r["shifted"], 1)
                        nc.scalar.activation(PR[:, :, 0:8], PR[:, :, 0:8], ACT.Exp).then_inc(r["expd"], 1)

                        def experts(i):
                            if i < 4 * NE:
                                act.wait_ge(hp, i + 1)
                                if i >= 2:
                                    act.wait_ge(sqs, i - 1)
                                nc.scalar.activation(RL[:, i % 2, :], PS[:, i % 4, :], ACT.Relu).then_inc(rl, 1)

                        for k in range(NC):
                            act.wait_ge(op, k + 1)
                            nc.scalar.activation(OT[:, k * CH:(k + 1) * CH], PS[:, 7, 0:CH], ACT.Copy,
                                                 accum_out=OS[:, k:k + 1]).then_inc(ot, 1)
                            experts(STEPS * k)
                            act.wait_ge(h1, k + 1)
                            nc.scalar.activation(HS[:, k * CH:(k + 1) * CH], PS[:, 6, 0:CH], ACT.Silu,
                                                 accum_out=HA[:, k:k + 1]).then_inc(hs, 1)
                            for i in range(1, STEPS):
                                experts(STEPS * k + i)
                        act.wait_ge(fo, 1)
                        nc.scalar.activation(SA[:, :, :].rearrange(flat), PS[:, 6, :], ACT.Copy).then_inc(fos, 1)
                        act.wait_ge(ad, NE)
                        nc.scalar.activation(GS[:, :, :], ACC[:, :, :], ACT.Silu).then_inc(gt, 1)

                    @block.vector
                    def _(v):
                        link = linker(v, dv)
                        norm_stats(link, X).then_inc(var, 1)
                        v.wait_ge(rs, 1)
                        norm_apply(XN, X).then_inc(xn, 1)
                        v.wait_ge(ns, T + 1)
                        link(nc.vector.tensor_scalar(NSQ[:, :], NSQ[:, :], 1e-5, None, ALU.max))
                        link(nc.vector.reciprocal(NSQ[:, :], NSQ[:, :]))
                        link(nc.vector.tensor_scalar(NSQ[:, :], NSQ[:, :], 1.0 / CH, None, ALU.mult))
                        nc.vector.tensor_tensor(KR[:, :, :], rep(NSQ[:, :], 2),
                                                halfsel[:, :].unsqueeze(1).to_broadcast([P, T, 2]), ALU.mult).then_inc(kr, 1)
                        v.wait_ge(ea, 1)
                        nc.vector.tensor_tensor(SG[:, :, :], PS[:, 2, 0:2 * T].rearrange("p (t w) -> p t w", w=2),
                                                eab[:, :].unsqueeze(1).to_broadcast([P, T, 2]), ALU.add).then_inc(eas, 1)
                        v.wait_ge(km, 1)
                        link(nc.vector.tensor_copy(KM[:, :], PS[:, 1, 0:NC]))
                        nc.vector.tensor_scalar(GK[:, :], KM[:, :], gw[:, :], None, ALU.mult).then_inc(gp, 1)
                        v.wait_ge(sg, 1)
                        for w in range(2):
                            last = nc.vector.tensor_tensor(SM[:, w, :, :], rep(SG[:, :, w], 2),
                                                           halfsel[:, :].unsqueeze(1).to_broadcast([P, T, 2]), ALU.mult)
                        last.then_inc(sm, 1)
                        v.wait_ge(gsum, 1)
                        nc.vector.tensor_scalar(GK[:, :], PS[:, 4, 0:NC], gb[:, :], None, ALU.add).then_inc(gs_, 1)
                        link(nc.vector.tensor_copy(XK[:, :, CH], KM[:, :]))
                        v.wait_ge(xts, 1)
                        link(nc.vector.tensor_copy(XK[:, :, 0:CH], XNT[:, :].rearrange("p (k c) -> p k c", c=CH)))
                        link(nc.vector.tensor_copy(N[:, :], M0T[:, :]))
                        v.wait_ge(co, 1)
                        link(nc.vector.tensor_scalar(EA[:, 0, :], PS[:, 3, 0:NC], 0.2 / CH, None, ALU.mult))
                        link(nc.vector.tensor_scalar(EA[:, 1, :], PS[:, 3, NC:2 * NC], 0.5 / CH, -0.5, ALU.mult, ALU.add))
                        v.wait_ge(gate, 1)
                        link(nc.vector.tensor_tensor(CA[:, :], EA[:, 1, :], GK[:, :], ALU.mult))
                        link(nc.vector.tensor_scalar(CA[:, :], CA[:, :], 1.0, None, ALU.add))
                        link(nc.vector.tensor_tensor(KB[:, :], EA[:, 0, :], GK[:, :], ALU.mult))
                        link(nc.vector.tensor_tensor(KB[:, :], KB[:, :], KM[:, :], ALU.mult))
                        v.wait_ge(r["logits"], 1)
                        shifted_logits(link, 7, None, 8).then_inc(r["shifted"], 1)
                        v.wait_ge(r["expd"], 1)
                        link(route_top(link, 8, 2, True))
                        link(nc.vector.memset(WG[:, :, 8:9], 1.0))
                        nc.vector.memset(ACC[:, :, :], 0.0).then_inc(ready, 1)
                        v.wait_ge(ready, 1)

                        def experts(i):
                            e, k = divmod(i, 4)
                            if e < NE:
                                v.wait_ge(rl, i + 1)
                                if e >= 2 and k == 0:
                                    v.wait_ge(yp, e - 1)
                                nc.vector.tensor_tensor(HH[:, e % 2, k, :], RL[:, i % 2, :], PS[:, i % 4, :],
                                                        ALU.mult).then_inc(sqs, 1)
                            if e >= 2 and k == 0:
                                add_expert(e - 2)

                        def add_expert(u):
                            v.wait_ge(yp, u + 1)
                            if u:
                                v.wait_ge(ad, u)
                            for t in range(T):
                                last = nc.vector.scalar_tensor_tensor(ACC[:, t, :], PS[:, 4 + u % 2, t * P:(t + 1) * P],
                                                                      WG[:, t, u:u + 1], ACC[:, t, :], ALU.mult, ALU.add)
                            last.then_inc(ad, 1)

                        for k in range(NC):
                            link(nc.vector.tensor_scalar(NA[:, :], N[:, :], CA[:, k:k + 1], None, ALU.mult))
                            experts(STEPS * k)
                            experts(STEPS * k + 1)
                            v.wait_ge(vt, k + 1)
                            v.wait_ge(hs, k + 1)
                            link(nc.vector.tensor_tensor(ER[:, 0:1], PS[:, 6, 0:1], OS[:, k:k + 1], ALU.add))
                            link(nc.vector.scalar_tensor_tensor(ER[:, 1:2], ER[:, 0:1], 1.0 / CH, PS[:, 7, CH:CH + 1],
                                                                ALU.mult, ALU.subtract))
                            nc.vector.tensor_scalar(DG[:, :], ident[:, :], ER[:, 1:2], None, ALU.mult).then_inc(dg, 1)
                            experts(STEPS * k + 2)
                            v.wait_ge(eb, k + 1)
                            link(nc.vector.scalar_tensor_tensor(N2[:, :], PS[:, 6, 0:P], KB[:, k:k + 1], NA[:, :],
                                                                ALU.mult, ALU.add))
                            nc.vector.scalar_tensor_tensor(NJ[:, :], N2[:, :], 1.0, N2[:, :], ALU.mult, ALU.mult,
                                                           accum_out=NQ[:, k:k + 1]).then_inc(nq, 1)
                            experts(STEPS * k + 3)
                            v.wait_ge(nn, k + 1)
                            nc.vector.tensor_copy(NR[:, k:k + 1], PS[:, 6, 0:1]).then_inc(nrm, 1)
                            experts(STEPS * k + 4)
                            v.wait_ge(srt, k + 1)
                            nr = NR[:, k:k + 1]
                            link(nc.vector.tensor_scalar(nr, nr, 1e-6, None, ALU.add))
                            link(nc.vector.reciprocal(nr, nr))
                            link(nc.vector.tensor_scalar(nr, nr, 30.0, 1.0, ALU.mult, ALU.min))
                            nc.vector.tensor_scalar(N[:, :], N2[:, :], nr, None, ALU.mult).then_inc(ready, 1)
                            v.wait_ge(ready, k + 2)
                        add_expert(NE - 1)
                        v.wait_ge(gt, 1)
                        v.wait_ge(fos, 1)
                        gate_and_add(link, GS[:, :, :], SA[:, :, :])
        out_t = out.rearrange("b (t p) d -> b p t d", p=P)
        x_t = I["L0_attn_resid_pre"].rearrange("b (t p) d -> b p t d", p=P)
        with nc.Fori(0, B) as b:
            x_in = lsem("x_in")
            with nc.Block() as block:
                @block.sync
                def _(sp):
                    sp.dma_start(X[:, :, :], x_t[bass.ds(b, 1)].rearrange("a p t d -> (a p) t d")).then_inc(x_in, 16)
                    sp.wait_ge(x_in, 16)
            end_stage()
            layer0()
            end_stage()
            layer1()
            end_stage()
            layer2()
            end_stage()
            layer3()
            end_stage()
            x_out = lsem("x_out")
            with nc.Block() as block:
                @block.sync
                def _(sp):
                    sp.dma_start(out_t[bass.ds(b, 1)].rearrange("a p t d -> (a p) t d"), X[:, :, :]).then_inc(x_out, 16)
                    sp.wait_ge(x_out, 16)
            end_stage()


def kernel(**inputs):
    import numpy as _np
    import concourse.bacc as _bacc
    from concourse import mybir as _mybir
    from concourse.bass_utils import run_bass_kernel_spmd as _run

    nc = _bacc.Bacc("TRN2", target_bir_lowering=False, num_devices=1)
    arrays, aps = {}, {}
    for name in inputs:
        a = _np.ascontiguousarray(inputs[name])
        arrays[f"in_{name}"] = a
        aps[name] = nc.dram_tensor(f"in_{name}", a.shape, _mybir.dt.from_np(a.dtype), kind="ExternalInput").ap()
    out = nc.dram_tensor("out_0", (B, S, D), F32, kind="ExternalOutput").ap()
    build(nc, aps, out)
    r = _run(nc, [arrays], core_ids=[0])
    return r.results[0]["out_0"]
```

```python
from contextlib import ExitStack

import concourse.bass as bass
from concourse import mybir

F32 = mybir.dt.float32
F32R = mybir.dt.float32r
U32 = mybir.dt.uint32
ALU = mybir.AluOpType
ACT = mybir.ActivationFunctionType
AX = mybir.AxisListType

P = 128
D = 128
B, S = 4, 512
T = S // P
EPS = 1e-5
A_LOG_MAX = 80.0
NEG = -3.4028234663852886e38


def build(nc, I, out):
    ctx = ExitStack()
    with ctx:
        def sb(name, shape, dt=F32, c=ctx):
            return c.enter_context(nc.sbuf_tensor(name, shape, dt))

        def sem(name):
            return ctx.enter_context(nc.semaphore(name))

        def linker(eng, chain):
            n = [0]

            def link(ins):
                n[0] += 1
                ins.then_inc(chain, 1)
                eng.wait_ge(chain, n[0])
            return link

        PS = ctx.enter_context(nc.psum_tensor("banks", [P, 8, 512], F32))

        ident = sb("ident", [P, P])
        identR = sb("identR", [P, P], F32R)
        ones = sb("ones", [P, P])
        causal = sb("causal", [P, 7 * P])
        tri = causal[:, 3 * P:4 * P]
        iota = sb("iota", [P, T, 16])
        headsel = sb("headsel", [P, 8, 16])
        neg_half = sb("neg_half", [P, 16])
        half_pow = sb("half_pow", [P, 4])
        halfsel = sb("halfsel", [P, 2])

        WQ = sb("WQ", [P, 8, P])
        WK = sb("WK", [P, 8, P])
        WV = sb("WV", [P, 8 * P])
        WO = sb("WO", [P, 8, D])
        bQ = sb("bQ", [P, 8])
        bK = sb("bK", [P, 8])
        bV = sb("bV", [P, 8])
        bO = sb("bO", [P, D])
        ln1w = sb("ln1w", [P, 1])
        ln1b = sb("ln1b", [P, 1])
        ln2w = sb("ln2w", [P, D])
        ln2b = sb("ln2b", [P, D])
        Wr0 = sb("Wr0", [P, 16])
        br0 = sb("br0", [P, 16])
        W1 = sb("W1", [P, 16, P])
        b1 = sb("b1", [P, 16, P])
        g1 = sb("g1", [P, 16])
        be1 = sb("be1", [P, 16])
        W2 = sb("W2", [P, 16, D])
        b2 = sb("b2", [16, D])
        wqp = sb("wqp", [P, P])
        wkp = sb("wkp", [P, P])
        wv1 = sb("wv1", [P, D])
        Wr1 = sb("Wr1", [P, 8])
        br1 = sb("br1", [P, 8])
        EW = sb("EW", [P, 8, D])
        Eb = sb("Eb", [8, D])
        WinT = sb("WinT", [P, 4, P])
        convw = sb("convw", [P, 2, 3])
        convb = sb("convb", [P, 2])
        WxT = sb("WxT", [P, 2, 96])
        WdtT = sb("WdtT", [P, 2, P])
        bdt = sb("bdt", [P, 2])
        Aneg = sb("Aneg", [P, 2, 16])
        Dp = sb("Dp", [P, 2])
        WoutT = sb("WoutT", [P, 2, D])
        gamma = sb("gamma", [P, D])
        beta = sb("beta", [P, D])
        rw1 = sb("rw1", [P, P])
        rb1 = sb("rb1", [P, 1])
        rw2 = sb("rw2", [P, 8])
        rb2 = sb("rb2", [P, 8])
        we1 = sb("we1", [P, 8, 512])
        be1f = sb("be1f", [P, 8, 4])
        we2 = sb("we2", [P, 8, 4, D])
        be2f = sb("be2f", [8, D])
        M0T = sb("M0T", [P, P])
        eab = sb("eab", [P, 2])
        gw = sb("gw", [P, 1])
        gb = sb("gb", [P, 1])
        vg1T = sb("vg1T", [P, P])
        vg2T = sb("vg2T", [P, P])
        WrT3 = sb("WrT3", [P, 10])
        fcT = sb("fcT", [P, 9, 512])
        pjT = sb("pjT", [P, 9, 4, D])

        s_zero = sem("s_zeroed")
        s_const = sem("s_constants")
        s_in = sem("s_layer0_loads")
        s_pad = sem("s_padded_loads")
        s_late = sem("s_late_loads")
        s_small = sem("s_small_staged")
        s_fc = sem("s_fc_staged")
        s_pj = sem("s_proj_staged")
        s_tr = sem("s_transposed")
        s_cpv = sem("s_stored_by_dve")
        s_cpa = sem("s_stored_by_act")
        s_steps = sem("s_dve_steps")
        s_alog = sem("s_a_log")
        s_x = sem("s_first_input")
        x_out = sem("x_stored")

        def col(ap):
            return ap.rearrange("(p a) -> p a", a=1)

        def bcast(ap, n):
            return ap.rearrange("(a n) -> a n", a=1).to_broadcast([P, n])

        X = sb("X", [P, T, D])
        XN = sb("XN", [P, T, D])
        XNT = sb("XNT", [P, S])
        XIN = sb("XIN", [P, T, D])
        SA = sb("SA", [P, T, D])
        stats = sb("stats", [P, T, 6])
        mv = sb("mv", [P, T, 2])
        rstd = sb("rstd", [P, T])
        x_t = I["L0_attn_resid_pre"].rearrange("b (t p) d -> b p t d", p=P)
        out_t = out.rearrange("b (t p) d -> b p t d", p=P)

        with ExitStack() as c:
            stage = sb("stage", [P, 40, P], c=c)
            plan = []
            loads = []
            n_st = 0

            def st(src, rows, dst, cols=P):
                nonlocal n_st
                plan.append((n_st, rows, cols, dst))
                loads.append((stage[0:rows, n_st, 0:cols], src))
                n_st += 1
            Win = I["L2_attn_W_in"]
            for m in range(4):
                st(Win[m * P:(m + 1) * P, :], P, WinT[:, m, :])
            for m in range(2):
                st(I["L2_attn_W_x"][:, m * P:(m + 1) * P], 96, WxT[:, m, :])
                st(I["L2_attn_W_dt"][m * P:(m + 1) * P, :], P, WdtT[0:64, m, :], 64)
                st(I["L2_attn_W_out"][:, m * P:(m + 1) * P], P, WoutT[:, m, :])
            st(I["L3_attn_M_init"], P, M0T[:, :])
            st(I["L3_attn_vg_w1"], P, vg1T[:, :])
            st(I["L3_attn_vg_w2"], P, vg2T[:, :])
            wvdT = sb("wvdT", [32, P], c=c)
            st(I["L1_attn_Wvdown"], P, wvdT[:, :], 32)
            st(I["L3_ffn_router_w"], 8, WrT3[:, 0:8])
            for name, dst in (("L0_attn_b_Q", bQ), ("L0_attn_b_K", bK), ("L0_attn_b_V", bV)):
                st(I[name].rearrange("(j s) k -> j (s k)", s=2), 8, dst[:, :])
            st(I["L0_ffn_g1"], 16, g1[:, :])
            st(I["L0_ffn_be1"], 16, be1[:, :])
            for name, dst in (("L2_attn_conv_b", convb), ("L2_attn_b_dt", bdt), ("L2_attn_D_param", Dp)):
                st(I[name].rearrange("(m p) -> m p", p=P), 2, dst[:, :])
            st(I["L2_ffn_be1"].rearrange("e (c p) -> (e c) p", p=P), 32, be1f[:, :, :].rearrange("p e c -> p (e c)"))
            fc_stage = sb("fc_stage", [P, 36, P], c=c)
            pj_stage = sb("pj_stage", [P, 36, P], c=c)
            jobs = []
            for r in range(9):
                jobs.append((fc_stage[:, 4 * r:4 * r + 4, :], fcT[:, r, :]))
            for r in range(9):
                jobs.append((pj_stage[:, 4 * r:4 * r + 4, :], pjT[:, r, :, :].rearrange("p c d -> p (c d)")))
            n_big = len(jobs)
            for slot, rows, cols, dst in plan:
                jobs.append((stage[0:rows, slot:slot + 1, 0:cols], dst))

            def bank_of(n, src):
                return PS[0:src.shape[2], n % 4, 0:src.shape[0] * src.shape[1]]

            wup = sb("wup", [32, D], c=c)
            cen = sb("cen", [P, 16], c=c)

            direct = [
                (WQ[:, :, :].rearrange("p j (s k) -> p (j s) k", s=2), I["L0_attn_W_Q"].rearrange("h d k -> d h k")),
                (WK[:, :, :].rearrange("p j (s k) -> p (j s) k", s=2), I["L0_attn_W_K"].rearrange("h d k -> d h k")),
                (WV[:, :].rearrange("p (h k) -> p h k", k=64), I["L0_attn_W_V"].rearrange("h d k -> d h k")),
                (WO[:, :, :], I["L0_attn_W_O"].rearrange("(j s) k d -> (s k) j d", s=2)),
                (bO[:, :], bcast(I["L0_attn_b_O"], D)),
                (ln1w[:, :], col(I["L0_attn_ln1_w"])),
                (ln1b[:, :], col(I["L0_attn_ln1_b"])),
                (ln2w[:, :], bcast(I["L0_attn_ln2_w"], D)),
                (ln2b[:, :], bcast(I["L0_attn_ln2_b"], D)),
                (Wr0[:, :], I["L0_ffn_Wr"]),
                (br0[:, :], bcast(I["L0_ffn_br"], 16)),
                (W1[:, :, :], I["L0_ffn_W1"].rearrange("e c h -> c e h")),
                (b1[:, :, :].rearrange("p e h -> p (e h)"), bcast(I["L0_ffn_b1"].rearrange("e h -> (e h)"), 2048)),
                (W2[:, :, :], I["L0_ffn_W2"].rearrange("e h o -> h e o")),
                (b2[:, :], I["L0_ffn_b2"]),
                (Eb[:, :], I["L1_ffn_expert_b"]),
                (be2f[:, :], I["L2_ffn_be2"]),
                (wup[:, :], I["L1_attn_Wvup"]),
                (Wr1[:, :], I["L1_ffn_router_w"]),
                (br1[:, :], bcast(I["L1_ffn_router_b"], 8)),
                (convw[:, :, :], I["L2_attn_conv_w"].rearrange("(m p) a k -> p m (a k)", p=P)),
                (gamma[:, :], bcast(I["L2_attn_gamma"], D)),
                (beta[:, :], bcast(I["L2_attn_beta"], D)),
                (rw1[:, :], I["L2_ffn_rw1"]),
                (rb1[:, :], col(I["L2_ffn_rb1"])),
                (rw2[:, :], I["L2_ffn_rw2"]),
                (rb2[:, :], bcast(I["L2_ffn_rb2"], 8)),
                (WrT3[:, 8:9], col(I["L3_attn_eta_w"])),
                (WrT3[:, 9:10], col(I["L3_attn_alpha_w"])),
                (eab[:, 0:1], bcast(I["L3_attn_eta_b"], 1)),
                (eab[:, 1:2], bcast(I["L3_attn_alpha_b"], 1)),
                (gw[:, :], col(I["L3_attn_gate_w"])),
                (gb[:, :], bcast(I["L3_attn_gate_b"], 1)),
            ]
            late = [
                (EW[:, :, :], I["L1_ffn_expert_w"].rearrange("e h d -> h e d")),
                (we1[:, :, :], I["L2_ffn_we1"].rearrange("e d h -> d e h")),
                (we2[:, :, :, :].rearrange("p e c d -> p (e c) d"), I["L2_ffn_we2"].rearrange("e (c p) d -> p (e c) d", p=P)),
            ]
            n_late = len(late)
            padded = [
                (wqp[:, 0:32], I["L1_attn_Wq"]),
                (wkp[:, 0:32], I["L1_attn_Wk"]),
            ]
            fc = I["L3_ffn_w_fc"].rearrange("e (c p) d -> p (e c) d", p=P)
            sfc = I["L3_ffn_shared_fc"].rearrange("(c p) d -> p c d", p=P)
            pj = I["L3_ffn_w_proj"].rearrange("e o f -> o e f")
            spj = I["L3_ffn_shared_proj"].rearrange("o (a f) -> o a f", a=1)

            block = nc.Block()
            with block:
                @block.sync
                def _(sp):
                    sp.dma_start(fc_stage[:, 0:32, :], fc).then_inc(s_fc, 16)
                    sp.dma_start(fc_stage[:, 32:36, :], sfc).then_inc(s_fc, 16)
                    sp.dma_start(pj_stage[:, 0:32, :].rearrange("p (e c) f -> p e (c f)", c=4), pj).then_inc(s_pj, 16)
                    sp.dma_start(pj_stage[:, 32:36, :].rearrange("p (e c) f -> p e (c f)", c=4), spj).then_inc(s_pj, 16)
                    for dst, src in loads:
                        sp.dma_start(dst, src).then_inc(s_small, 16)
                    sp.wait_ge(s_zero, 3)
                    for dst, src in padded:
                        sp.dma_start(dst, src).then_inc(s_pad, 16)
                    sp.wait_ge(s_in, 16 * len(direct))
                    for dst, src in late:
                        sp.dma_start(dst, src).then_inc(s_late, 16)
                    sp.wait_ge(s_pad, 16 * len(padded))

                @block.scalar
                def _(act):
                    act.dma_start(XIN[:, :, :], x_t[0]).then_inc(s_x, 16)
                    act.dma_start(Aneg[:, :, :], I["L2_attn_A_log"].rearrange("(m p) n -> p m n", p=P)).then_inc(s_alog, 16)
                    for dst, src in direct:
                        act.dma_start(dst, src).then_inc(s_in, 16)
                    act.wait_ge(s_alog, 17)
                    nc.scalar.activation(Aneg[:, :, :], Aneg[:, :, :], ACT.Exp).then_inc(s_alog, 1)
                    act.wait_ge(s_x, 16)
                    act.wait_ge(s_zero, 1)
                    for n in range(1, len(jobs), 2):
                        src, dst = jobs[n]
                        act.wait_ge(s_tr, n + 1)
                        nc.scalar.activation(dst, bank_of(n, src), ACT.Copy).then_inc(s_cpa, 1)

                @block.gpsimd
                def _(g):
                    nc.gpsimd.memset(ident[:, :], 0.0).then_inc(s_const, 1)
                    g.wait_ge(s_const, 1)
                    nc.gpsimd.affine_select(out=ident[:, :], in_=ident[:, :], compare_op=ALU.not_equal, fill=1.0,
                                            base=0, pattern=[[-1, P]], channel_multiplier=1).then_inc(s_const, 1)
                    for tile in (WdtT, wqp, wkp):
                        ap = tile[:, :, :] if len(tile.shape) == 3 else tile[:, :]
                        nc.gpsimd.memset(ap, 0.0).then_inc(s_zero, 1)
                    nc.gpsimd.memset(neg_half[:, :], -0.5).then_inc(s_zero, 1)
                    nc.gpsimd.memset(half_pow[:, :], 0.5).then_inc(s_zero, 1)
                    nc.gpsimd.memset(ones[:, :], 1.0).then_inc(x_out, 16)
                    nc.gpsimd.memset(causal[:, :], 1.0).then_inc(s_const, 1)
                    nc.gpsimd.memset(headsel[:, :, :], 0.0).then_inc(s_const, 1)
                    nc.gpsimd.memset(halfsel[:, :], 0.0).then_inc(s_const, 1)
                    nc.gpsimd.iota(iota[:, :, :], pattern=[[0, T], [1, 16]], base=0, channel_multiplier=0,
                                   allow_small_or_imprecise_dtypes=True).then_inc(s_const, 1)
                    g.wait_ge(s_const, 6)
                    nc.gpsimd.affine_select(out=causal[:, :], in_=causal[:, :], compare_op=ALU.is_ge, fill=0.0,
                                            base=3 * P, pattern=[[-1, 7 * P]], channel_multiplier=1).then_inc(s_const, 1)
                    g.wait_ge(s_const, 7)
                    for half in range(2):
                        rows = slice(64 * half, 64 * half + 64)
                        nc.gpsimd.affine_select(out=headsel[rows, :, :], in_=headsel[rows, :, :],
                                                compare_op=ALU.not_equal, fill=1.0, base=half,
                                                pattern=[[2, 8], [-1, 16]], channel_multiplier=0).then_inc(s_const, 1)
                        g.wait_ge(s_const, 8 + 2 * half)
                        nc.gpsimd.memset(halfsel[rows, half:half + 1], 1.0).then_inc(s_const, 1)
                        g.wait_ge(s_const, 9 + 2 * half)

                @block.vector
                def _(v):
                    link = linker(v, s_steps)
                    v.wait_ge(s_const, 2)
                    link(nc.vector.tensor_copy(identR[:, :], ident[:, :]))
                    v.wait_ge(s_alog, 16)
                    nc.vector.tensor_scalar(Aneg[:, :, :], Aneg[:, :, :], A_LOG_MAX, None, ALU.min).then_inc(s_alog, 1)
                    v.wait_ge(s_alog, 18)
                    link(nc.vector.tensor_scalar(Aneg[:, :, :], Aneg[:, :, :], -1.0, None, ALU.mult))
                    v.wait_ge(s_zero, 1)
                    for n in range(0, len(jobs), 2):
                        src, dst = jobs[n]
                        v.wait_ge(s_tr, n + 1)
                        nc.vector.tensor_copy(dst, bank_of(n, src)).then_inc(s_cpv, 1)
                    v.wait_ge(s_in, 16 * len(direct))
                    for w in (W1, b1):
                        link(nc.vector.reduce_sum(cen[:, :], w[:, :, :], AX.X))
                        link(nc.vector.tensor_scalar(cen[:, :], cen[:, :], 1.0 / P, None, ALU.mult))
                        link(nc.vector.tensor_tensor(w[:, :, :], w[:, :, :],
                                                     cen[:, :].unsqueeze(2).to_broadcast([P, 16, P]), ALU.subtract))
                    v.wait_ge(s_tr, len(jobs) + 1)
                    nc.vector.tensor_copy(wv1[:, :], PS[:, 4, 0:D]).then_inc(s_cpv, 1)

                @block.tensor
                def _(pe):
                    pe.wait_ge(s_const, 2)
                    for n, (src, dst) in enumerate(jobs):
                        if n == 0:
                            pe.wait_ge(s_fc, 32)
                        elif n == n_big // 2:
                            pe.wait_ge(s_pj, 32)
                        elif n == n_big:
                            pe.wait_ge(s_small, 16 * n_st)
                        if n >= 4:
                            pe.wait_ge((s_cpv, s_cpa)[n % 2], (n - 4) // 2 + 1)
                        rows = src.shape[0]
                        for k in range(src.shape[1]):
                            last = nc.tensor.transpose(bank_of(n, src)[:, k * rows:(k + 1) * rows], src[:, k, :],
                                                       ident[0:rows, 0:rows])
                        last.then_inc(s_tr, 1)
                    pe.wait_ge(s_in, 16 * len(direct))
                    nc.tensor.matmul(PS[:, 4, 0:D], wvdT[:, :], wup[:, :], start=True, stop=True).then_inc(s_tr, 1)

        flat = "p t d -> p (t d)"

        def norm_pool(plink, var, rs):
            plink(nc.gpsimd.tensor_scalar(rs, var, EPS, None, ALU.add))
            return nc.gpsimd.tensor_tensor(rs, rs, neg_half[:, 0:rs.shape[1]], ALU.pow)

        def norm_stats(link, src):
            for t in range(T):
                last = nc.vector.bn_stats(stats[:, t, :], src[:, t, :])
            link(last)
            for t in range(T):
                last = nc.vector.bn_aggr(mv[:, t, :], stats[:, t, :])
            return last

        def norm_apply(dst, src, done=None):
            for t in range(T):
                last = nc.vector.tensor_scalar(dst[:, t, :], src[:, t, :], mv[:, t, 0:1], rstd[:, t:t + 1],
                                               ALU.subtract, ALU.mult)
                if done is not None:
                    last.then_inc(done, 1)
            return last

        def transpose_tiles(pe, bank, src, ready, count=0):
            for t in range(T):
                pe.wait_ge(ready, count + t + 1)
                last = nc.tensor.transpose(PS[:, bank, t * P:(t + 1) * P], src[:, t, :], ident[:, :])
            return last

        def mm(o, l, r, start=True, stop=True):
            return nc.tensor.matmul(o, l, r, start=start, stop=stop)

        lsems = []
        scope = [ExitStack()]

        def lsem(name):
            h = scope[0].enter_context(nc.semaphore(name))
            lsems.append(h)
            return h

        def end_stage(*more):
            nums = sorted(h.num for h in (*lsems, *more))
            starts = [n for n in nums if n - 1 not in nums]
            ends = [n for n in nums if n + 1 not in nums]
            for first, last in zip(starts, ends):
                nc.all_engine_barrier(sems_to_clear=range(first, last + 1))
            lsems.clear()
            scope[0].close()
            scope[0] = ExitStack()

        def gate_logits(lhs, w, E, bank):
            for t in range(T):
                last = mm(PS[:, bank, t * E:(t + 1) * E], lhs[:, t * P:(t + 1) * P], w[:, 0:E])
            return last

        LG = sb("LG", [P, T, 16])
        PR = sb("PR", [P, T, 16])
        OH = sb("OH", [P, T, 16])
        OH2 = sb("OH2", [P, T, 16])
        WG = sb("WG", [P, T, 16])
        WGT = sb("WGT", [P, S])
        top8 = sb("top8", [P, T, 8])
        idx8 = sb("idx8", [P, T, 8], U32)
        idxf = sb("idxf", [P, T, 8])
        rt = sb("rt", [P, T, 4])

        def rep(ap, n):
            return ap.unsqueeze(2).to_broadcast([P, T, n])

        def best(link, pick, E, k):
            oh, oh2 = OH[:, :, 0:E], OH2[:, :, 0:E]
            for t in range(T):
                last = nc.vector.max(top8[:, t, :], pick[:, t, :])
            link(last)
            for t in range(T):
                last = nc.vector.max_index(idx8[:, t, :], top8[:, t, :], pick[:, t, :])
            link(last)
            link(nc.vector.tensor_copy(idxf[:, :, :], idx8[:, :, :]))
            if k == 2:
                nc.vector.tensor_tensor(oh2, iota[:, :, 0:E], rep(idxf[:, :, 1], E), ALU.is_equal)
            link(nc.vector.tensor_tensor(oh, iota[:, :, 0:E], rep(idxf[:, :, 0], E), ALU.is_equal))
            if k == 2:
                link(nc.vector.tensor_tensor(oh, oh, oh2, ALU.add))

        def logit_rows(bank, E):
            return PS[:, bank, 0:T * E].rearrange("p (t e) -> p t e", e=E)

        def gate_and_add(link, silu_out, s_ap, to):
            link(nc.vector.tensor_tensor(silu_out, silu_out, s_ap, ALU.mult))
            return nc.vector.tensor_tensor(to[:, :, :], X[:, :, :], silu_out, ALU.add)

        def shifted_logits(link, rows, bias, E):
            lg, pr = LG[:, :, 0:E], PR[:, :, 0:E]
            if bias is None:
                link(nc.vector.tensor_copy(lg, rows))
            else:
                link(nc.vector.tensor_tensor(lg, rows, bias[:, 0:E].unsqueeze(1).to_broadcast([P, T, E]), ALU.add))
            link(nc.vector.reduce_max(rt[:, :, 0], lg, AX.X))
            return nc.vector.tensor_tensor(pr, lg, rep(rt[:, :, 0], E), ALU.subtract)

        def route_share(link, E):
            pr = PR[:, :, 0:E]
            link(nc.vector.tensor_tensor(pr, pr, OH[:, :, 0:E], ALU.mult))
            link(nc.vector.reduce_sum(rt[:, :, 3], pr, AX.X))
            link(nc.vector.reciprocal(rt[:, :, 3], rt[:, :, 3]))
            return nc.vector.tensor_tensor(WG[:, :, 0:E], pr, rep(rt[:, :, 3], E), ALU.mult)

        def route_top(link, E, k, renorm):
            pr, oh = PR[:, :, 0:E], OH[:, :, 0:E]
            link(nc.vector.reduce_sum(rt[:, :, 1], pr, AX.X))
            link(nc.vector.reciprocal(rt[:, :, 2], rt[:, :, 1]))
            link(nc.vector.tensor_tensor(pr, pr, rep(rt[:, :, 2], E), ALU.mult))
            best(link, pr, E, k)
            if not renorm:
                return nc.vector.tensor_tensor(WG[:, :, 0:E], pr, oh, ALU.mult)
            link(nc.vector.tensor_tensor(pr, pr, oh, ALU.mult))
            link(nc.vector.reduce_sum(rt[:, :, 3], pr, AX.X))
            link(nc.vector.tensor_scalar(rt[:, :, 3], rt[:, :, 3], 1e-9, None, ALU.max))
            link(nc.vector.reciprocal(rt[:, :, 3], rt[:, :, 3]))
            return nc.vector.tensor_tensor(WG[:, :, 0:E], pr, rep(rt[:, :, 3], E), ALU.mult)

        def transpose_weights(bank, E):
            for t in range(T):
                last = nc.tensor.transpose(PS[0:E, bank, t * P:(t + 1) * P], WG[:, t, 0:E], ident[:, :])
            return last

        def weighted_biases(bank, E, b):
            for t in range(T):
                last = mm(PS[:, bank, t * P:(t + 1) * P], WGT[0:E, t * P:(t + 1) * P], b[0:E, :])
            return last



        def layer0():
            xn_ok, xt_ok, xt_sb = lsem("a0_xn"), lsem("a0_xt"), lsem("a0_xt_sb")
            var, rs = lsem("a0_var"), lsem("a0_rs")
            dv = lsem("a0_dve_steps")
            vp, vs = lsem("a0_v_products"), lsem("a0_v_stored")
            qk, qks = lsem("a0_qk_products"), lsem("a0_qk_stored")
            sc, nm, ex, ee = lsem("a0_scores"), lsem("a0_neg_max"), lsem("a0_exps"), lsem("a0_tail_exps")
            rc, pn = lsem("a0_inv_sums"), lsem("a0_probs")
            trA, trB, ptA, ptB = lsem("a0_trA"), lsem("a0_trB"), lsem("a0_ptA"), lsem("a0_ptB")
            pv, zs = lsem("a0_pv"), lsem("a0_z_stored")
            tl, tls, cts, ao = lsem("a0_tail"), lsem("a0_tail_stored"), lsem("a0_ct_stored"), lsem("a0_out")
            tz = lsem("a0_zeroed")
            OFF = [0, P, 3 * P, 6 * P]
            NG = 8 * T
            LAG = 3
            QK_AT = (0, 2)
            r = {k: lsem(f"f0_{k}") for k in ("logits", "shifted", "expd", "weights", "wT", "wT_stored", "bias")}
            hp, hb, sq, hn, ht = (lsem(f"f0_{k}") for k in ("hidden", "biased", "squares", "normed", "hiddenT"))
            gl, yp, ac, gt = (lsem(f"f0_{k}") for k in ("gelus", "outs", "added", "gate"))
            NU = 16
            with ExitStack() as c:
                X1 = sb("X1", [P, T, D], c=c)
                X1T = sb("X1T", [P, S], c=c)
                QT = sb("QT", [P, 2, S], c=c)
                KZ = sb("KZ", [P, 2, 2, S], c=c)
                V = sb("V", [P, 8, T, P], c=c)
                PR0 = sb("PR0", [P, 2, 2, 10 * P], c=c)
                PTS = sb("PTS", [P, 2, 2, S], c=c)
                NM = sb("NM", [P, NG, 2], c=c)
                L = sb("L", [P, NG, 2], c=c)
                E0 = sb("E0", [P, NG, 2], c=c)
                R = sb("R", [P, NG, 2], c=c)
                MX = R
                CC = sb("CC", [P, 3, 3, 16], c=c)
                CT = WGT[:, 0:3 * P].rearrange("p (t q) -> p t q", t=3)
                xtail = sb("xtail", [P, 4], c=c)
                xsum = sb("xsum", [P, 4], c=c)
                VT = sb("VT", [P, 8, 3], c=c)
                VTS = PTS[:, 0, 0, 0:384].rearrange("p (j a h) -> p j a h", j=8, a=3)
                G = sb("G", [P, P], c=c)[:, :]
                four = "p (i e d) -> p i e d"
                HB = KZ[:, :, :, :].rearrange("p a s k -> p (a s k)")[:, 0:3 * S].rearrange(four, i=3, e=4)
                SQ = QT[:, :, :].rearrange("p i (e d) -> p i e d", e=4)
                pair0 = PR0[:, 0, :, :].rearrange("p s k -> p (s k)")
                HN = pair0[:, 0:2 * S].rearrange(four, i=2, e=4)
                GT = pair0[:, 2 * S:4 * S].rearrange(four, i=2, e=4)
                pair1 = PR0[:, 1, :, :].rearrange("p s k -> p (s k)")
                ACC = pair1[:, 0:S].rearrange("p (t d) -> p t d", t=T)
                GS = pair1[:, S:2 * S].rearrange("p (t d) -> p t d", t=T)
                SS = sb("SS", [P, NU, 4], c=c)

                def bank(k, i):
                    return PS[:, k + i % 2, :].rearrange("p (e d) -> p e d", e=4)

                def ps2(g):
                    b0 = 2 * (g % 2)
                    return PS[:, b0:b0 + 2, :]

                with nc.Block() as block:
                    @block.gpsimd
                    def _(g):
                        plink = linker(g, lsem("a0_pool_steps"))
                        nc.gpsimd.memset(KZ[:, :, :, :], 0.0).then_inc(tz, 1)
                        nc.gpsimd.memset(CC[:, :, :, :], 0.0).then_inc(tz, 1)
                        nc.gpsimd.memset(CT, 0.0).then_inc(tz, 1)
                        nc.gpsimd.memset(G, 0.0).then_inc(tz, 1)
                        for k in range(2):
                            g.wait_ge(var, k + 1)
                            norm_pool(plink, mv[:, :, 1], rstd[:, :]).then_inc(rs, 1)
                        plink(nc.gpsimd.tensor_copy(X[:, :, :], XIN[:, :, :]))
                        for n in range(NG):
                            j, t = divmod(n, T)
                            g.wait_ge(rc, n + 1)
                            w = (t + 1) * P
                            p = PR0[:, j % 2, :, OFF[t]:OFF[t] + w]
                            nc.gpsimd.tensor_tensor(p, p, R[:, n, :].unsqueeze(2).to_broadcast([P, 2, w]),
                                                    ALU.mult).then_inc(pn, 1)
                        def unit_norm(i):
                            g.wait_ge(sq, i + 1)
                            plink(norm_pool(plink, SS[:, i, :], SS[:, i, :]))
                            if i >= 2:
                                g.wait_ge(ht, i - 1)
                            else:
                                g.wait_ge(trA, NG)
                                g.wait_ge(trB, NG)
                            nc.gpsimd.tensor_tensor(HN[:, i % 2, :, :], HB[:, i % 3, :, :],
                                                    SS[:, i, :].unsqueeze(2).to_broadcast([P, 4, P]),
                                                    ALU.mult).then_inc(hn, 1)
                        unit_norm(0)
                        unit_norm(1)
                        g.wait_ge(var, 3)
                        norm_pool(plink, mv[:, :, 1], rstd[:, :]).then_inc(rs, 1)
                        for i in range(2, NU):
                            unit_norm(i)

                    @block.tensor
                    def _(pe):
                        transpose_tiles(pe, 0, XN, xn_ok).then_inc(xt_ok, 1)
                        pe.wait_ge(xt_sb, 1)
                        gate_logits(XNT, Wr0, 16, 7).then_inc(r["logits"], 1)
                        transpose_tiles(pe, 1, X1, xn_ok, T).then_inc(xt_ok, 1)
                        pe.wait_ge(xt_sb, 2)
                        for i in range(8):
                            t, half = divmod(i, 2)
                            if i >= 2:
                                pe.wait_ge(vs, i - 1)
                            mm(PS[:, 2 + i % 2, :], X1T[:, t * P:(t + 1) * P],
                               WV[:, half * 512:(half + 1) * 512]).then_inc(vp, 1)
                        pe.wait_ge(tls, 1)
                        for j in range(8):
                            last = mm(PS[:, 0, 3 * j:3 * j + 3], WV[:, j * P:(j + 1) * P], xtail[:, 0:3])
                        last.then_inc(tl, 1)
                        pe.wait_ge(tls, 3)
                        for j in range(8):
                            last = mm(PS[0:48, 1, 0:P], PTS[:, 0, 0, 48 * j:48 * j + 48], WO[:, j, :],
                                      start=j == 0, stop=j == 7)
                        last.then_inc(tl, 1)

                        def project(j, which):
                            if j or which:
                                pe.wait_ge(qks, 3 * j + which)
                            w = (WQ, WK)[which]
                            mm(PS[:, 7, :], w[:, j, :], X1T[:, :]).then_inc(qk, 1)

                        def scores(n):
                            j, t = divmod(n, T)
                            if t == 0:
                                pe.wait_ge(qks, 3 * j + 3)
                            if n >= 2:
                                pe.wait_ge(ex, 2 * (n - 1))
                            for s in range(2):
                                last = mm(ps2(n)[:, s, 0:(t + 1) * P], QT[:, j % 2, t * P:(t + 1) * P],
                                          KZ[:, j % 2, s, 0:(t + 1) * P])
                            last.then_inc(sc, 1)

                        def hidden(i):
                            t, g = divmod(i, 4)
                            if i >= 2:
                                pe.wait_ge(hb, i - 1)
                            else:
                                pe.wait_ge(ex, 2 * NG - 2)
                            mm(PS[:, i % 2, :], XNT[:, t * P:(t + 1) * P],
                               W1[:, 4 * g:4 * g + 4, :].rearrange("p e h -> p (e h)")).then_inc(hp, 1)

                        def transposes(n):
                            t = n % T
                            if n >= 1:
                                pe.wait_ge(ptA, n)
                                pe.wait_ge(ptB, n)
                            pe.wait_ge(pn, n + 1)
                            for s, tr in enumerate((trA, trB)):
                                for k in range(t + 1):
                                    a = OFF[t] + k * P
                                    last = nc.tensor.transpose(PS[:, 4 + s, k * P:(k + 1) * P],
                                                               PR0[:, (n // T) % 2, s, a:a + P], ident[:, :])
                                last.then_inc(tr, 1)

                        def values(n):
                            j, t = divmod(n, T)
                            pe.wait_ge(ptA, n + 1)
                            pe.wait_ge(ptB, n + 1)
                            if t == 0 and j:
                                pe.wait_ge(zs, j)
                            for s in range(2):
                                for k in range(t + 1):
                                    last = mm(PS[64 * s:64 * s + 64, 6, t * P:(t + 1) * P],
                                              V[:, j, k, 64 * s:64 * s + 64], PTS[:, n % 2, s, k * P:(k + 1) * P],
                                              start=k == 0, stop=k == t)
                            last.then_inc(pv, 1)

                        pe.wait_ge(vs, 8)
                        pe.wait_ge(tls, 4)
                        pe.wait_ge(r["shifted"], 1)
                        project(0, 0)
                        project(0, 1)
                        for n in range(NG + LAG):
                            if n >= LAG:
                                transposes(n - LAG)
                            if n < NG:
                                scores(n)
                                if n + T < NG and n % T in QK_AT:
                                    project(n // T + 1, QK_AT.index(n % T))
                            if n in (NG, NG + 1):
                                hidden(n - NG)
                            if n >= LAG:
                                values(n - LAG)
                        for t in range(3):
                            last = nc.tensor.transpose(PS[0:48, 3, t * P:(t + 1) * P],
                                                       CC[:, t, :, :].rearrange("p a h -> p (a h)"), ident[:, :])
                        last.then_inc(tl, 1)
                        pe.wait_ge(zs, 8)
                        pe.wait_ge(cts, 1)
                        for t in range(T):
                            for j in range(8):
                                last = mm(PS[:, 2, t * P:(t + 1) * P], V[:, j, t, :], WO[:, j, :],
                                          start=j == 0, stop=j == 7 and t == 3)
                            if t < 3:
                                last = mm(PS[:, 2, t * P:(t + 1) * P], CT[:, t, :], G, start=False, stop=True)
                        last.then_inc(ao, 1)

                        transpose_weights(3, 16).then_inc(r["wT"], 1)
                        for i in range(2, NU + 3):
                            if i < NU:
                                hidden(i)
                            u = i - 2
                            if 0 <= u < NU:
                                pe.wait_ge(hn, u + 1)
                                if u >= 2:
                                    pe.wait_ge(gl, u - 1)
                                for e in range(4):
                                    last = nc.tensor.transpose(bank(4, u)[:, e, :], HN[:, u % 2, e, :], ident[:, :])
                                last.then_inc(ht, 1)
                            if i == 2:
                                pe.wait_ge(r["wT_stored"], 1)
                                weighted_biases(3, 16, b2).then_inc(r["bias"], 1)
                            u = i - 3
                            if 0 <= u:
                                g = u % 4
                                pe.wait_ge(gl, u + 1)
                                if u >= 2:
                                    pe.wait_ge(ac, u - 1)
                                for e in range(4):
                                    last = mm(bank(6, u)[:, e, :], GT[:, u % 2, e, :], W2[:, 4 * g + e, :])
                                last.then_inc(yp, 1)

                    @block.scalar
                    def _(act):
                        act.wait_ge(xt_ok, 1)
                        nc.scalar.activation(XNT[:, :], PS[:, 0, :], ACT.Copy).then_inc(xt_sb, 1)
                        act.wait_ge(xt_ok, 2)
                        nc.scalar.activation(X1T[:, :], PS[:, 1, :], ACT.Identity, bias=ln1b[:, :],
                                             scale=ln1w[:, :]).then_inc(xt_sb, 1)
                        for i in range(8):
                            t, half = divmod(i, 2)
                            act.wait_ge(vp, i + 1)
                            nc.scalar.activation(V[:, 4 * half:4 * half + 4, t, :],
                                                 PS[:, 2 + i % 2, :].rearrange("p (j d) -> p j d", j=4),
                                                 ACT.Copy).then_inc(vs, 1)
                            if i == 2:
                                act.wait_ge(r["shifted"], 1)
                                nc.scalar.activation(PR[:, :, :], PR[:, :, :], ACT.Exp).then_inc(r["expd"], 1)

                        def qk_evac(j, which):
                            act.wait_ge(qk, 2 * j + which + 1)
                            if which == 0:
                                nc.scalar.activation(QT[:, j % 2, :], PS[:, 7, :], ACT.Identity,
                                                     bias=bQ[:, j:j + 1]).then_inc(qks, 1)
                            else:
                                for s in range(2):
                                    r = slice(64 * s, 64 * s + 64)
                                    nc.scalar.activation(KZ[r, j % 2, s, :], PS[r, 7, :], ACT.Identity,
                                                         bias=bK[r, j:j + 1]).then_inc(qks, 1)

                        def exps(n):
                            j, t = divmod(n, T)
                            w = (t + 1) * P
                            act.wait_ge(nm, n + 1)
                            for s in range(2):
                                nc.scalar.activation(PR0[:, j % 2, s, OFF[t]:OFF[t] + w], ps2(n)[:, s, 0:w], ACT.Exp,
                                                     bias=NM[:, n, s:s + 1], scale=0.125,
                                                     accum_out=L[:, n, s:s + 1]).then_inc(ex, 1)
                            nc.scalar.activation(E0[:, n, :], NM[:, n, :], ACT.Exp).then_inc(ee, 1)

                        def squares(i):
                            act.wait_ge(hb, i + 1)
                            if i >= 2:
                                act.wait_ge(sq, i - 1)
                            for e in range(4):
                                last = nc.scalar.activation(SQ[:, i % 2, e, :], HB[:, i % 3, e, :], ACT.Square,
                                                            scale=float(P) ** -0.5, accum_out=SS[:, i, e:e + 1])
                            last.then_inc(sq, 1)

                        def store_pt(m):
                            act.wait_ge(trA, m + 1)
                            if m >= 2:
                                act.wait_ge(pv, m - 1)
                            w = (m % T + 1) * P
                            nc.scalar.activation(PTS[:, m % 2, 0, 0:w], PS[:, 4, 0:w], ACT.Copy).then_inc(ptA, 1)

                        act.wait_ge(tz, 4)
                        qk_evac(0, 0)
                        qk_evac(0, 1)
                        for n in range(NG + LAG):
                            t = n % T
                            if n >= LAG and t != 0 and t != 3:
                                store_pt(n - LAG)
                            if n >= LAG - 1 and t == 3:
                                store_pt(n + 1 - LAG)
                            if n < NG:
                                exps(n)
                            if LAG - 1 <= n < NG + LAG - 1 and t == 2:
                                store_pt(n + 1 - LAG)
                            if n + T < NG and t in QK_AT:
                                qk_evac(n // T + 1, QK_AT.index(t))
                            if n in (NG, NG + 1):
                                squares(n - NG)
                        for i in range(2, NU + 2):
                            if i < NU:
                                squares(i)
                            u = i - 2
                            if u >= 0:
                                g = u % 4
                                act.wait_ge(ht, u + 1)
                                if u >= 2:
                                    act.wait_ge(yp, u - 1)
                                for e in range(4):
                                    n = 4 * g + e
                                    last = nc.scalar.activation(GT[:, u % 2, e, :], bank(4, u)[:, e, :], ACT.Gelu,
                                                                bias=be1[:, n:n + 1], scale=g1[:, n:n + 1])
                                last.then_inc(gl, 1)
                        act.wait_ge(ac, NU)
                        nc.scalar.activation(GS, ACC, ACT.Silu).then_inc(gt, 1)


                    @block.vector
                    def _(v):
                        link = linker(v, dv)
                        norm_stats(link, XIN).then_inc(var, 1)
                        v.wait_ge(rs, 1)
                        v.wait_ge(x_out, 16)
                        norm_apply(XN, XIN, xn_ok)
                        v.wait_ge(xn_ok, T)
                        norm_stats(link, XN).then_inc(var, 1)
                        v.wait_ge(rs, 2)
                        norm_apply(X1, XN, xn_ok)
                        v.wait_ge(xt_sb, 2)
                        link(nc.vector.reduce_sum(xsum[:, 0:T], X1T[:, :].rearrange("p (t q) -> p t q", t=T), AX.X))
                        link(nc.vector.tensor_copy(xtail[:, 2:3], xsum[:, 3:4]))
                        link(nc.vector.tensor_tensor(xtail[:, 1:2], xtail[:, 2:3], xsum[:, 2:3], ALU.add))
                        nc.vector.tensor_tensor(xtail[:, 0:1], xtail[:, 1:2], xsum[:, 1:2], ALU.add).then_inc(tls, 1)
                        v.wait_ge(r["logits"], 1)
                        shifted_logits(link, logit_rows(7, 16), br0, 16).then_inc(r["shifted"], 1)
                        v.wait_ge(r["expd"], 1)
                        route_top(link, 16, 2, True).then_inc(r["weights"], 1)
                        v.wait_ge(tl, 1)
                        nc.vector.tensor_copy(VT[:, :, :], PS[:, 0, 0:24].rearrange("p (j a) -> p j a", a=3)).then_inc(tls, 1)
                        v.wait_ge(tls, 2)
                        nc.vector.tensor_tensor(VTS, VT[:, :, :].unsqueeze(3).to_broadcast([P, 8, 3, 16]),
                                                headsel[:, :, :].unsqueeze(2).to_broadcast([P, 8, 3, 16]),
                                                ALU.mult).then_inc(tls, 1)
                        v.wait_ge(tl, 2)
                        v.wait_ge(tz, 4)
                        nc.vector.tensor_copy(G[0:48, :], PS[0:48, 1, 0:P]).then_inc(tls, 1)

                        def hidden_bias(i):
                            g = i % 4
                            v.wait_ge(hp, i + 1)
                            if i >= 3:
                                v.wait_ge(hn, i - 2)
                                v.wait_ge(sq, i - 2)
                            else:
                                v.wait_ge(sc, NG)
                            nc.vector.tensor_tensor(HB[:, i % 3, :, :], bank(0, i), b1[:, 4 * g:4 * g + 4, :],
                                                    ALU.add).then_inc(hb, 1)

                        def row_max(n):
                            t = n % T
                            v.wait_ge(sc, n + 1)
                            d = ps2(n)[:, :, t * P:(t + 1) * P]
                            link(nc.vector.tensor_tensor(d, d, tri.unsqueeze(1).to_broadcast([P, 2, P]), ALU.mult))
                            link(nc.vector.reduce_max(MX[:, n, :], ps2(n)[:, :, 0:(t + 1) * P], AX.X))
                            if t < T - 1:
                                nc.vector.tensor_scalar(NM[:, n, :], MX[:, n, :], 0.0, -0.125, ALU.max,
                                                        ALU.mult).then_inc(nm, 1)
                            else:
                                nc.vector.tensor_scalar(NM[:, n, :], MX[:, n, :], -0.125, None, ALU.mult).then_inc(nm, 1)

                        def store_pt(m):
                            v.wait_ge(trB, m + 1)
                            if m >= 2:
                                v.wait_ge(pv, m - 1)
                            w = (m % T + 1) * P
                            nc.vector.tensor_copy(PTS[:, m % 2, 1, 0:w], PS[:, 5, 0:w]).then_inc(ptB, 1)

                        def z_store(j):
                            v.wait_ge(pv, T * (j + 1))
                            nc.vector.tensor_scalar(V[:, j, :, :].rearrange("p t d -> p (t d)"), PS[:, 6, :],
                                                    bV[:, j:j + 1], None, ALU.add).then_inc(zs, 1)

                        def row_sum(n):
                            j, t = divmod(n, T)
                            v.wait_ge(ex, 2 * n + 2)
                            v.wait_ge(ee, n + 1)
                            link(nc.vector.scalar_tensor_tensor(L[:, n, :], E0[:, n, :], float((T - 1 - t) * P),
                                                                L[:, n, :], ALU.mult, ALU.add))
                            nc.vector.reciprocal(R[:, n, :], L[:, n, :]).then_inc(rc, 1)
                            if t < T - 1:
                                v.wait_ge(rc, n + 1)
                                nc.vector.tensor_tensor(CC[:, t, t, 2 * j:2 * j + 2], E0[:, n, :], R[:, n, :],
                                                        ALU.mult).then_inc(tls, 1)

                        for n in range(NG + LAG):
                            if n >= LAG and n % T != 0:
                                store_pt(n - LAG)
                            if n < NG and n % T == 3:
                                row_sum(n - 1)
                            if n < NG:
                                row_max(n)
                            if n >= LAG - 1 and n % T == 3:
                                store_pt(n + 1 - LAG)
                            if n in (NG, NG + 1):
                                hidden_bias(n - NG)
                            if n > LAG and (n + 1 - LAG) % T == 0:
                                z_store((n + 1 - LAG) // T - 1)
                            if 1 <= n <= NG and n % T != 3:
                                row_sum(n - 1)
                        v.wait_ge(tl, 3)
                        nc.vector.tensor_copy(CT[0:48, :, :], PS[0:48, 3, 0:3 * P].rearrange("p (t q) -> p t q", t=3)).then_inc(cts, 1)
                        v.wait_ge(ao, 1)
                        sa = SA[:, :, :]
                        link(nc.vector.tensor_tensor(sa, PS[:, 2, :].rearrange("p (t d) -> p t d", t=T),
                                                     XN[:, :, :], ALU.add))
                        link(nc.vector.tensor_tensor(sa, sa, bO[:, :].unsqueeze(1).to_broadcast([P, T, D]), ALU.add))
                        norm_stats(link, SA).then_inc(var, 1)
                        hidden_bias(2)
                        v.wait_ge(r["wT"], 1)
                        nc.vector.tensor_copy(WGT[0:16, :], PS[0:16, 3, :]).then_inc(r["wT_stored"], 1)
                        v.wait_ge(rs, 3)
                        link(norm_apply(X1, SA))
                        link(nc.vector.tensor_tensor(X1[:, :, :], X1[:, :, :], ln2w[:, :].unsqueeze(1).to_broadcast([P, T, D]), ALU.mult))
                        link(nc.vector.tensor_tensor(X1[:, :, :], X1[:, :, :], ln2b[:, :].unsqueeze(1).to_broadcast([P, T, D]), ALU.add))
                        link(nc.vector.tensor_tensor(sa, sa, X1[:, :, :], ALU.add))
                        v.wait_ge(r["bias"], 1)
                        v.wait_ge(trA, NG)
                        v.wait_ge(trB, NG)
                        link(nc.vector.tensor_copy(ACC, PS[:, 3, :].rearrange("p (t d) -> p t d", t=T)))
                        for i in range(3, NU + 4):
                            if i < NU:
                                hidden_bias(i)
                            u = i - 4
                            if u >= 0:
                                t, g = divmod(u, 4)
                                v.wait_ge(yp, u + 1)
                                for e in range(4):
                                    ins = nc.vector.scalar_tensor_tensor(ACC[:, t, :], bank(6, u)[:, e, :],
                                                                         WG[:, t, 4 * g + e:4 * g + e + 1],
                                                                         ACC[:, t, :], ALU.mult, ALU.add)
                                    if e < 3:
                                        link(ins)
                                ins.then_inc(ac, 1)
                                v.wait_ge(ac, u + 1)
                        v.wait_ge(gt, 1)
                        gate_and_add(link, GS, SA[:, :, :], X)

        def layer1():
            dv, pl = lsem("a1_dve_steps"), lsem("a1_pool_steps")
            var, rs, xn, xt, xts = (lsem(f"a1_{k}") for k in ("var", "rstd", "xn", "xT", "xT_stored"))
            qk, qks, vp, vs, sc = (lsem(f"a1_{k}") for k in ("qk", "qk_stored", "v", "v_stored", "scores"))
            sm, fi, fd, nm, ex, inv = (lsem(f"a1_{k}") for k in ("masked", "fills", "filled", "neg_max", "exps", "inv_sums"))
            tr, pt, pv, so = (lsem(f"a1_{k}") for k in ("transposes", "pT", "pv", "s_stored"))
            r = {k: lsem(f"f1_{k}") for k in ("logits", "shifted", "expd", "weights", "wT", "wT_stored", "bias")}
            yp, ad, gt = (lsem(f"f1_{k}") for k in ("outs", "added", "gate"))
            NE = 8
            SCALE = 32.0 ** -0.5
            with ExitStack() as c:
                QK = sb("QK", [P, 2, S], c=c)
                V = sb("V1", [P, T, D], c=c)
                SC = sb("SC", [P, T, S], c=c)
                FI = sb("FI", [P, T, S], c=c)
                PB = sb("PB", [P, T, S], c=c)
                PT = sb("PT", [P, T, S], c=c)
                NM = sb("NM1", [P, T], c=c)
                MX = sb("MX1", [P, T], c=c)
                L = sb("L1", [P, T], c=c)
                R = sb("R1", [P, T], c=c)
                ACC = sb("ACC1", [P, T, D], c=c)
                GS = sb("GS1", [P, T, D], c=c)
                with nc.Block() as block:
                    @block.gpsimd
                    def _(g):
                        plink = linker(g, pl)
                        g.wait_ge(var, 1)
                        norm_pool(plink, mv[:, :, 1], rstd[:, :]).then_inc(rs, 1)
                        for t in range(T):
                            g.wait_ge(fi, t + 1)
                            nc.gpsimd.tensor_tensor(SC[:, t, :], SC[:, t, :], FI[:, t, :], ALU.add).then_inc(fd, 1)

                    @block.tensor
                    def _(pe):
                        transpose_tiles(pe, 0, XN, xn).then_inc(xt, 1)
                        pe.wait_ge(xts, 1)
                        for i, w in enumerate((wqp, wkp)):
                            mm(PS[:, 1 + i, :], w[:, :], XNT[:, :]).then_inc(qk, 1)
                        gate_logits(XNT, Wr1, NE, 0).then_inc(r["logits"], 1)
                        pe.wait_ge(qks, 2)
                        for t in range(T):
                            mm(PS[:, 4 + t, :], QK[:, 0, t * P:(t + 1) * P], QK[:, 1, :]).then_inc(sc, 1)
                        for t in range(T):
                            last = mm(PS[:, 3, t * P:(t + 1) * P], XNT[:, t * P:(t + 1) * P], wv1[:, :])
                        last.then_inc(vp, 1)

                        def expert(e):
                            if e == 0:
                                pe.wait_ge(s_late, 16 * n_late)
                            if e == 2:
                                pe.wait_ge(vs, 1)
                            if e >= 3:
                                pe.wait_ge(ad, e - 2)
                            for t in range(T):
                                last = mm(PS[:, 1 + e % 3, t * P:(t + 1) * P], XNT[:, t * P:(t + 1) * P], EW[:, e, :])
                            last.then_inc(yp, 1)

                        for e in range(3):
                            expert(e)
                        pe.wait_ge(r["weights"], 1)
                        transpose_weights(0, NE).then_inc(r["wT"], 1)
                        pe.wait_ge(r["wT_stored"], 1)
                        weighted_biases(0, NE, Eb).then_inc(r["bias"], 1)

                        def transposes(t):
                            pe.wait_ge(ex, t + 1)
                            pe.wait_ge(sm, t + 1)
                            for kt in range(T):
                                last = nc.tensor.transpose(PS[:, 4 + t, kt * P:(kt + 1) * P],
                                                           PB[:, t, kt * P:(kt + 1) * P], ident[:, :])
                            last.then_inc(tr, 1)

                        def values(t):
                            pe.wait_ge(pt, t + 1)
                            for kt in range(T):
                                last = mm(PS[:, 4 + t, 0:P], PT[:, t, kt * P:(kt + 1) * P], V[:, kt, :],
                                          start=kt == 0, stop=kt == T - 1)
                            last.then_inc(pv, 1)
                        for t in range(T):
                            transposes(t)
                            expert(3 + t)
                            values(t)
                        expert(7)

                    @block.scalar
                    def _(act):
                        act.wait_ge(xt, 1)
                        nc.scalar.activation(XNT[:, :], PS[:, 0, :], ACT.Copy).then_inc(xts, 1)
                        for i in range(2):
                            act.wait_ge(qk, i + 1)
                            nc.scalar.activation(QK[:, i, :], PS[:, 1 + i, :], ACT.Copy).then_inc(qks, 1)
                        act.wait_ge(r["shifted"], 1)
                        nc.scalar.activation(PR[:, :, 0:NE], PR[:, :, 0:NE], ACT.Exp).then_inc(r["expd"], 1)
                        act.wait_ge(vp, 1)
                        nc.scalar.activation(V[:, :, :].rearrange(flat), PS[:, 3, :], ACT.Copy).then_inc(vs, 1)

                        def store_s(t):
                            act.wait_ge(pv, t + 1)
                            act.wait_ge(inv, t + 1)
                            nc.scalar.activation(SA[:, t, :], PS[:, 4 + t, 0:P], ACT.Copy,
                                                 scale=R[:, t:t + 1]).then_inc(so, 1)
                        for t in range(T):
                            act.wait_ge(nm, t + 1)
                            nc.scalar.activation(PB[:, t, :], SC[:, t, :], ACT.Exp, bias=NM[:, t:t + 1],
                                                 accum_out=L[:, t:t + 1]).then_inc(ex, 1)
                            if t == 1:
                                act.wait_ge(r["wT"], 1)
                                nc.scalar.activation(WGT[0:NE, :], PS[0:NE, 0, :], ACT.Copy).then_inc(r["wT_stored"], 1)
                        act.wait_ge(r["bias"], 1)
                        nc.scalar.activation(ACC[:, :, :].rearrange(flat), PS[:, 0, :], ACT.Copy).then_inc(r["bias"], 1)
                        for t in range(T):
                            act.wait_ge(tr, t + 1)
                            nc.scalar.activation(PT[:, t, :], PS[:, 4 + t, :], ACT.Copy).then_inc(pt, 1)
                            if t:
                                store_s(t - 1)
                        store_s(T - 1)
                        act.wait_ge(ad, NE)
                        nc.scalar.activation(GS[:, :, :], ACC[:, :, :], ACT.Silu).then_inc(gt, 1)

                    @block.vector
                    def _(v):
                        link = linker(v, dv)
                        norm_stats(link, X).then_inc(var, 1)
                        v.wait_ge(rs, 1)
                        norm_apply(XN, X, xn)

                        def expd():
                            for t in range(T):
                                v.wait_ge(sc, t + 1)
                                a = (T - 1 - t) * P
                                nc.vector.scalar_tensor_tensor(SC[:, t, :], PS[:, 4 + t, :], SCALE,
                                                               causal[:, a:a + S], ALU.mult, ALU.mult).then_inc(sm, 1)
                                v.wait_ge(sm, t + 1)
                                nc.vector.tensor_scalar(FI[:, t, :], SC[:, t, :], 0.0, NEG, ALU.is_equal,
                                                        ALU.mult).then_inc(fi, 1)
                            v.wait_ge(r["expd"], 1)

                        def row_max(t):
                            v.wait_ge(fd, t + 1)
                            link(nc.vector.reduce_max(MX[:, t:t + 1], SC[:, t, :], AX.X))
                            nc.vector.tensor_scalar(NM[:, t:t + 1], MX[:, t:t + 1], -1.0, None, ALU.mult).then_inc(nm, 1)

                        v.wait_ge(r["logits"], 1)
                        shifted_logits(link, logit_rows(0, NE), br1, NE).then_inc(r["shifted"], 1)
                        expd()
                        row_max(0)
                        row_max(1)
                        route_top(link, NE, 1, False).then_inc(r["weights"], 1)
                        row_max(2)
                        row_max(3)
                        v.wait_ge(r["bias"], 2)
                        for e in range(NE):
                            v.wait_ge(yp, e + 1)
                            if e:
                                v.wait_ge(ad, e)
                            for t in range(T):
                                last = nc.vector.scalar_tensor_tensor(ACC[:, t, :], PS[:, 1 + e % 3, t * P:(t + 1) * P],
                                                                      WG[:, t, e:e + 1], ACC[:, t, :], ALU.mult, ALU.add)
                            last.then_inc(ad, 1)
                            if e < T:
                                v.wait_ge(ex, e + 1)
                                nc.vector.reciprocal(R[:, e:e + 1], L[:, e:e + 1]).then_inc(inv, 1)
                        v.wait_ge(gt, 1)
                        v.wait_ge(so, T)
                        gate_and_add(link, GS[:, :, :], SA[:, :, :], X)

        def layer2():
            dv, pl = lsem("a2_dve_steps"), lsem("a2_pool_steps")
            var, rs, xn, xt, xts = (lsem(f"a2_{k}") for k in ("var", "rstd", "xn", "xT", "xT_stored"))
            zr, xz, xm, cv, zg, xs = (lsem(f"a2_{k}") for k in ("zeroed", "xz", "x_stored", "conv", "z_silus", "x_silus"))
            db, dbs, bcr = (lsem(f"a2_{k}") for k in ("dbc", "dbc_stored", "bc_split"))
            dtp, dta, dte, dtl, dtx = (lsem(f"a2_{k}") for k in ("dt_raw", "dt_abs", "dt_exp", "dt_log", "dt_x"))
            bp, cp = lsem("a2_b_rows"), lsem("a2_c_rows")
            bm, ex, scn, hc, ya = (lsem(f"a2_{k}") for k in ("inputs", "decays", "scans", "outs", "y"))
            yg, wo = lsem("a2_gated"), lsem("a2_projected")
            r = {k: lsem(f"f2_{k}") for k in ("logits", "shifted", "expd", "weights", "wT", "wT_stored", "bias")}
            r1, r1s, hp, hs, yp, ad, gt = (lsem(f"f2_{k}") for k in (
                "router", "router_stored", "hidden", "silus", "outs", "added", "gate"))
            NS, NE = 16, 8
            LEAD = 2
            with ExitStack() as c:
                XM = sb("XM", [P, 2, S], c=c)
                ZS = sb("ZS", [P, 2, S], c=c)
                DT = sb("DT", [P, 2, S], c=c)
                DTX = sb("DTX", [P, 2, S], c=c)
                DAS = sb("DAS", [P, 8 * S + 4], c=c)
                H = sb("H", [P, 2, 2, S], c=c)
                BCR = sb("BCR", [96, 2, S], F32R, c=c)
                ACC = XIN
                H1 = sb("H1", [P, S], c=c)
                HH = sb("HH", [P, 2, 4, S], c=c)
                DA = DAS[:, 0:8 * S].rearrange("p (i m s) -> p i m s", i=4, m=2)
                XP = DAS[:, 6 * S:8 * S + 4].rearrange("p (m s) -> p m s", m=2)
                DBC = DAS[0:96, 4 * S:5 * S]
                E, LN = DA[:, 0, :, :], DA[:, 1, :, :]
                Y = [SA[:, :, :].rearrange(flat), H1[:, :]]
                GS = H1[:, :].rearrange("p (t d) -> p t d", t=T)
                GG = DT[:, 0, :].rearrange("p (t d) -> p t d", t=T)
                GB = DT[:, 1, :].rearrange("p (t d) -> p t d", t=T)
                with nc.Block() as block:
                    @block.gpsimd
                    def _(g):
                        plink = linker(g, pl)
                        nc.gpsimd.memset(XP[:, :, :], 0.0).then_inc(zr, 1)
                        g.wait_ge(var, 1)
                        norm_pool(plink, mv[:, :, 1], rstd[:, :]).then_inc(rs, 1)
                        g.wait_ge(r["logits"], 1)
                        for m in range(2):
                            g.wait_ge(xs, m + 1)
                            nc.gpsimd.tensor_tensor(Y[m], XM[:, m, :], Dp[:, m:m + 1].to_broadcast([P, S]),
                                                    ALU.mult).then_inc(ya, 1)
                        for n in range(NS):
                            for m in range(2):
                                g.wait_ge(hc, 2 * n + m + 1)
                                g.wait_ge(ya, 2 * n + m + 1)
                                nc.gpsimd.tensor_tensor(Y[m], Y[m], H[:, n % 2, m, :], ALU.add).then_inc(ya, 1)
                        g.wait_ge(gt, 1)
                        nc.gpsimd.tensor_tensor(GG, GS, gamma[:, :].unsqueeze(1).to_broadcast([P, T, D]),
                                                ALU.mult).then_inc(gt, 1)
                        g.wait_ge(var, 2)
                        norm_pool(plink, mv[:, :, 1], rstd[:, :]).then_inc(rs, 1)

                    @block.tensor
                    def _(pe):
                        transpose_tiles(pe, 7, XN, xn).then_inc(xt, 1)
                        pe.wait_ge(xts, 1)
                        for m in range(4):
                            mm(PS[:, m, :], WinT[:, m, :], XNT[:, :]).then_inc(xz, 1)
                        mm(PS[:, 6, :], rw1[:, :], XNT[:, :]).then_inc(r1, 1)

                        def hidden(n):
                            e, k = divmod(n, 4)
                            if n >= 4:
                                pe.wait_ge(hs, n - 3)
                            elif n < 2:
                                pe.wait_ge(zg, n + 1)
                            mm(PS[:, 2 + n % 4, :], we1[:, e, k * P:(k + 1) * P], XNT[:, :]).then_inc(hp, 1)

                        def outs(n):
                            u, t = divmod(n, 4)
                            if t == 0:
                                pe.wait_ge(hs, 4 * u + 4)
                                if u >= 2:
                                    pe.wait_ge(ad, u - 1)
                            for k in range(4):
                                last = mm(PS[:, 6 + u % 2, t * P:(t + 1) * P], HH[:, u % 2, k, t * P:(t + 1) * P],
                                          we2[:, u, k, :], start=k == 0, stop=k == 3)
                            if t == 3:
                                last.then_inc(yp, 1)

                        def rows(n, k, done):
                            i = 64 + NS * k + n
                            for part in range(2):
                                last = mm(PS[:, k, :], identR[0:96, i:i + 1].to_broadcast([96, P]), BCR[:, part, :],
                                          start=part == 0, stop=part == 1)
                            last.then_inc(done, 1)

                        for n in range(3):
                            hidden(n)
                        pe.wait_ge(r1s, 1)
                        gate_logits(H1, rw2, NE, 7).then_inc(r["logits"], 1)
                        hidden(3)
                        pe.wait_ge(xs, 2)
                        for m in range(2):
                            last = mm(PS[0:96, 0, :], WxT[:, m, :], XM[:, m, :], start=m == 0, stop=m == 1)
                        last.then_inc(db, 1)
                        hidden(4)
                        pe.wait_ge(dbs, 1)
                        for m in range(2):
                            mm(PS[:, m, :], WdtT[0:96, m, :], DBC).then_inc(dtp, 1)
                        for n in range(5, 8):
                            hidden(n)
                        pe.wait_ge(bcr, 1)
                        pe.wait_ge(dta, 2)
                        rows(0, 0, bp)
                        rows(0, 1, cp)
                        pe.wait_ge(r["weights"], 1)
                        transpose_weights(6, NE).then_inc(r["wT"], 1)
                        pe.wait_ge(r["wT_stored"], 1)
                        weighted_biases(6, NE, be2f).then_inc(r["bias"], 1)

                        pe.wait_ge(r["bias"], 2)
                        for n in range(NS):
                            work = [(outs, 2 * n), (outs, 2 * n + 1)]
                            if 2 * n + 4 * LEAD < 4 * NE:
                                if n % 2:
                                    work += [(hidden, 2 * n - 2 + 4 * LEAD + k) for k in range(4)]
                            if n + 1 < NS:
                                pe.wait_ge(bm, 2 * n + 2)
                                rows(n + 1, 0, bp)
                            half = len(work) // 2
                            for f, i in work[:half]:
                                f(i)
                            if n + 1 < NS:
                                pe.wait_ge(hc, 2 * n + 2)
                                rows(n + 1, 1, cp)
                            for f, i in work[half:]:
                                f(i)
                        pe.wait_ge(yg, 1)
                        for t in range(T):
                            for m in range(2):
                                last = mm(PS[:, 0, t * P:(t + 1) * P], H[:, 0, m, t * P:(t + 1) * P], WoutT[:, m, :],
                                          start=m == 0, stop=m == 1)
                        last.then_inc(wo, 1)

                    @block.scalar
                    def _(act):
                        act.wait_ge(xt, 1)
                        nc.scalar.activation(XNT[:, :], PS[:, 7, :], ACT.Copy).then_inc(xts, 1)
                        act.wait_ge(zr, 1)
                        for m in range(2):
                            act.wait_ge(xz, m + 1)
                            nc.scalar.activation(XP[:, m, 1:S + 1], PS[:, m, :], ACT.Copy).then_inc(xm, 1)
                        for m in range(2):
                            act.wait_ge(xz, m + 3)
                            nc.scalar.activation(ZS[:, m, :], PS[:, 2 + m, :], ACT.Silu).then_inc(zg, 1)
                        act.wait_ge(r1, 1)
                        nc.scalar.activation(H1[:, :], PS[:, 6, :], ACT.Silu, bias=rb1[:, :]).then_inc(r1s, 1)

                        def hidden(n):
                            e, k = divmod(n, 4)
                            act.wait_ge(hp, n + 1)
                            if e >= 2 and k == 0:
                                act.wait_ge(yp, e - 1)
                            nc.scalar.activation(HH[:, e % 2, k, :], PS[:, 2 + n % 4, :], ACT.Silu,
                                                 bias=be1f[:, e, k:k + 1]).then_inc(hs, 1)

                        hidden(0)
                        for m in range(2):
                            act.wait_ge(cv, m + 1)
                            nc.scalar.activation(XM[:, m, :], H[:, 0, m, :], ACT.Silu,
                                                 bias=convb[:, m:m + 1]).then_inc(xs, 1)
                        hidden(1)
                        hidden(2)
                        act.wait_ge(db, 1)
                        nc.scalar.activation(DBC, PS[0:96, 0, :], ACT.Copy).then_inc(dbs, 1)
                        hidden(3)
                        hidden(4)
                        for m in range(2):
                            act.wait_ge(dtp, m + 1)
                            nc.scalar.activation(DT[:, m, :], PS[:, m, :], ACT.Relu, bias=bdt[:, m:m + 1])
                            nc.scalar.activation(E[:, m, :], PS[:, m, :], ACT.Abs, bias=bdt[:, m:m + 1]).then_inc(dta, 1)
                        act.wait_ge(dta, 2)
                        nc.scalar.activation(E, E, ACT.Exp, scale=-1.0).then_inc(dte, 1)
                        act.wait_ge(r["shifted"], 1)
                        nc.scalar.activation(PR[:, :, 0:NE], PR[:, :, 0:NE], ACT.Exp).then_inc(r["expd"], 1)
                        act.wait_ge(dte, 1)
                        nc.scalar.activation(LN, E, ACT.Ln, bias=1.0).then_inc(dtl, 1)

                        def decays(n):
                            if n >= 4:
                                act.wait_ge(scn, 2 * (n - 3))
                            elif n == 2:
                                act.wait_ge(dtp, 2)
                                act.wait_ge(bcr, 1)
                            for m in range(2):
                                nc.scalar.activation(DA[:, n % 4, m, :], DT[:, m, :], ACT.Exp,
                                                     scale=Aneg[:, m, n:n + 1]).then_inc(ex, 1)
                        act.wait_ge(dtx, 1)
                        decays(0)
                        decays(1)
                        for n in range(0, NS, 2):
                            if n + 2 < NS:
                                decays(n + 2)
                                decays(n + 3)
                            if n == 0:
                                for k in range(5, 4 * LEAD):
                                    hidden(k)
                            if 2 * n + 4 * LEAD < 4 * NE:
                                for k in range(4):
                                    hidden(2 * n + 4 * LEAD + k)
                        act.wait_ge(ad, NE)
                        act.wait_ge(yg, 1)
                        nc.scalar.activation(GS, ACC[:, :, :], ACT.Silu).then_inc(gt, 1)

                    @block.vector
                    def _(v):
                        link = linker(v, dv)
                        norm_stats(link, X).then_inc(var, 1)
                        v.wait_ge(rs, 1)
                        norm_apply(XN, X, xn)
                        for m in range(2):
                            v.wait_ge(xm, m + 1)
                            o = H[:, 0, m, :]
                            link(nc.vector.tensor_scalar(o, XP[:, m, 0:S], convw[:, m, 0:1], None, ALU.mult))
                            link(nc.vector.scalar_tensor_tensor(o, XP[:, m, 1:S + 1], convw[:, m, 1:2], o, ALU.mult, ALU.add))
                            nc.vector.scalar_tensor_tensor(o, XP[:, m, 2:S + 2], convw[:, m, 2:3], o, ALU.mult,
                                                           ALU.add).then_inc(cv, 1)
                        v.wait_ge(r["logits"], 1)
                        shifted_logits(link, logit_rows(7, NE), rb2, NE).then_inc(r["shifted"], 1)
                        best(link, LG[:, :, 0:NE], NE, 2)
                        v.wait_ge(dbs, 1)
                        link(nc.vector.tensor_copy(BCR[:, 0, :], DBC))
                        nc.vector.tensor_tensor(BCR[:, 1, :], DBC, BCR[:, 0, :].bitcast(F32), ALU.subtract).then_inc(bcr, 1)
                        v.wait_ge(dte, 1)
                        link(nc.vector.tensor_scalar(DTX[:, :, :], E, 1.0, -1.0, ALU.add, ALU.add))
                        link(nc.vector.tensor_tensor(DTX[:, :, :], E, DTX[:, :, :], ALU.subtract))
                        v.wait_ge(r["expd"], 1)
                        route_share(link, NE).then_inc(r["weights"], 1)
                        v.wait_ge(dta, 2)
                        link(nc.vector.tensor_tensor(DT[:, :, :], DT[:, :, :], DTX[:, :, :], ALU.add))
                        v.wait_ge(dtl, 1)
                        nc.vector.tensor_tensor(DT[:, :, :], DT[:, :, :], LN, ALU.add).then_inc(dtx, 1)
                        v.wait_ge(r["wT"], 1)
                        nc.vector.tensor_copy(WGT[0:NE, :], PS[0:NE, 6, :]).then_inc(r["wT_stored"], 1)
                        v.wait_ge(dtx, 1)
                        v.wait_ge(xs, 2)
                        nc.vector.tensor_tensor(DTX[:, :, :], DT[:, :, :], XM[:, :, :], ALU.mult).then_inc(dtx, 1)
                        v.wait_ge(r["bias"], 1)
                        nc.vector.tensor_tensor(ACC[:, :, :].rearrange(flat), PS[:, 6, :], XN[:, :, :].rearrange(flat),
                                                ALU.add).then_inc(r["bias"], 1)

                        def add_expert(e):
                            v.wait_ge(yp, e + 1)
                            if e:
                                v.wait_ge(ad, e)
                            else:
                                v.wait_ge(r["bias"], 2)
                            for t in range(T):
                                last = nc.vector.scalar_tensor_tensor(ACC[:, t, :], PS[:, 6 + e % 2, t * P:(t + 1) * P],
                                                                      WG[:, t, e:e + 1], ACC[:, t, :], ALU.mult, ALU.add)
                            last.then_inc(ad, 1)

                        v.wait_ge(dtx, 2)
                        for n in range(NS):
                            v.wait_ge(bp, n + 1)
                            for m in range(2):
                                if n >= 2:
                                    v.wait_ge(ya, 2 * n + m - 1)
                                nc.vector.tensor_tensor(H[:, n % 2, m, :], DTX[:, m, :], PS[:, 0, :], ALU.mult).then_inc(bm, 1)
                            for m in range(2):
                                v.wait_ge(bm, 2 * n + m + 1)
                                v.wait_ge(ex, 2 * n + m + 1)
                                nc.vector.tensor_tensor_scan(H[:, n % 2, m, :], DA[:, n % 4, m, :],
                                                             H[:, n % 2, m, :], 0.0, ALU.mult, ALU.add).then_inc(scn, 1)
                            v.wait_ge(cp, n + 1)
                            for m in range(2):
                                v.wait_ge(scn, 2 * n + m + 1)
                                nc.vector.tensor_tensor(H[:, n % 2, m, :], H[:, n % 2, m, :], PS[:, 1, :],
                                                        ALU.mult).then_inc(hc, 1)
                            if n >= 3 and n % 2:
                                add_expert((n - 3) // 2)
                        for m in range(2):
                            v.wait_ge(ya, 2 * NS + m + 1)
                            last = nc.vector.tensor_tensor(H[:, 0, m, :], Y[m], ZS[:, m, :], ALU.mult)
                        last.then_inc(yg, 1)
                        add_expert(NE - 1)
                        v.wait_ge(gt, 1)
                        link(nc.vector.tensor_tensor(GB, GS, beta[:, :].unsqueeze(1).to_broadcast([P, T, D]), ALU.mult))
                        v.wait_ge(wo, 1)
                        sa = SA[:, :, :]
                        link(nc.vector.tensor_tensor(sa, PS[:, 0, :].rearrange("p (t d) -> p t d", t=T), XN[:, :, :], ALU.add))
                        norm_stats(link, SA).then_inc(var, 1)
                        link(nc.vector.tensor_tensor(GB, GB, X[:, :, :], ALU.add))
                        v.wait_ge(rs, 2)
                        v.wait_ge(gt, 2)
                        for t in range(T):
                            last = nc.vector.scalar_tensor_tensor(SA[:, t, :], SA[:, t, :], mv[:, t, 0:1], GG[:, t, :],
                                                                  ALU.subtract, ALU.mult)
                        link(last)
                        for t in range(T):
                            last = nc.vector.scalar_tensor_tensor(X[:, t, :], SA[:, t, :], rstd[:, t:t + 1], GB[:, t, :],
                                                                  ALU.mult, ALU.add)
                        link(last)

        def layer3(b):
            dv, pl = lsem("a3_dve_steps"), lsem("a3_pool_steps")
            var, rs, xn, xt, xts = (lsem(f"a3_{k}") for k in ("var", "rstd", "xn", "xT", "xT_stored"))
            ns, kr, km, eas, sg, sm, co, gp, gs_, gate = (lsem(f"a3_{k}") for k in (
                "norms", "key_scales", "key_means", "rates_shifted", "sigmoids", "masked", "rate_sums",
                "gate_parts", "gate_shifted", "gates"))
            done, x_in = lsem("a3_output"), lsem("a3_next_input")
            gsum, xk = lsem("a3_gate_sums"), lsem("a3_chunks_laid")
            ready, op, ot, h1, hs, vt, dg, eb, nq, nn, nrm, srt = (lsem(f"a3_{k}") for k in (
                "ready", "outs", "outs_stored", "hidden", "silus", "targets", "diag", "err_rows", "squares",
                "norm_sum", "norm_stored", "norm_root"))
            fo, fos = lsem("a3_final"), lsem("a3_final_stored")
            r = {k: lsem(f"f3_{k}") for k in ("logits", "shifted", "expd")}
            hp, rl, sqs, yp, ad, gt = (lsem(f"f3_{k}") for k in ("hidden", "relus", "squares", "outs", "added", "gate"))
            NE = 9
            CH = 64
            NC = S // CH
            with ExitStack() as c:
                XK = sb("XK", [P, NC, CH + 1], c=c)
                KM = sb("KM", [P, NC], c=c)
                NSQ = sb("NSQ", [P, T], c=c)
                KR = sb("KR", [P, T, 2], c=c)
                SQJ = sb("SQJ", [P, T, D], c=c)
                SG = sb("SG", [P, T, 2], c=c)
                SM = sb("SM", [P, 2, T, 2], c=c)
                EA = sb("EA", [P, 2, NC], c=c)
                GK = sb("GK", [P, NC], c=c)
                CA = sb("CA", [P, NC], c=c)
                KB = sb("KB", [P, NC], c=c)
                N = sb("N", [P, P], c=c)
                NA = sb("NA", [P, P], c=c)
                N2 = sb("N2", [P, P], c=c)
                NJ = sb("NJ", [P, P], c=c)
                DG = sb("DG", [P, P], c=c)
                OT = sb("OT", [P, S], c=c)
                HS = sb("HS", [P, S], c=c)
                OS = sb("OS", [P, NC], c=c)
                HA = sb("HA", [P, NC], c=c)
                ER = sb("ER", [P, 2], c=c)
                NQ = sb("NQ", [P, NC], c=c)
                NR = sb("NR", [P, NC], c=c)
                ACC = sb("ACC3", [P, T, D], c=c)
                GS = sb("GS3", [P, T, D], c=c)
                RL = sb("RL", [P, 3, S], c=c)
                HH = sb("HH3", [P, 2, 4, S], c=c)
                EARLY_HIDDEN, EARLY_OUTS = 8, 4
                work = []
                for n in range(EARLY_HIDDEN, 4 * NE + 4):
                    if n < 4 * NE:
                        work.append(("hidden", n))
                    elif n < 4 * NE + 3:
                        work.append(("final", n - 4 * NE))
                    work.append(("outs", n - 4))
                fill = []
                for k in range(NC):
                    fill.append([])
                    for size in (1, 1, 2, 1, 2 + (k + 1) % 2):
                        fill[k].append(work[:size])
                        work = work[size:]
                fill[-1][-1] += work
                with nc.Block() as block:
                    @block.sync
                    def _(sp):
                        sp.dma_start(XIN[:, :, :], x_t[bass.ds((b + 1) % B, 1)].rearrange("a p t d -> (a p) t d"))\
                            .then_inc(x_in, 16)
                        sp.wait_ge(x_in, 16)
                        sp.wait_ge(done, 1)
                        sp.dma_start(out_t[bass.ds(b, 1)].rearrange("a p t d -> (a p) t d"), XN[:, :, :])\
                            .then_inc(x_out, 16)

                    @block.gpsimd
                    def _(g):
                        plink = linker(g, pl)
                        g.wait_ge(var, 1)
                        norm_pool(plink, mv[:, :, 1], rstd[:, :]).then_inc(rs, 1)
                        g.wait_ge(ns, T)
                        nc.gpsimd.tensor_tensor(NSQ[:, :], NSQ[:, :], half_pow[:, 0:T], ALU.pow).then_inc(ns, 1)
                        nc.gpsimd.tensor_copy(N[:, :], M0T[:, :]).then_inc(xk, 1)
                        g.wait_ge(xts, 1)
                        nc.gpsimd.tensor_copy(XK[:, :, 0:CH], XNT[:, :].rearrange("p (k c) -> p k c", c=CH)).then_inc(xk, 1)
                        nc.gpsimd.memset(ACC[:, :, :], 0.0).then_inc(xk, 1)
                        nc.gpsimd.memset(WG[:, :, NE - 1:NE], 1.0).then_inc(xk, 1)
                        for k in range(NC - 1):
                            g.wait_ge(nrm, k + 1)
                            nc.gpsimd.tensor_tensor(NR[:, k:k + 1], NR[:, k:k + 1], half_pow[:, 0:1], ALU.pow).then_inc(srt, 1)

                    @block.tensor
                    def _(pe):
                        transpose_tiles(pe, 0, XN, xn).then_inc(xt, 1)
                        pe.wait_ge(xts, 1)
                        gate_logits(XNT, WrT3, 10, 7).then_inc(r["logits"], 1)

                        def hidden(n):
                            e, k = divmod(n, 4)
                            if n >= 4:
                                pe.wait_ge(rl, n - 3)
                            mm(PS[:, n % 4, :], fcT[:, e, k * P:(k + 1) * P], XNT[:, :]).then_inc(hp, 1)

                        def outs(n):
                            u, t = divmod(n, 4)
                            if t == 0:
                                pe.wait_ge(sqs, 4 * u + 4)
                                if u >= 2:
                                    pe.wait_ge(ad, u - 1)
                            for q in range(4):
                                last = mm(PS[:, 4 + u % 2, t * P:(t + 1) * P], HH[:, u % 2, q, t * P:(t + 1) * P],
                                          pjT[:, u, q, :], start=q == 0, stop=q == 3)
                            if t == 3:
                                last.then_inc(yp, 1)

                        def final(t):
                            pe.wait_ge(rl, 4 * NE - 3)
                            pe.wait_ge(hs, 2 * t + 2)
                            mm(PS[:, 0, t * P:(t + 1) * P], HS[:, t * P:(t + 1) * P], vg2T[:, :], start=True, stop=False)
                            mm(PS[:, 0, t * P:(t + 1) * P], OT[:, t * P:(t + 1) * P], ident[:, :],
                               start=False, stop=True).then_inc(fo, 1)

                        kinds = {"hidden": hidden, "outs": outs, "final": final}
                        hidden(0)
                        hidden(1)
                        pe.wait_ge(kr, 1)
                        pe.wait_ge(r["shifted"], 1)
                        for t in range(T):
                            last = mm(PS[:, 6, 2 * t:2 * t + 2], XN[:, t, :], KR[:, t, :])
                        last.then_inc(km, 1)
                        hidden(2)
                        pe.wait_ge(sm, 1)
                        mm(PS[:, 7, 0:2 * NC], ones[:, :], SM[:, :, :, :].rearrange("p w t h -> p (w t h)")).then_inc(co, 1)
                        hidden(3)
                        pe.wait_ge(gp, 1)
                        mm(PS[:, 5, 0:NC], ones[:, :], GK[:, :]).then_inc(gsum, 1)
                        for n in range(4, EARLY_HIDDEN):
                            hidden(n)
                        for n in range(EARLY_OUTS):
                            outs(n)
                        pe.wait_ge(xk, 2)
                        for k in range(NC):
                            last_chunk = k == NC - 1
                            pe.wait_ge(ready, k + 1)
                            mm(PS[:, 7, 0:CH + 1], N[:, :], XK[:, k, :]).then_inc(op, 1)
                            for kind, n in fill[k][0]:
                                kinds[kind](n)
                            pe.wait_ge(ot, k + 1)
                            mm(PS[:, 6, 0:CH], vg1T[:, :], OT[:, k * CH:(k + 1) * CH]).then_inc(h1, 1)
                            for kind, n in fill[k][1]:
                                kinds[kind](n)
                            pe.wait_ge(hs, k + 1)
                            if not last_chunk:
                                mm(PS[:, 6, 0:1], vg2T[:, :], HA[:, k:k + 1]).then_inc(vt, 1)
                            for kind, n in fill[k][2]:
                                kinds[kind](n)
                            if not last_chunk:
                                pe.wait_ge(dg, k + 1)
                                mm(PS[:, 6, 0:P], ones[:, :], DG[:, :]).then_inc(eb, 1)
                            for kind, n in fill[k][3]:
                                kinds[kind](n)
                            if not last_chunk:
                                pe.wait_ge(nq, k + 1)
                                mm(PS[:, 6, 0:1], ones[:, :], NQ[:, k:k + 1]).then_inc(nn, 1)
                            for kind, n in fill[k][4]:
                                kinds[kind](n)
                        final(T - 1)

                    @block.scalar
                    def _(act):
                        act.wait_ge(xt, 1)
                        nc.scalar.activation(XNT[:, :], PS[:, 0, :], ACT.Copy).then_inc(xts, 1)
                        for t in range(T):
                            nc.scalar.activation(SQJ[:, t, :], XN[:, t, :], ACT.Square,
                                                 accum_out=NSQ[:, t:t + 1]).then_inc(ns, 1)

                        def hidden(n):
                            act.wait_ge(hp, n + 1)
                            if n >= 3:
                                act.wait_ge(sqs, n - 2)
                            nc.scalar.activation(RL[:, n % 3, :], PS[:, n % 4, :], ACT.Relu).then_inc(rl, 1)

                        def relus(items):
                            for kind, n in items:
                                if kind == "hidden":
                                    hidden(n)

                        act.wait_ge(r["shifted"], 1)
                        nc.scalar.activation(PR[:, :, 0:8], PR[:, :, 0:8], ACT.Exp).then_inc(r["expd"], 1)
                        act.wait_ge(eas, 1)
                        nc.scalar.activation(SG[:, :, :], SG[:, :, :], ACT.Sigmoid).then_inc(sg, 1)
                        hidden(0)
                        hidden(1)
                        hidden(2)
                        hidden(3)
                        act.wait_ge(gs_, 1)
                        nc.scalar.activation(GK[:, :], GK[:, :], ACT.Sigmoid).then_inc(gate, 1)
                        for n in range(4, EARLY_HIDDEN):
                            hidden(n)
                        for k in range(NC):
                            act.wait_ge(op, k + 1)
                            nc.scalar.activation(OT[:, k * CH:(k + 1) * CH], PS[:, 7, 0:CH], ACT.Copy,
                                                 accum_out=OS[:, k:k + 1]).then_inc(ot, 1)
                            relus(fill[k][0])
                            act.wait_ge(h1, k + 1)
                            nc.scalar.activation(HS[:, k * CH:(k + 1) * CH], PS[:, 6, 0:CH], ACT.Silu,
                                                 accum_out=HA[:, k:k + 1]).then_inc(hs, 1)
                            for items in fill[k][1:4]:
                                relus(items)
                            if k < NC - 1:
                                act.wait_ge(nn, k + 1)
                                nc.scalar.activation(NR[:, k:k + 1], PS[:, 6, 0:1], ACT.Copy).then_inc(nrm, 1)
                            relus(fill[k][4])
                        act.wait_ge(fo, T)
                        nc.scalar.activation(SA[:, :, :].rearrange(flat), PS[:, 0, :], ACT.Copy).then_inc(fos, 1)
                        act.wait_ge(ad, NE)
                        nc.scalar.activation(GS[:, :, :], ACC[:, :, :], ACT.Silu).then_inc(gt, 1)

                    @block.vector
                    def _(v):
                        link = linker(v, dv)
                        norm_stats(link, X).then_inc(var, 1)
                        v.wait_ge(rs, 1)
                        norm_apply(XN, X, xn)

                        def hidden(n):
                            e, k = divmod(n, 4)
                            v.wait_ge(rl, n + 1)
                            if e >= 2 and k == 0:
                                v.wait_ge(yp, e - 1)
                            nc.vector.tensor_tensor(HH[:, e % 2, k, :], RL[:, n % 3, :], RL[:, n % 3, :],
                                                    ALU.mult).then_inc(sqs, 1)

                        def outs(n):
                            u, t = divmod(n, 4)
                            if t < 3:
                                return
                            v.wait_ge(yp, u + 1)
                            if u:
                                v.wait_ge(ad, u)
                            for t in range(T):
                                last = nc.vector.scalar_tensor_tensor(ACC[:, t, :], PS[:, 4 + u % 2, t * P:(t + 1) * P],
                                                                      WG[:, t, u:u + 1], ACC[:, t, :], ALU.mult, ALU.add)
                            last.then_inc(ad, 1)

                        kinds = {"hidden": hidden, "outs": outs, "final": lambda t: None}
                        rows = PS[:, 7, 0:10 * T].rearrange("p (t e) -> p t e", e=10)
                        v.wait_ge(r["logits"], 1)
                        nc.vector.tensor_tensor(SG[:, :, :], rows[:, :, 8:10],
                                                eab[:, :].unsqueeze(1).to_broadcast([P, T, 2]), ALU.add).then_inc(eas, 1)
                        shifted_logits(link, rows[:, :, 0:8], None, 8).then_inc(r["shifted"], 1)
                        v.wait_ge(ns, T + 1)
                        link(nc.vector.tensor_scalar(NSQ[:, :], NSQ[:, :], 1e-5, None, ALU.max))
                        link(nc.vector.reciprocal(NSQ[:, :], NSQ[:, :]))
                        link(nc.vector.tensor_scalar(NSQ[:, :], NSQ[:, :], 1.0 / CH, None, ALU.mult))
                        nc.vector.tensor_tensor(KR[:, :, :], rep(NSQ[:, :], 2),
                                                halfsel[:, :].unsqueeze(1).to_broadcast([P, T, 2]), ALU.mult).then_inc(kr, 1)
                        hidden(0)
                        hidden(1)
                        v.wait_ge(sg, 1)
                        for w in range(2):
                            last = nc.vector.tensor_tensor(SM[:, w, :, :], rep(SG[:, :, w], 2),
                                                           halfsel[:, :].unsqueeze(1).to_broadcast([P, T, 2]), ALU.mult)
                        last.then_inc(sm, 1)
                        v.wait_ge(km, 1)
                        link(nc.vector.tensor_copy(KM[:, :], PS[:, 6, 0:NC]))
                        nc.vector.tensor_scalar(GK[:, :], KM[:, :], gw[:, :], None, ALU.mult).then_inc(gp, 1)
                        hidden(2)
                        hidden(3)
                        v.wait_ge(gsum, 1)
                        nc.vector.tensor_scalar(GK[:, :], PS[:, 5, 0:NC], gb[:, :], None, ALU.add).then_inc(gs_, 1)
                        link(nc.vector.tensor_copy(XK[:, :, CH], KM[:, :]))
                        v.wait_ge(co, 1)
                        nc.vector.tensor_scalar(EA[:, 0, :], PS[:, 7, 0:NC], 0.2 / CH, None, ALU.mult)
                        link(nc.vector.tensor_scalar(EA[:, 1, :], PS[:, 7, NC:2 * NC], 0.5 / CH, -0.5, ALU.mult, ALU.add))
                        hidden(4)
                        v.wait_ge(gate, 1)
                        link(nc.vector.tensor_tensor(CA[:, :], EA[:, 1, :], GK[:, :], ALU.mult))
                        nc.vector.tensor_scalar(CA[:, :], CA[:, :], 1.0, None, ALU.add)
                        link(nc.vector.tensor_tensor(KB[:, :], EA[:, 0, :], GK[:, :], ALU.mult))
                        nc.vector.tensor_tensor(KB[:, :], KB[:, :], KM[:, :], ALU.mult).then_inc(ready, 1)
                        hidden(5)
                        hidden(6)
                        v.wait_ge(xk, 4)
                        v.wait_ge(ready, 1)
                        link(nc.vector.tensor_scalar(NA[:, :], N[:, :], CA[:, 0:1], None, ALU.mult))
                        hidden(7)
                        v.wait_ge(r["expd"], 1)
                        link(route_top(link, 8, 2, True))
                        outs(3)
                        for k in range(NC):
                            last_chunk = k == NC - 1
                            if k:
                                link(nc.vector.tensor_scalar(NA[:, :], N[:, :], CA[:, k:k + 1], None, ALU.mult))
                            for kind, n in fill[k][0] + fill[k][1]:
                                kinds[kind](n)
                            if not last_chunk:
                                v.wait_ge(vt, k + 1)
                                v.wait_ge(hs, k + 1)
                                link(nc.vector.tensor_tensor(ER[:, 0:1], PS[:, 6, 0:1], OS[:, k:k + 1], ALU.add))
                                link(nc.vector.scalar_tensor_tensor(ER[:, 1:2], ER[:, 0:1], 1.0 / CH, PS[:, 7, CH:CH + 1],
                                                                    ALU.mult, ALU.subtract))
                                nc.vector.tensor_scalar(DG[:, :], ident[:, :], ER[:, 1:2], None, ALU.mult).then_inc(dg, 1)
                            for kind, n in fill[k][2]:
                                kinds[kind](n)
                            if not last_chunk:
                                v.wait_ge(eb, k + 1)
                                link(nc.vector.scalar_tensor_tensor(N2[:, :], PS[:, 6, 0:P], KB[:, k:k + 1], NA[:, :],
                                                                    ALU.mult, ALU.add))
                                nc.vector.scalar_tensor_tensor(NJ[:, :], N2[:, :], 1.0, N2[:, :], ALU.mult, ALU.mult,
                                                               accum_out=NQ[:, k:k + 1]).then_inc(nq, 1)
                            for kind, n in fill[k][3]:
                                kinds[kind](n)
                            if not last_chunk:
                                nr = NR[:, k:k + 1]
                                v.wait_ge(srt, k + 1)
                                link(nc.vector.tensor_scalar(nr, nr, 1e-6, 30.0, ALU.add, ALU.max))
                                link(nc.vector.reciprocal(nr, nr))
                                nc.vector.tensor_scalar(N[:, :], N2[:, :], nr, 30.0, ALU.mult, ALU.mult).then_inc(ready, 1)
                                v.wait_ge(ready, k + 2)
                            for kind, n in fill[k][4]:
                                kinds[kind](n)
                        v.wait_ge(fos, 1)
                        v.wait_ge(gt, 1)
                        gate_and_add(link, GS[:, :, :], SA[:, :, :], XN).then_inc(done, 1)
        with nc.Fori(0, B) as b:
            layer0()
            end_stage(x_out)
            layer1()
            end_stage()
            layer2()
            end_stage()
            layer3(b)
            end_stage()
        with nc.Block() as block:
            @block.sync
            def _(sp):
                sp.wait_ge(x_out, 16)


def kernel(**inputs):
    import numpy as _np
    import concourse.bacc as _bacc
    from concourse import mybir as _mybir
    from concourse.bass_utils import run_bass_kernel_spmd as _run

    nc = _bacc.Bacc("TRN2", target_bir_lowering=False, num_devices=1)
    arrays, aps = {}, {}
    for name in inputs:
        a = _np.ascontiguousarray(inputs[name])
        arrays[f"in_{name}"] = a
        aps[name] = nc.dram_tensor(f"in_{name}", a.shape, _mybir.dt.from_np(a.dtype), kind="ExternalInput").ap()
    out = nc.dram_tensor("out_0", (B, S, D), F32, kind="ExternalOutput").ap()
    build(nc, aps, out)
    r = _run(nc, [arrays], core_ids=[0])
    return r.results[0]["out_0"]
```
